# Optimizing a Trainium2 kernel written in Bass

```python
import numpy as np
import jax
import jax.numpy as jnp

def _softmax(x, axis=-1):
    return jax.nn.softmax(x, axis=axis)

def _gelu(x):
    return jax.nn.gelu(x, approximate=True)

def _silu(x):
    return jax.nn.silu(x)

def _sigmoid(x):
    return jax.nn.sigmoid(x)

def _layernorm(x, axis=-1, eps=1e-05):
    m = jnp.mean(x, axis=axis, keepdims=True)
    v = jnp.var(x, axis=axis, keepdims=True)
    return (x - m) / jnp.sqrt(v + eps)

def _scatter_add(tgt, idx, src, axis=0):
    return tgt.at[idx].add(src)

def _segment_sum(src, seg, n):
    return jax.ops.segment_sum(src, seg, n)
kernel_name = 'mk_adaln_d1_jaxref_r8_4af303'

def setup_inputs(seed: int=0):
    np.random.seed(seed)
    _w = jnp.asarray

    def _L0_attn_setup():
        import jax, jax.numpy as jnp
        import numpy as np
        D = 128
        H = 16
        HD = D // H
        EPS = 1e-06

        def _rmsnorm(x, w):
            xf = x.astype(jnp.float32)
            var = jnp.mean(xf * xf, axis=-1, keepdims=True)
            return (w * (xf * jax.lax.rsqrt(var + EPS))).astype(x.dtype)
        key = jax.random.key(seed)
        ks = jax.random.split(key, 10)
        B, N = (2, 256)
        s = 0.02
        return {'x': jax.random.normal(ks[0], (B, N, D), jnp.float32), 'Wq': jax.random.normal(ks[1], (D, D + H), jnp.float32) * s, 'bq': jnp.zeros((D + H,), jnp.float32), 'Wk': jax.random.normal(ks[2], (D, D), jnp.float32) * s, 'bk': jnp.zeros((D,), jnp.float32), 'Wv': jax.random.normal(ks[3], (D, D), jnp.float32) * s, 'bv': jnp.zeros((D,), jnp.float32), 'Wo': jax.random.normal(ks[4], (D, D), jnp.float32) * s, 'bo': jnp.zeros((D,), jnp.float32), 'qn_w': jnp.ones((HD,), jnp.float32), 'kn_w': jnp.ones((HD,), jnp.float32)}
    _L0_attn_in = _L0_attn_setup()

    def _L0_ffn_setup():
        import jax, jax.numpy as jnp
        import numpy as np
        TOP_K = 2
        key = jax.random.key(seed)
        k1, k2, k3 = jax.random.split(key, 3)
        B, S, H, E, D = (4, 128, 128, 32, 128)
        x = jax.random.normal(k1, (B, S, H), dtype=jnp.float32)
        router_w = jax.random.normal(k2, (E, H), dtype=jnp.float32) * (1.0 / np.sqrt(H))
        bound = float(np.sqrt(6.0 / ((1.0 + 0.01 ** 2) * H)))
        expert_weights = jax.random.uniform(k3, (E, H, D), dtype=jnp.float32, minval=-bound, maxval=bound)
        return {'x': x, 'router_w': router_w, 'expert_weights': expert_weights}
    _L0_ffn_in = _L0_ffn_setup()
    _L0_c = _w((lambda *s: np.random.randn(*s).astype(np.float32) * 0.05)(32, 128))
    _L0_wmod = _w((lambda *s: np.random.randn(*s).astype(np.float32) * 0.05)(128, 6 * 128) * 128 ** (-0.5))
    _d = {'L0_attn_x': _L0_attn_in['x'], 'L0_attn_Wq': _L0_attn_in['Wq'], 'L0_attn_bq': _L0_attn_in['bq'], 'L0_attn_Wk': _L0_attn_in['Wk'], 'L0_attn_bk': _L0_attn_in['bk'], 'L0_attn_Wv': _L0_attn_in['Wv'], 'L0_attn_bv': _L0_attn_in['bv'], 'L0_attn_Wo': _L0_attn_in['Wo'], 'L0_attn_bo': _L0_attn_in['bo'], 'L0_attn_qn_w': _L0_attn_in['qn_w'], 'L0_attn_kn_w': _L0_attn_in['kn_w'], 'L0_ffn_router_w': _L0_ffn_in['router_w'], 'L0_ffn_expert_weights': _L0_ffn_in['expert_weights'], 'L0_c': _L0_c, 'L0_wmod': _L0_wmod}
    _x0 = _d['L0_attn_x']
    _d['L0_attn_x'] = jax.random.normal(jax.random.fold_in(jax.random.key(seed), 1), (32, 256, 128), dtype=_x0.dtype)
    del _x0
    return _d

def reference(L0_attn_x, L0_attn_Wq, L0_attn_bq, L0_attn_Wk, L0_attn_bk, L0_attn_Wv, L0_attn_bv, L0_attn_Wo, L0_attn_bo, L0_attn_qn_w, L0_attn_kn_w, L0_ffn_router_w, L0_ffn_expert_weights, L0_c, L0_wmod):

    def _L0_attn_ref(x, Wq, bq, Wk, bk, Wv, bv, Wo, bo, qn_w, kn_w):
        import jax, jax.numpy as jnp
        import numpy as np
        D = 128
        H = 16
        HD = D // H
        EPS = 1e-06

        def _rmsnorm(x, w):
            xf = x.astype(jnp.float32)
            var = jnp.mean(xf * xf, axis=-1, keepdims=True)
            return (w * (xf * jax.lax.rsqrt(var + EPS))).astype(x.dtype)
        B, N, _ = x.shape
        qg = x @ Wq + bq
        Q, gate = (qg[..., :D], qg[..., D:])
        K = x @ Wk + bk
        V = x @ Wv + bv
        Q = Q.reshape(B, N, H, HD).transpose(0, 2, 1, 3)
        K = K.reshape(B, N, H, HD).transpose(0, 2, 1, 3)
        V = V.reshape(B, N, H, HD).transpose(0, 2, 1, 3)
        Q = _rmsnorm(Q, qn_w)
        K = _rmsnorm(K, kn_w)
        scores = jnp.einsum('bhqd,bhkd->bhqk', Q, K) / jnp.sqrt(jnp.float32(HD))
        attn = jax.nn.softmax(scores.astype(jnp.float32), axis=-1).astype(Q.dtype)
        out = jnp.einsum('bhqk,bhkd->bhqd', attn, V)
        out = out.transpose(0, 2, 1, 3)
        out = out * jax.nn.sigmoid(gate)[..., None]
        out = out.reshape(B, N, D)
        return out @ Wo + bo

    def _L0_ffn_ref(x, router_w, expert_weights):
        import jax, jax.numpy as jnp
        import numpy as np
        TOP_K = 2
        B, S, H = x.shape
        E = router_w.shape[0]
        T = B * S
        logits = jnp.einsum('bsh,eh->bse', x, router_w)
        rw = jax.nn.softmax(logits, axis=-1).reshape(T, E)
        x_flat = x.reshape(T, H)
        vals, idx = jax.lax.top_k(rw, TOP_K)
        w_masked = jnp.zeros_like(rw).at[jnp.arange(T)[:, None], idx].set(vals)

        def body(acc, we):
            w_e, W_e = we
            return (acc + x_flat * w_e[:, None] @ W_e, None)
        out_flat, _ = jax.lax.scan(body, jnp.zeros((T, H), dtype=x.dtype), (w_masked.T, expert_weights))
        return out_flat.reshape(B, S, H)
    x = L0_attn_x
    mod = (_silu(L0_c) @ L0_wmod).reshape(L0_c.shape[0], 6, 1, -1)
    sa, ca, ga, sb, cb, gb = (mod[:, 0], mod[:, 1], mod[:, 2], mod[:, 3], mod[:, 4], mod[:, 5])
    ga = (2 * (ga >= 0) - 1) * jnp.maximum(jnp.abs(ga), 0.25)
    gb = (2 * (gb >= 0) - 1) * jnp.maximum(jnp.abs(gb), 0.25)
    h = _layernorm(x, axis=-1) * (1 + ca) + sa
    x = x + ga * _L0_attn_ref(h, L0_attn_Wq, L0_attn_bq, L0_attn_Wk, L0_attn_bk, L0_attn_Wv, L0_attn_bv, L0_attn_Wo, L0_attn_bo, L0_attn_qn_w, L0_attn_kn_w)
    h = _layernorm(x, axis=-1) * (1 + cb) + sb
    x = x + gb * _L0_ffn_ref(h, L0_ffn_router_w, L0_ffn_expert_weights)
    return x

_drawn_inputs = setup_inputs


def setup_inputs(seed=0):
    import zlib

    import numpy as np

    out = dict(_drawn_inputs(seed))
    spreads = {'L0_attn_bq': (0.0, 0.8),
     'L0_attn_bk': (0.0, 2.0),
     'L0_attn_bv': (0.0, 0.8),
     'L0_attn_bo': (0.0, 0.3),
     'L0_attn_qn_w': (1.0, 0.6),
     'L0_attn_kn_w': (1.0, 0.6)}
    factors = {'L0_attn_Wq': 8.0, 'L0_attn_Wk': 8.0, 'L0_attn_Wv': 8.0, 'L0_attn_Wo': 8.0}
    for name, (base, spread) in spreads.items():
        noise = np.random.default_rng([zlib.crc32(name.encode()), seed]).standard_normal(out[name].shape)
        drawn = base * np.exp(spread * noise) if base else spread * noise
        out[name] = jnp.asarray(drawn.astype(out[name].dtype))
    for name, factor in factors.items():
        out[name] = (out[name] * factor).astype(out[name].dtype)
    return out
```

```python
import numpy as np

import concourse.bass as bass
import concourse.mybir as mybir

F32 = mybir.dt.float32
BF16 = mybir.dt.bfloat16
I32 = mybir.dt.int32
U32 = mybir.dt.uint32
ALU = mybir.AluOpType
ACT = mybir.ActivationFunctionType
AX = mybir.AxisListType

P = 128
NB, NT = 32, 256
TB = NT // P
H, HD = 16, 8
E, TOPK = 32, 2
TOK = NB * NT
QKVG = 3 * P + H
TERMS = (3, 2, 1)
ROWS = HD * sum(TERMS)
MROW = ROWS
UNITS = H // 2
GROUPS = H // 4
VW = 32
REGION = TOK + P
DUMP = E * REGION
MAX_TILES = (TOPK * TOK + E * (P - 1)) // P
TG = 4
GROUPS_E = -(-MAX_TILES // TG)
GROUPS_E += GROUPS_E % 2
TILES = GROUPS_E * TG
LN_EPS, RMS_EPS = 1e-5, 1e-6
SCALE = float(HD) ** -0.5
TABLE_STEPS = 19
MAX_HEADS = (3, 2, 3, 2, 3, 3, 0, 0)
STAGES = (("L", 3), ("N", 3), ("P", 2), ("M", 1), ("A", 0), ("X", 0), ("O", -1), ("R", -2))
SA, CA, GA, GABO, SB, CB, GB, MODS = range(8)
assert sum(MAX_HEADS) == H


def build(nc, x, Wq, bq, Wk, bk, Wv, bv, Wo, bo, qn_w, kn_w, router_w, expert_w, c_in, wmod, out):
    from contextlib import ExitStack

    ctx = ExitStack()
    LOADS = 16 * (13 + 2 * HD)

    def sb(name, shape, dt=F32):
        return ctx.enter_context(nc.sbuf_tensor(name, shape, dt))

    def ps(name, shape, dt=F32):
        return ctx.enter_context(nc.psum_tensor(name, shape, dt))

    def sem(name):
        return ctx.enter_context(nc.semaphore(name))

    def dram(name, shape, dt=F32):
        return nc.dram_tensor(name, shape, dt, kind="Internal").ap()

    with ctx:
        mod_d = dram("mod_d", (NB, MODS * P))
        q_d = dram("q_d", (2, sum(TERMS), P, NT), BF16)
        k_d = dram("k_d", (2, 3, P, NT), BF16)
        x1_d = dram("x1_d", (NB, NT, P))
        xs_d = dram("xs_d", (DUMP + P, P))
        ys_d = dram("ys_d", (TILES * P, P))

        ident = sb("ident", [P, P])
        ones_f = sb("ones_f", [P, P])
        tri = sb("tri", [P, P], BF16)
        ones_b = sb("ones_b", [P, P], BF16)
        iota_e = sb("iota_e", [P, E])
        iota_t = sb("iota_t", [P, 2])
        iota_n = sb("iota_n", [P, TOK // P])
        region0 = sb("region0", [P, E])
        eps = sb("eps", [P, 2])
        zeros = sb("zeros", [P, P])
        wqkv = sb("wqkv", [P, QKVG])
        bqkv = sb("bqkv", [P, QKVG])
        wo = sb("wo", [P, P])
        bo_b = sb("bo_b", [P, P])
        wraw = sb("wraw", [P, 2 * P])
        braw = sb("braw", [P, 2 * P])
        w_col = sb("w_col", [P, 2])
        rw = sb("rw", [E, P])
        rwT = sb("rwT", [P, E])
        we = sb("we", [P, E * P])
        c_sb = sb("c_sb", [NB, P])
        sc = sb("sc", [NB, P])
        cT = sb("cT", [P, NB])
        wm = sb("wm", [P, 6 * P])
        mod = sb("mod", [NB, MODS * P])
        sgn = sb("sgn", [NB, P])
        mag = sb("mag", [NB, P])

        x_p = sb("x_p", [P, 2, TB, P])
        mod_p = sb("mod_p", [P, 2, 2, P])
        st1 = sb("st1", [P, TB, 6])
        mv1 = sb("mv1", [P, TB, 2])
        lnv1 = sb("lnv1", [P, TB])
        y1 = sb("y1", [P, TB])
        n1 = sb("n1", [P, TB])
        n1b = sb("n1b", [P, TB])
        rstd1 = sb("rstd1", [P, TB])
        xh1 = sb("xh1", [P, TB, P])
        h1a = sb("h1a", [P, TB, P])
        h1 = sb("h1", [P, TB, P])
        hT = sb("hT", [P, NT])
        qkvg = sb("qkvg", [P, 2, TB, QKVG])
        sq = sb("sq", [P, TB, 2 * P])
        ss = sb("ss", [P, TB * 2 * H])
        ms = sb("ms", [P, TB * 2 * H])
        lnm = sb("lnm", [P, TB * 2 * H])
        r0 = sb("r0", [P, TB * 2 * H])
        n2 = sb("n2", [P, TB * 2 * H])
        n2b = sb("n2b", [P, TB * 2 * H])
        rr = sb("rr", [P, TB * 2 * H])
        qn = sb("qn", [P, TB, 2 * P])
        parts = sb("parts", [P, 2, 3, NT], BF16)
        rest = sb("rest", [P, 2, NT])
        q_aug = [sb(f"q_aug{i}", [64, H, NT], BF16) for i in range(2)]
        k_aug = [sb(f"k_aug{i}", [64, H, NT], BF16) for i in range(2)]
        negmax = sb("negmax", [P, TB, H])
        mhi = sb("mhi", [H, NT], BF16)
        mmid = sb("mmid", [H, NT], BF16)
        v_aug = [sb(f"v_aug{i}", [P, TB, H, VW]) for i in range(2)]
        eg = sb("eg", [P, 2, TB, H])
        pr = [sb(f"pr{i}", [P, 2, TB, NT]) for i in range(4)]
        oT = sb("oT", [P, GROUPS, NT])
        den = sb("den", [P, TB, H])
        fac = sb("fac", [P, TB, H])
        on = sb("on", [P, TB, P])
        onT = sb("onT", [P, NT])
        x_o = sb("x_o", [P, 2, TB, P])
        mod_o = sb("mod_o", [P, 2, 4, P])
        xga = sb("xga", [P, TB, P])
        attg = sb("attg", [P, TB, P])
        x1 = sb("x1", [P, 2, TB, P])
        st2 = sb("st2", [P, TB, 6])
        mv2 = sb("mv2", [P, TB, 2])
        lnv2 = sb("lnv2", [P, TB])
        y2 = sb("y2", [P, TB])
        n3 = sb("n3", [P, TB])
        n3b = sb("n3b", [P, TB])
        rstd2 = sb("rstd2", [P, TB])
        xh2 = sb("xh2", [P, TB, P])
        h2a = sb("h2a", [P, TB, P])
        h2 = sb("h2", [P, 2, TB, P])
        h2T = sb("h2T", [P, NT])
        lg = sb("lg", [P, TB, E])
        top = sb("top", [P, TB, 8])
        topi = sb("topi", [P, TB, 8], U32)
        dlg = sb("dlg", [P, TB, E + TOPK])
        elg = sb("elg", [P, TB, E + TOPK])
        esum = sb("esum", [P, TB])
        rsum = sb("rsum", [P, TB])
        idx = sb("idx", [P, TOPK, TB])
        oh = sb("oh", [P, TOPK, TB, E])
        mask = sb("mask", [P, TB, E], BF16)
        carry = sb("carry", [P, E])
        rk = sb("rk", [P, TB, E])
        ohr = sb("ohr", [P, TOPK, TB, E])
        slot_f = sb("slot_f", [P, TOPK * TB])
        slot = sb("slot", [P, 2, TOPK * TB], U32)
        slot_all = sb("slot_all", [P, NB * TOPK * TB])
        idx_all = sb("idx_all", [P, NB * TOPK * TB])
        p_all = sb("p_all", [P, NB * TOPK * TB])
        gtn = sb("gtn", [P, E, TOK // P])
        cnt = sb("cnt", [P, E])
        ntile = sb("ntile", [P, E])
        tend = sb("tend", [P, E])
        tbeg = sb("tbeg", [P, E])
        tb128 = sb("tb128", [P, E])
        cmap = sb("cmap", [P, E])
        delta = sb("delta", [P, E])
        tge = sb("tge", [P, 2, E])
        tlt = sb("tlt", [P, 2, E])
        tin = sb("tin", [P, 2, E])
        tsel = sb("tsel", [P, 2, E])
        tse = sb("tse", [P, 2, E])
        tcol = sb("tcol", [P, 4])
        tcol2 = sb("tcol2", [P, 2])
        tnum = sb("tnum", [P, 2])
        table = sb("table", [P, 4 * P], I32)
        tail = sb("tail", [P, E], I32)
        xs_sb = [sb(f"xs{i}", [P, TG, P]) for i in range(2)]
        xsT = [sb(f"xsT{i}", [P, TG * P]) for i in range(2)]
        ys_sb = [sb(f"ys{i}", [P, TG, P]) for i in range(2)]
        NPAIR = NB * TOPK * TB
        CH = 32
        ohd = sb("ohd", [P, CH, E])
        ohd2 = sb("ohd2", [P, CH, E])
        dsl = sb("dsl", [P, NPAIR])
        gidx_f = sb("gidx_f", [P, NPAIR])
        gidx = sb("gidx", [P, NPAIR], I32)
        gi = sb("gi", [P, 2, TOPK * TB], U32)
        yg = sb("yg", [P, 2, TOPK * TB, P])
        x1_f = sb("x1_f", [P, 2, TB, P])
        gb_f = sb("gb_f", [P, 2, P])
        yw = sb("yw", [P, TB, P])
        yc = sb("yc", [P, TB, P])
        yb = sb("yb", [P, TB, P])
        of = sb("of", [P, 2, TB, P])

        st_ps = [ps(f"st_ps{i}", [P, 2, TB, NT]) for i in range(2)]
        mx_ps = [ps(f"mx_ps{i}", [P, TB, NT]) for i in range(2)]
        o_ps = ps("o_ps", [P, 512])
        misc = ps("misc", [P, 512])

        loads = sem("loads")
        we_ld = sem("we_ld")
        perm = sem("perm")
        gp_const = sem("gp_const")
        dve_const = sem("dve_const")
        s_exp = sem("s_exp")
        s_e1 = sem("s_e1")
        s_sc = sem("s_sc")
        cT_ps, cT_done, mod_ps, mod_sb, rwT_ps, rwT_done = (
            sem(n) for n in ("cT_ps", "cT_done", "mod_ps", "mod_sb", "rwT_ps", "rwT_done"))
        clamp = sem("clamp")
        mod_st = sem("mod_st")
        xp_ld = [sem(f"xp_ld{i}") for i in range(2)]
        xo_ld = [sem(f"xo_ld{i}") for i in range(2)]
        st1_d, mv1_d, lnv1_d, y1_d, n1_d, n1b_d, rstd1_d, xh1_d, h1a_d, h1_d = (
            sem(n) for n in ("st1_d", "mv1_d", "lnv1_d", "y1_d", "n1_d", "n1b_d", "rstd1_d", "xh1_d", "h1a_d", "h1_d"))
        hT_ps, hT_d, qkv_ps, qkv_d = (sem(n) for n in ("hT_ps", "hT_d", "qkv_ps", "qkv_d"))
        sq_d, ss_d, ms_d, lnm_d, r0_d, n2_d, n2b_d, rr_d, qn_d = (
            sem(n) for n in ("sq_d", "ss_d", "ms_d", "lnm_d", "r0_d", "n2_d", "n2b_d", "rr_d", "qn_d"))
        qkT_ps, hi_d, rest_d, mid_d, lo_d = (sem(n) for n in ("qkT_ps", "hi_d", "rest_d", "mid_d", "lo_d"))
        parts_st = sem("parts_st")
        aug_ld = [[sem(f"aug_ld{i}{j}") for j in range(2)] for i in range(2)]
        mps_r, mx_d = sem("mps_r"), sem("mx_d")
        mT_ps, mhi_d, mmid_d = sem("mT_ps"), sem("mhi_d"), sem("mmid_d")
        mrow_ld = sem("mrow_ld")
        v_d, eg_d = sem("v_d"), sem("eg_d")
        st_r, exp_d = sem("st_r"), sem("exp_d")
        pv_d, oT_d = sem("pv_d"), sem("oT_d")
        o2_ps, den_d, fac_d, on_d = sem("o2_ps"), sem("den_d"), sem("fac_d"), sem("on_d")
        onT_ps, onT_d, wo_ps, xga_d, attg_d, x1_done, x1_st = (
            sem(n) for n in ("onT_ps", "onT_d", "wo_ps", "xga_d", "attg_d", "x1_done", "x1_st"))
        st2_d, mv2_d, lnv2_d, y2_d, n3_d, n3b_d, rstd2_d, xh2_d, h2a_d, h2_d = (
            sem(n) for n in ("st2_d", "mv2_d", "lnv2_d", "y2_d", "n3_d", "n3b_d", "rstd2_d", "xh2_d", "h2a_d", "h2_d"))
        h2T_ps, h2T_d, lg_ps, lg_d, top_d, topi_d, dlg_d, elg_d, esum_d, rsum_d, p_d, idx_d, idxa_d, oh_d, mask_d = (
            sem(n) for n in ("h2T_ps", "h2T_d", "lg_ps", "lg_d", "top_d", "topi_d", "dlg_d", "elg_d", "esum_d",
                             "rsum_d", "p_d", "idx_d", "idxa_d", "oh_d", "mask_d"))
        rank_ps, rk_d, carry_d, ohr_d, slotf_d, slot_d, slota_d = (
            sem(n) for n in ("rank_ps", "rk_d", "carry_d", "ohr_d", "slotf_d", "slot_d", "slota_d"))
        scat = [sem(f"scat{i}") for i in range(2)]
        tab = sem("tab")
        tab_ps, table_d, tail_st, dump_st = sem("tab_ps"), sem("table_d"), sem("tail_st"), sem("dump_st")
        xs_ld = [sem(f"xs_ld{i}") for i in range(2)]
        xsT_ps, xsT_d, ye_ps, ye_d = sem("xsT_ps"), sem("xsT_d"), sem("ye_ps"), sem("ye_d")
        ys_st = [sem(f"ys_st{i}") for i in range(2)]
        look = sem("look")
        gidx_d, gi_d = sem("gidx_d"), sem("gi_d")
        yg_ld = [sem(f"yg_ld{i}") for i in range(2)]
        f_ld = [sem(f"f_ld{i}") for i in range(2)]
        yw_d, yc_d, yb_d, of_d = sem("yw_d"), sem("yc_d"), sem("yb_d"), sem("of_d")
        out_st = [sem(f"out_st{i}") for i in range(2)]

        def wait(eng, s, n):
            if isinstance(n, int) and n <= 0:
                return
            eng.wait_ge(s, n)

        class Step:

            def __init__(self, s, parity=None, pair=None):
                self.s, self.parity, self.pair = s, parity if parity is not None else s % 2, pair

            def at(self, k):
                return self.s + k

            def par(self, k):
                return (self.parity + k) % 2

            def nth(self, k):
                if self.pair is None:
                    return (self.s + k) // 2
                return self.pair + (self.parity + k - self.par(k)) // 2

        def stages(s):
            return {n for n, k in STAGES if 0 <= s + k < NB}

        def run(eng, step):
            for s in range(-3, 2):
                step(Step(s), stages(s))
            with eng.Fori(1, NB // 2 - 2) as pair:
                for parity in range(2):
                    step(Step(pair * 2 + parity, parity, pair), {n for n, _ in STAGES})
            for s in range(NB - 4, NB + 2):
                step(Step(s), stages(s))

        block = ctx.enter_context(nc.Block())

        @block.sync
        def _(sp):
            for dst, src in (
                (c_sb[:], c_in), (wm[:], wmod), (rw[:], router_w), (wraw[:, 0:P], Wq[:, 0:P]), (wraw[:, P:2 * P], Wk),
                (wqkv[:, 2 * P:3 * P], Wv), (wqkv[:, 3 * P:QKVG], Wq[:, P:P + H]),
                (braw[:, 0:P], bq[0:P].partition_broadcast(P)), (braw[:, P:2 * P], bk.partition_broadcast(P)),
                (bqkv[:, 2 * P:3 * P], bv.partition_broadcast(P)), (bqkv[:, 3 * P:QKVG], bq[P:P + H].partition_broadcast(P)),
                (wo[:], Wo), (bo_b[:], bo.partition_broadcast(P)),
            ):
                sp.dma_start(dst, src).then_inc(loads, 16)
            for d in range(HD):
                for k, w in enumerate((qn_w, kn_w)):
                    sp.dma_start(w_col[d * H:(d + 1) * H, k:k + 1], w[d:d + 1].partition_broadcast(H)).then_inc(loads, 16)
            sp.wait_ge(mod_sb, 3)
            sp.dma_start(mod_d, mod[:]).then_inc(mod_st, 16)
            sp.wait_ge(dve_const, 1)
            sp.dma_start(xs_d[DUMP:DUMP + P, :], zeros[:]).then_inc(dump_st, 16)
            sp.wait_ge(mod_st, 16)

            def load_x(dst, s, b):
                sp.dma_start(dst, x[b].rearrange("(p t) f -> p t f", t=TB) if isinstance(b, int)
                             else x[bass.ds(b, 1)].rearrange("o (p t) f -> (o p) t f", t=TB)).then_inc(s, 16)

            def mod_rows(dst, s, b, lo, n):
                row = mod_d[b, lo * P:(lo + n) * P] if isinstance(b, int) else \
                    mod_d[bass.ds(b, 1), lo * P:(lo + n) * P].rearrange("o f -> (o f)")
                sp.dma_start(dst, row.partition_broadcast(P)).then_inc(s, 16)

            def aug_loads(st, j):
                par, b, nth = st.par(2), st.at(2), st.nth(2)
                wait(sp, st_r, UNITS * (b - 2) + (j + 1) * UNITS // 2)
                hs = slice(j * H // 2, (j + 1) * H // 2)
                loaded = aug_ld[par][j]
                sp.dma_start(q_aug[par][0:ROWS, hs, :],
                             q_d[par].rearrange("a (d h) t -> (a d) h t", h=H)[:, hs]).then_inc(loaded, 16)
                row = 0
                for n in TERMS:
                    sp.dma_start(k_aug[par][row:row + n * HD, hs, :],
                                 k_d[par, 0:n].rearrange("a (d h) t -> (a d) h t", h=H)[:, hs]).then_inc(loaded, 16)
                    row += n * HD

            def step(st, do):
                if "L" in do:
                    b, par = st.at(3), st.par(3)
                    wait(sp, xh1_d, b - 1)
                    wait(sp, h1_d, b - 1)
                    load_x(x_p[:, par], xp_ld[par], b)
                    mod_rows(mod_p[:, par].rearrange("p a f -> p (a f)"), xp_ld[par], b, SA, 2)
                if "X" in do:
                    b, par = st.at(0), st.par(0)
                    wait(sp, h2_d, b - 1)
                    load_x(x_o[:, par], xo_ld[par], b)
                    mod_rows(mod_o[:, par].rearrange("p a f -> p (a f)"), xo_ld[par], b, GA, 4)
                if isinstance(st.s, int) and st.s == -3:
                    sp.dma_start(we[:].rearrange("k (e n) -> k e n", e=E), expert_w.rearrange("e k n -> k e n")).then_inc(we_ld, 16)
                if "O" in do:
                    b, par = st.at(-1), st.par(-1)
                    wait(sp, x1_done, b + 1)
                    dst = x1_d[b] if isinstance(b, int) else x1_d[bass.ds(b, 1)].rearrange("o t f -> (o t) f")
                    sp.dma_start(dst.rearrange("(p t) f -> p t f", t=TB), x1[:, par]).then_inc(x1_st, 16)
                if "P" in do:
                    b, par = st.at(2), st.par(2)
                    wait(sp, lo_d, b + 1)
                    row = 0
                    for a, n in enumerate(TERMS):
                        sp.dma_start(q_d[par, row:row + n].rearrange("a p t -> p a t"),
                                     parts[:, 0, a:a + 1, :].broadcast_to([P, n, NT])).then_inc(parts_st, 16)
                        row += n
                    sp.dma_start(k_d[par].rearrange("a p t -> p a t"), parts[:, 1]).then_inc(parts_st, 16)
                if "M" in do:
                    b, par = st.at(1), st.par(1)
                    wait(sp, mhi_d, b + 1)
                    wait(sp, mmid_d, b + 1)
                    sp.dma_start(q_aug[par][MROW:MROW + 1], mhi[:]).then_inc(mrow_ld, 16)
                    sp.dma_start(q_aug[par][MROW + 1:MROW + 2], mmid[:]).then_inc(mrow_ld, 16)
                if "P" in do:
                    wait(sp, parts_st, 64 * (st.at(2) + 1))
                    aug_loads(st, 0)
                    aug_loads(st, 1)

            run(sp, step)

            for i in range(2):
                sp.wait_ge(scat[i], 16 * TOPK * TB * NB // 2)
            sp.wait_ge(table_d, 1)
            sp.wait_ge(dump_st, 16)
            with sp.Fori(0, E) as e:
                row = sp.value_load(tail[0:1, bass.ds(e, 1)], min_val=0, max_val=DUMP - P)
                sp.dma_start(xs_d[bass.ds(row, P), :], zeros[:]).then_inc(tail_st, 16)
            sp.wait_ge(tail_st, 16 * E)
            sp.wait_ge(table_d, 2)

            def rows_in(g, i, first):
                if not first:
                    sp.wait_ge(xsT_ps, g - 1)
                for k in range(TG):
                    row = sp.value_load(table[0:1, bass.ds(g * TG + k, 1)], min_val=0, max_val=DUMP)
                    sp.dma_start(xs_sb[i][:, k, :], xs_d[bass.ds(row, P), :]).then_inc(xs_ld[i], 16)

            rows_in(0, 0, True)
            rows_in(1, 1, True)
            with sp.Fori(1, GROUPS_E // 2) as n:
                for i in range(2):
                    rows_in(n * 2 + i, i, False)

            sp.wait_ge(x1_st, 16 * NB)

            def final_loads(b, nth, par):
                wait(sp, of_d, b - 1)
                src = x1_d[b] if isinstance(b, int) else x1_d[bass.ds(b, 1)].rearrange("o t f -> (o t) f")
                sp.dma_start(x1_f[:, par], src.rearrange("(p t) f -> p t f", t=TB)).then_inc(f_ld[par], 16)
                mod_rows(gb_f[:, par], f_ld[par], b, GB, 1)

            def final_store(b, par):
                wait(sp, of_d, b + 1)
                dst = out[b] if isinstance(b, int) else out[bass.ds(b, 1)].rearrange("o t f -> (o t) f")
                sp.dma_start(dst.rearrange("(p t) f -> p t f", t=TB), of[:, par]).then_inc(out_st[par], 16)

            final_loads(0, 0, 0)
            final_loads(1, 0, 1)
            with sp.Fori(1, NB // 2) as n:
                for par in range(2):
                    final_store(n * 2 + (par - 2), par)
                    final_loads(n * 2 + par, n, par)
            final_store(NB - 2, 0)
            final_store(NB - 1, 1)
            for i in range(2):
                sp.wait_ge(out_st[i], 16 * NB // 2)

        @block.gpsimd
        def _(gp):
            nc.gpsimd.memset(ones_f[:], 1.0).then_inc(gp_const, 1)
            nc.gpsimd.memset(ones_b[:], 1.0).then_inc(gp_const, 1)
            gp.wait_ge(gp_const, 2)
            nc.gpsimd.affine_select(out=ident[:], in_=ones_f[:], pattern=[[1, P]], compare_op=ALU.is_equal,
                                    fill=0.0, base=0, channel_multiplier=-1).then_inc(gp_const, 1)
            nc.gpsimd.affine_select(out=tri[:], in_=ones_b[:], pattern=[[1, P]], compare_op=ALU.is_gt,
                                    fill=0.0, base=0, channel_multiplier=-1).then_inc(gp_const, 1)
            for dst, pattern, mult in (
                (iota_e, [[1, E]], 0), (iota_t, [[P, 2]], 1), (iota_n, [[P, TOK // P]], 0), (region0, [[REGION, E]], 0),
                (carry, [[REGION, E]], 0),
            ):
                nc.gpsimd.iota(dst[:], pattern=pattern, base=0, channel_multiplier=mult,
                               allow_small_or_imprecise_dtypes=True).then_inc(gp_const, 1)
            for i in range(2):
                nc.gpsimd.memset(v_aug[i][:], 0.0).then_inc(gp_const, 1)
                nc.gpsimd.memset(k_aug[i][:], 1.0).then_inc(gp_const, 1)
            gp.wait_ge(gp_const, 13)
            for i in range(2):
                nc.gpsimd.memset(v_aug[i][:, :, :, HD:HD + 1], 1.0).then_inc(gp_const, 1)

            def scatter(st, k):
                par = st.par(-2)
                j, t = divmod(k, TB)
                nc.gpsimd.indirect_dma_start(xs_d, bass.IndirectOffsetOnAxis(ap=slot[:, par, k:k + 1], axis=0),
                                             h2[:, par, t, :], None).then_inc(scat[par], 16)

            def step(st, do):
                if "M" in do:
                    b, par = st.at(1), st.par(1)
                    wait(gp, qkv_d, TB * (b + 1))
                    wait(gp, pv_d, GROUPS * (b - 1))
                    gp.nop(nofuse=True)
                    nc.gpsimd.tensor_copy(v_aug[par][:, :, :, 0:HD],
                                          qkvg[:, par, :, 2 * P:3 * P].rearrange("p t (h d) -> p t h d", d=HD)).then_inc(v_d, 1)
                if "O" in do:
                    b, par, nth = st.at(-1), st.par(-1), st.nth(-1)
                    wait(gp, xo_ld[par], 32 * (nth + 1))
                    nc.gpsimd.tensor_tensor(xga[:], x_o[:, par], mod_o[:, par, 1:2, :].broadcast_to([P, TB, P]),
                                            ALU.add).then_inc(xga_d, 1)
                if "R" in do:
                    wait(gp, slot_d, st.at(-2) + 1)
                    gp.nop(nofuse=True)
                    scatter(st, 0)
                if "P" in do:
                    b, par = st.at(2), st.par(2)
                    wait(gp, rr_d, b + 1)
                    gp.nop(nofuse=True)
                    for t in range(TB):
                        nc.gpsimd.tensor_tensor(
                            qn[:, t].rearrange("p (k d h) -> p k d h", k=2, h=H),
                            qkvg[:, par, t, 0:2 * P].rearrange("p (k d h) -> p k d h", k=2, h=H),
                            rr[:, t * 2 * H:(t + 1) * 2 * H].rearrange("p (k h) -> p k h", h=H).unsqueeze(2).broadcast_to(
                                [P, 2, HD, H]), ALU.mult).then_inc(qn_d, 1)
                if "O" in do:
                    b, par = st.at(-1), st.par(-1)
                    wait(gp, attg_d, b + 1)
                    wait(gp, xga_d, b + 1)
                    wait(gp, x1_st, 16 * (b - 1))
                    nc.gpsimd.tensor_tensor(x1[:, par], attg[:], xga[:], ALU.add).then_inc(x1_done, 1)
                if "R" in do:
                    scatter(st, 1)
                if "P" in do:
                    b, par = st.at(2), st.par(2)
                    wait(gp, rest_d, b + 1)
                    wait(gp, parts_st, 64 * b)
                    gp.nop(nofuse=True)
                    nc.gpsimd.tensor_copy(parts[:, :, 1], rest[:]).then_inc(mid_d, 1)
                    wait(gp, mid_d, b + 1)
                    nc.gpsimd.tensor_tensor(parts[:, :, 2], rest[:], parts[:, :, 1], ALU.subtract).then_inc(lo_d, 1)
                if "O" in do:
                    b, par = st.at(-1), st.par(-1)
                    wait(gp, xh2_d, b + 1)
                    gp.nop(nofuse=True)
                    nc.gpsimd.tensor_tensor(h2a[:], xh2[:], mod_o[:, par, 3:4, :].broadcast_to([P, TB, P]),
                                            ALU.mult).then_inc(h2a_d, 1)
                    wait(gp, h2a_d, b + 1)
                    wait(gp, scat[par], 64 * st.nth(-1))
                    nc.gpsimd.tensor_tensor(h2[:, par], h2a[:], mod_o[:, par, 2:3, :].broadcast_to([P, TB, P]),
                                            ALU.add).then_inc(h2_d, 1)
                if "R" in do:
                    scatter(st, 2)
                if "N" in do:
                    b, par, nth = st.at(3), st.par(3), st.nth(3)
                    wait(gp, xp_ld[par], 32 * (nth + 1))
                    wait(gp, xh1_d, b + 1)
                    gp.nop(nofuse=True)
                    nc.gpsimd.tensor_tensor(h1a[:], xh1[:], mod_p[:, par, 1:2, :].broadcast_to([P, TB, P]),
                                            ALU.mult).then_inc(h1a_d, 1)
                    wait(gp, h1a_d, b + 1)
                    wait(gp, hT_ps, b)
                    nc.gpsimd.tensor_tensor(h1[:], h1a[:], mod_p[:, par, 0:1, :].broadcast_to([P, TB, P]),
                                            ALU.add).then_inc(h1_d, 1)
                if "R" in do:
                    scatter(st, 3)

            run(gp, step)

            for i in range(2):
                gp.wait_ge(ys_st[i], 16 * GROUPS_E // 2)

            def gathers(b, par):
                wait(gp, gi_d, b + 1)
                wait(gp, yc_d, TB * (b - 1))
                gp.nop(nofuse=True)
                for k in range(TOPK * TB):
                    nc.gpsimd.indirect_dma_start(
                        yg[:, par, k, :], None, ys_d,
                        bass.IndirectOffsetOnAxis(ap=gi[:, par, k:k + 1], axis=0)).then_inc(yg_ld[par], 16)

            gathers(0, 0)
            gathers(1, 1)
            with gp.Fori(1, NB // 2) as n:
                for par in range(2):
                    gathers(n * 2 + par, par)

        @block.scalar
        def _(act):
            act.preload_act_table_set("natural_log_exp_and_others")
            act.wait_ge(loads, LOADS)
            nc.scalar.activation(sc[:], c_sb[:], ACT.Exp, scale=-1.0).then_inc(s_exp, 1)
            act.wait_ge(cT_ps, 1)
            nc.scalar.activation(cT[:], misc[:, 0:NB], ACT.Copy).then_inc(cT_done, 1)
            act.wait_ge(rwT_ps, 1)
            nc.scalar.activation(rwT[:], misc[:, 0:E], ACT.Copy).then_inc(rwT_done, 1)
            act.wait_ge(dve_const, 3)

            def rsqrt_seed(b, src, scale, bias, ready, tmp, tmp_d, dst, dst_d):
                wait(act, ready, b + 1)
                nc.scalar.activation(tmp, src, ACT.Ln, bias=bias, scale=scale).then_inc(tmp_d, 1)
                wait(act, tmp_d, b + 1)
                nc.scalar.activation(dst, tmp, ACT.Exp, scale=-0.5).then_inc(dst_d, 1)

            def exp_unit(b, u):
                wait(act, st_r, UNITS * b + u + 1)
                wait(act, pv_d, GROUPS * b + u // 2 - 1)
                nc.scalar.activation(pr[u % 4][:], st_ps[u % 2][:], ACT.Exp, scale=SCALE).then_inc(exp_d, 1)

            def o_evacuate(b, g):
                wait(act, pv_d, GROUPS * b + g + 1)
                wait(act, o2_ps, TB * b)
                nc.scalar.activation(oT[:, g, :], o_ps[:, 0:NT], ACT.Copy).then_inc(oT_d, 1)

            def step(st, do):
                for u in range(UNITS):
                    if "A" in do:
                        exp_unit(st.at(0), u)
                    if u == 0 and "O" in do:
                        o_evacuate(st.at(-1), GROUPS - 1)
                    if u == 0 and "P" in do:
                        b = st.at(2)
                        wait(act, hT_ps, b + 1)
                        wait(act, qkv_ps, TB * b)
                        nc.scalar.activation(hT[:], misc[:, 0:NT], ACT.Copy).then_inc(hT_d, 1)
                    if u in (2, 4, 6) and "A" in do:
                        o_evacuate(st.at(0), u // 2 - 1)
                    if u == 1 and "M" in do:
                        b, par = st.at(1), st.par(1)
                        wait(act, qkv_d, TB * (b + 1))
                        wait(act, den_d, TB * (b - 1))
                        nc.scalar.activation(eg[:, par], qkvg[:, par, :, 3 * P:QKVG], ACT.Exp, scale=-1.0).then_inc(eg_d, 1)
                    if u == 2 and "O" in do:
                        b = st.at(-1)
                        wait(act, onT_ps, b + 1)
                        wait(act, wo_ps, b)
                        nc.scalar.activation(onT[:], misc[:, 0:NT], ACT.Copy).then_inc(onT_d, 1)
                    if u == 2 and "P" in do:
                        b, par = st.at(2), st.par(2)
                        wait(act, qkv_d, TB * (b + 1))
                        wait(act, ss_d, b)
                        nc.scalar.activation(sq[:], qkvg[:, par, :, 0:2 * P], ACT.Square).then_inc(sq_d, 1)
                    if u == 3 and "P" in do:
                        rsqrt_seed(st.at(2), ss[:], 1.0 / HD, eps[:, 1:2], ss_d, lnm[:], lnm_d, r0[:], r0_d)
                    if u == 4 and "O" in do:
                        rsqrt_seed(st.at(-1), mv2[:, :, 1], 1.0, eps[:, 0:1], mv2_d, lnv2[:], lnv2_d, y2[:], y2_d)
                    if u == 4 and "P" in do:
                        b = st.at(2)
                        wait(act, qkT_ps, b + 1)
                        wait(act, parts_st, 64 * b)
                        for k in range(2):
                            nc.scalar.activation(parts[:, k, 0], misc[:, k * NT:(k + 1) * NT], ACT.Copy,
                                                 scale=w_col[:, k:k + 1]).then_inc(hi_d, 1)
                    if u == 6 and "M" in do:
                        b = st.at(1)
                        wait(act, mT_ps, b + 1)
                        wait(act, mrow_ld, 32 * b)
                        nc.scalar.activation(mhi[:], misc[0:H, 0:NT], ACT.Copy).then_inc(mhi_d, 1)
                    if u == 6 and "N" in do:
                        rsqrt_seed(st.at(3), mv1[:, :, 1], 1.0, eps[:, 0:1], mv1_d, lnv1[:], lnv1_d, y1[:], y1_d)
                    if u == 6 and "O" in do:
                        b = st.at(-1)
                        wait(act, h2T_ps, b + 1)
                        wait(act, lg_ps, b)
                        nc.scalar.activation(h2T[:], misc[:, 0:NT], ACT.Copy).then_inc(h2T_d, 1)
                    if u == 7 and "O" in do:
                        b = st.at(-1)
                        wait(act, dlg_d, 2 * (b + 1))
                        wait(act, esum_d, b)
                        wait(act, p_d, b)
                        nc.scalar.activation(elg[:], dlg[:], ACT.Exp).then_inc(elg_d, 1)

            run(act, step)

            def results(g, nth, i, first):
                act.wait_ge(ye_ps, g + 1)
                if not first:
                    act.wait_ge(ys_st[i], 16 * nth)
                nc.scalar.activation(ys_sb[i][:].rearrange("p k f -> p (k f)"), st_ps[1][:, i].rearrange("p a b -> p (a b)"),
                                     ACT.Copy).then_inc(ye_d, 1)
                act.wait_ge(ye_d, g + 1)
                if isinstance(g, int):
                    dst = ys_d[g * TG * P:(g + 1) * TG * P, :]
                else:
                    dst = ys_d[bass.ds(g * (TG * P), TG * P), :]
                act.dma_start(dst.rearrange("(k p) f -> p k f", p=P), ys_sb[i][:]).then_inc(ys_st[i], 16)

            results(0, 0, 0, True)
            results(1, 0, 1, True)
            with act.Fori(1, GROUPS_E // 2) as n:
                for i in range(2):
                    results(n * 2 + i, n, i, False)

        @block.vector
        def _(dve):
            v = nc.vector
            v.memset(zeros[:], 0.0).then_inc(dve_const, 1)
            v.memset(eps[:, 0:1], LN_EPS).then_inc(dve_const, 1)
            v.memset(eps[:, 1:2], RMS_EPS).then_inc(dve_const, 1)
            dve.wait_ge(s_exp, 1)
            v.tensor_scalar(sgn[:], sc[:], 1.0, None, ALU.add).then_inc(s_e1, 1)
            dve.wait_ge(s_e1, 1)
            v.reciprocal(mag[:], sgn[:]).then_inc(s_e1, 1)
            dve.wait_ge(s_e1, 2)
            v.tensor_tensor(sc[:], c_sb[:], mag[:], ALU.mult).then_inc(s_sc, 1)
            dve.wait_ge(mod_ps, 1)
            v.tensor_copy(mod[:, SA * P:GABO * P], o_ps[0:NB, 0:3 * P]).then_inc(clamp, 1)
            v.tensor_copy(mod[:, SB * P:CB * P], o_ps[0:NB, 3 * P:4 * P]).then_inc(clamp, 1)
            v.tensor_copy(mod[:, CB * P:MODS * P], misc[0:NB, 0:2 * P]).then_inc(clamp, 1)
            dve.wait_ge(clamp, 3)
            k = 3
            for col in (CA, CB):
                m = mod[:, col * P:(col + 1) * P]
                v.tensor_scalar(m, m, 1.0, None, ALU.add).then_inc(mod_sb, 1)
            for col in (GA, GB):
                m = mod[:, col * P:(col + 1) * P]
                for ins in (
                    lambda: v.tensor_scalar(sgn[:], m, 0.0, 2.0, ALU.is_ge, ALU.mult),
                    lambda: v.scalar_tensor_tensor(mag[:], m, -1.0, m, ALU.mult, ALU.max),
                    lambda: v.tensor_scalar(mag[:], mag[:], 0.25, None, ALU.max),
                    lambda: v.scalar_tensor_tensor(m, sgn[:], -1.0, mag[:], ALU.add, ALU.mult),
                ):
                    ins().then_inc(clamp, 1)
                    k += 1
                    dve.wait_ge(clamp, k)
            v.tensor_tensor(mod[:, GABO * P:SB * P], mod[:, GA * P:GABO * P], bo_b[0:NB, :], ALU.mult).then_inc(mod_sb, 1)
            for raw, dst in ((wraw, wqkv), (braw, bqkv)):
                for k in range(2):
                    v.tensor_copy(dst[:, k * P:(k + 1) * P].rearrange("p (d h) -> p d h", h=H),
                                  raw[:, k * P:(k + 1) * P].rearrange("p (h d) -> p d h", d=HD)).then_inc(perm, 1)
            dve.wait_ge(perm, 4)
            dve.wait_ge(gp_const, 15)

            def newton(b, var, eps_v, y, t1, t1_d, t2, t2_d, dst, dst_d, ready, between=lambda: None):
                wait(dve, ready, b + 1)
                v.scalar_tensor_tensor(t1, y, -0.5, y, ALU.mult, ALU.mult).then_inc(t1_d, 1)
                between()
                wait(dve, t1_d, b + 1)
                v.scalar_tensor_tensor(t2, var, eps_v, t1, ALU.add, ALU.mult).then_inc(t2_d, 1)
                between()
                wait(dve, t2_d, b + 1)
                v.scalar_tensor_tensor(dst, t2, 1.5, y, ALU.add, ALU.mult).then_inc(dst_d, 1)
                between()

            def layernorm_stats(b, src, st_t, st_d, mv, mv_d, between=lambda: None):
                for t in range(TB):
                    v.bn_stats(st_t[:, t], src[:, t]).then_inc(st_d, 1)
                between()
                wait(dve, st_d, TB * (b + 1))
                dve.nop(nofuse=True)
                for t in range(TB):
                    ins = v.bn_aggr(mv[:, t], st_t[:, t])
                ins.then_inc(mv_d, 1)

            def normalise(b, src, mv, rstd, rstd_d, dst, dst_d):
                wait(dve, rstd_d, b + 1)
                for t in range(TB):
                    ins = v.tensor_scalar(dst[:, t], src[:, t], mv[:, t, 0:1], rstd[:, t:t + 1], ALU.subtract, ALU.mult)
                ins.then_inc(dst_d, 1)

            def step(st, do):
                heads = [0, 0]

                def max_head():
                    if "M" not in do or heads[0] >= heads[1]:
                        return
                    b, h = st.at(1), heads[0]
                    heads[0] += 1
                    wait(dve, mps_r, H * b + h + 1)
                    if h == 0:
                        wait(dve, mT_ps, b)
                    v.tensor_reduce(negmax[:, :, h], mx_ps[h % 2][:], AX.X, ALU.max, negate=True).then_inc(mx_d, 1)

                for u in range(UNITS):
                    heads[1] += MAX_HEADS[u]
                    if u == 1 and "O" in do:
                        b, par = st.at(-1), st.par(-1)
                        wait(dve, eg_d, b + 1)
                        o = misc[:].rearrange("p (h w) -> p h w", w=VW)
                        for qc in range(TB):
                            wait(dve, o2_ps, TB * b + qc + 1)
                            v.scalar_tensor_tensor(den[:, qc], eg[:, par, qc], 1.0, o[:, :, HD], ALU.add, ALU.mult).then_inc(den_d, 1)
                            wait(dve, den_d, TB * b + qc + 1)
                            v.reciprocal(fac[:, qc], den[:, qc]).then_inc(fac_d, 1)
                            wait(dve, fac_d, TB * b + qc + 1)
                            wait(dve, onT_ps, b)
                            v.tensor_tensor(on[:, qc].rearrange("p (h d) -> p h d", d=HD), o[:, :, 0:HD],
                                            fac[:, qc].unsqueeze(2).broadcast_to([P, H, HD]), ALU.mult).then_inc(on_d, 1)
                            max_head()
                    if u == 1 and "P" in do:
                        b, par = st.at(2), st.par(2)
                        wait(dve, v_d, b - 1)
                        wait(dve, eg_d, b - 1)
                        wait(dve, qn_d, TB * (b - 1))
                        for t in range(TB):
                            wait(dve, qkv_ps, TB * b + t + 1)
                            v.tensor_tensor(qkvg[:, par, t], misc[:, 0:QKVG], bqkv[:], ALU.add).then_inc(qkv_d, 1)
                            max_head()
                    if u == 2 and "R" in do:
                        b, par = st.at(-2), st.par(-2)
                        wait(dve, rank_ps, b + 1)
                        v.tensor_tensor(rk[:], misc[:, 0:TB * E].rearrange("p (t e) -> p t e", e=E),
                                        carry[:].unsqueeze(1).broadcast_to([P, TB, E]), ALU.add).then_inc(rk_d, 1)
                        wait(dve, rk_d, b + 1)
                        v.tensor_tensor(carry[:], misc[:, TB * E:(TB + 1) * E], carry[:], ALU.add).then_inc(carry_d, 1)
                        v.tensor_tensor(ohr[:].rearrange("p j t e -> p j (t e)"), oh[:].rearrange("p j t e -> p j (t e)"),
                                        rk[:].rearrange("p t e -> p (t e)").unsqueeze(1).broadcast_to([P, TOPK, TB * E]),
                                        ALU.mult).then_inc(ohr_d, 1)
                        max_head()
                        wait(dve, ohr_d, b + 1)
                        v.tensor_reduce(slot_f[:].rearrange("p (j t) -> p j t", t=TB), ohr[:], AX.X, ALU.add).then_inc(slotf_d, 1)
                        max_head()
                        wait(dve, slotf_d, b + 1)
                        v.tensor_copy(slot[:, par], slot_f[:]).then_inc(slot_d, 1)
                        v.tensor_copy(slot_all[:, bass.ts(b, TOPK * TB)], slot_f[:]).then_inc(slota_d, 1)
                    if u == 2 and "P" in do:
                        b = st.at(2)
                        wait(dve, sq_d, b + 1)
                        v.tensor_reduce(ss[:].rearrange("p (k h) -> p k h", h=H),
                                        sq[:].rearrange("p t (k d h) -> p (t k) h d", k=2, h=H), AX.X, ALU.add).then_inc(ss_d, 1)
                        max_head()
                        wait(dve, ss_d, b + 1)
                        v.tensor_scalar(ms[:], ss[:], 1.0 / HD, None, ALU.mult).then_inc(ms_d, 1)
                        if "R" in do:
                            wait(dve, slota_d, st.at(-2) + 1)
                    if u == 3 and "P" in do:
                        b = st.at(2)
                        max_head()
                        wait(dve, ms_d, b + 1)
                        wait(dve, qn_d, TB * b)
                        newton(b, ms[:], RMS_EPS, r0[:], n2[:], n2_d, n2b[:], n2b_d, rr[:], rr_d, r0_d, max_head)
                    if u == 3 and "O" in do:
                        b, par = st.at(-1), st.par(-1)
                        wait(dve, wo_ps, b + 1)
                        wait(dve, xo_ld[par], 32 * (st.nth(-1) + 1))
                        wait(dve, x1_done, b)
                        v.tensor_tensor(attg[:], misc[:, 0:NT].rearrange("p (t f) -> p t f", f=P),
                                        mod_o[:, par, 0:1, :].broadcast_to([P, TB, P]), ALU.mult).then_inc(attg_d, 1)
                    if u == 4 and "O" in do:
                        max_head()
                        b, par = st.at(-1), st.par(-1)
                        wait(dve, x1_done, b + 1)
                        layernorm_stats(b, x1[:, par], st2, st2_d, mv2, mv2_d, max_head)
                        max_head()
                    if u == 4 and "P" in do:
                        b = st.at(2)
                        wait(dve, hi_d, 2 * (b + 1))
                        wait(dve, lo_d, b)
                        for k in range(2):
                            ins = v.scalar_tensor_tensor(rest[:, k], misc[:, k * NT:(k + 1) * NT], w_col[:, k:k + 1],
                                                         parts[:, k, 0], ALU.mult, ALU.subtract)
                        ins.then_inc(rest_d, 1)
                    if u == 5 and "O" in do:
                        b, par = st.at(-1), st.par(-1)
                        newton(b, mv2[:, :, 1], LN_EPS, y2[:], n3[:], n3_d, n3b[:], n3b_d, rstd2[:], rstd2_d, y2_d, max_head)
                        wait(dve, h2a_d, b)
                        normalise(b, x1[:, par], mv2, rstd2, rstd2_d, xh2, xh2_d)
                    if u == 5 and "N" in do:
                        b, par, nth = st.at(3), st.par(3), st.nth(3)
                        wait(dve, xp_ld[par], 32 * (nth + 1))
                        layernorm_stats(b, x_p[:, par], st1, st1_d, mv1, mv1_d, max_head)
                    if u == 6 and "M" in do:
                        b = st.at(1)
                        wait(dve, mhi_d, b + 1)
                        wait(dve, mrow_ld, 32 * b)
                        v.tensor_tensor(mmid[:], misc[0:H, 0:NT], mhi[:], ALU.subtract).then_inc(mmid_d, 1)
                    if u == 6 and "N" in do:
                        b, par = st.at(3), st.par(3)
                        newton(b, mv1[:, :, 1], LN_EPS, y1[:], n1[:], n1_d, n1b[:], n1b_d, rstd1[:], rstd1_d, y1_d)
                        wait(dve, h1a_d, b)
                        normalise(b, x_p[:, par], mv1, rstd1, rstd1_d, xh1, xh1_d)
                    if u == 7 and "O" in do:
                        b, par = st.at(-1), st.par(-1)
                        wait(dve, lg_ps, b + 1)
                        v.tensor_copy(lg[:].rearrange("p t e -> p (t e)"), misc[:, 0:TB * E]).then_inc(lg_d, 1)
                        wait(dve, lg_d, b + 1)
                        dve.nop(nofuse=True)
                        for t in range(TB):
                            ins = v.max(top[:, t], lg[:, t])
                        ins.then_inc(top_d, 1)
                        wait(dve, top_d, b + 1)
                        wait(dve, elg_d, b)
                        v.tensor_tensor(dlg[:, :, 0:E], lg[:], top[:, :, 0:1].broadcast_to([P, TB, E]), ALU.subtract).then_inc(dlg_d, 1)
                        v.tensor_tensor(dlg[:, :, E:E + TOPK], top[:, :, 0:TOPK], top[:, :, 0:1].broadcast_to([P, TB, TOPK]),
                                        ALU.subtract).then_inc(dlg_d, 1)
                        for t in range(TB):
                            ins = v.max_index(topi[:, t], top[:, t], lg[:, t])
                        ins.then_inc(topi_d, 1)
                        wait(dve, topi_d, b + 1)
                        v.tensor_copy(idx[:], topi[:, :, 0:TOPK].rearrange("p t j -> p j t")).then_inc(idx_d, 1)
                        wait(dve, elg_d, b + 1)
                        v.tensor_reduce(esum[:], elg[:, :, 0:E], AX.X, ALU.add).then_inc(esum_d, 1)
                        wait(dve, idx_d, b + 1)
                        v.tensor_tensor(oh[:].rearrange("p j t e -> p (j t) e"),
                                        iota_e[:].unsqueeze(1).broadcast_to([P, TOPK * TB, E]),
                                        idx[:].rearrange("p j t -> p (j t)").unsqueeze(2).broadcast_to([P, TOPK * TB, E]),
                                        ALU.is_equal).then_inc(oh_d, 1)
                        wait(dve, esum_d, b + 1)
                        v.reciprocal(rsum[:], esum[:]).then_inc(rsum_d, 1)
                        wait(dve, oh_d, b + 1)
                        wait(dve, rank_ps, b)
                        v.tensor_tensor(mask[:], oh[:, 0], oh[:, 1], ALU.add).then_inc(mask_d, 1)
                        v.tensor_copy(idx_all[:, bass.ts(b, TOPK * TB)], idx[:].rearrange("p j t -> p (j t)")).then_inc(idxa_d, 1)
                        wait(dve, rsum_d, b + 1)
                        v.tensor_tensor(p_all[:, bass.ts(b, TOPK * TB)].rearrange("p (j t) -> p j t", t=TB),
                                        elg[:, :, E:E + TOPK].rearrange("p t j -> p j t"),
                                        rsum[:].unsqueeze(1).broadcast_to([P, TOPK, TB]), ALU.mult).then_inc(p_d, 1)
                        wait(dve, p_d, b + 1)
                        wait(dve, idxa_d, b + 1)
                    while "M" in do and heads[0] < heads[1]:
                        max_head()

            run(dve, step)

            steps = [0]

            def chained(ins, s=tab, n=steps):
                ins.then_inc(s, 1)
                n[0] += 1
                dve.wait_ge(s, n[0])

            chained(v.tensor_tensor(cnt[:], carry[:], region0[:], ALU.subtract))
            v.tensor_copy(tail[:], carry[:]).then_inc(table_d, 1)
            chained(v.tensor_tensor(gtn[:], cnt[:].unsqueeze(2).broadcast_to([P, E, TOK // P]),
                                    iota_n[:].unsqueeze(1).broadcast_to([P, E, TOK // P]), ALU.is_gt))
            chained(v.tensor_reduce(ntile[:], gtn[:], AX.X, ALU.add))
            chained(v.tensor_tensor_scan(tend[:], ones_f[:, 0:E], ntile[:], 0.0, ALU.mult, ALU.add))
            chained(v.tensor_tensor(tbeg[:], tend[:], ntile[:], ALU.subtract))
            chained(v.tensor_scalar(tb128[:], tbeg[:], float(P), None, ALU.mult))
            chained(v.tensor_tensor(delta[:], tb128[:], region0[:], ALU.subtract))
            chained(v.tensor_scalar(cmap[:], delta[:], -1.0, -float(DUMP), ALU.mult, ALU.add))
            wide = [P, 2, E]
            tile_no = iota_t[:].unsqueeze(2).broadcast_to(wide)
            chained(v.tensor_tensor(tge[:], tile_no, tbeg[:].unsqueeze(1).broadcast_to(wide), ALU.is_ge))
            chained(v.tensor_tensor(tlt[:], tile_no, tend[:].unsqueeze(1).broadcast_to(wide), ALU.is_lt))
            chained(v.tensor_tensor(tin[:], tge[:], tlt[:], ALU.mult))
            chained(v.tensor_scalar(tnum[:], iota_t[:], float(P), None, ALU.mult))
            chained(v.tensor_tensor(tsel[:], cmap[:].unsqueeze(1).broadcast_to(wide),
                                    tnum[:].unsqueeze(2).broadcast_to(wide), ALU.add))
            chained(v.tensor_tensor(tse[:], tsel[:], tin[:], ALU.mult))
            chained(v.tensor_reduce(tcol2[:], tse[:], AX.X, ALU.add))
            chained(v.tensor_scalar(tcol[:, 0:2], tcol2[:], float(DUMP), None, ALU.add))
            chained(v.tensor_tensor(tsel[:], iota_e[:].unsqueeze(1).broadcast_to(wide), tin[:], ALU.mult))
            chained(v.tensor_reduce(tcol2[:], tsel[:], AX.X, ALU.add))
            chained(v.tensor_scalar(tcol[:, 2:4], tcol2[:], float(P), None, ALU.mult))
            assert steps[0] == TABLE_STEPS
            dve.wait_ge(tab_ps, 1)
            v.tensor_copy(table[0:1, :], o_ps[0:1, :]).then_inc(table_d, 1)

            nlook = [0]

            def rows_out(g, i):
                wait(dve, xsT_ps, g + 1)
                wait(dve, ye_ps, g - 1)
                v.tensor_copy(xsT[i][:], st_ps[0][:, i].rearrange("p a b -> p (a b)")).then_inc(xsT_d, 1)

            rows_out(0, 0)
            rows_out(1, 1)
            dve.wait_ge(slota_d, NB)
            for c in range(NPAIR // CH):
                pairs = slice(c * CH, (c + 1) * CH)
                chained(v.tensor_tensor(ohd[:], iota_e[:].unsqueeze(1).broadcast_to([P, CH, E]),
                                        idx_all[:, pairs].unsqueeze(2).broadcast_to([P, CH, E]), ALU.is_equal), look, nlook)
                chained(v.tensor_tensor(ohd2[:], ohd[:], delta[:].unsqueeze(1).broadcast_to([P, CH, E]), ALU.mult), look, nlook)
                chained(v.tensor_reduce(dsl[:, pairs], ohd2[:], AX.X, ALU.add), look, nlook)
            chained(v.tensor_tensor(gidx_f[:], slot_all[:], dsl[:], ALU.add), look, nlook)
            with dve.Fori(1, GROUPS_E // 2) as n:
                for i in range(2):
                    rows_out(n * 2 + i, i)

            def gather_rows(b, par, first):
                if not first:
                    dve.wait_ge(yg_ld[par], 64 * (b // 2) if isinstance(b, int) else b)
                v.tensor_copy(gi[:, par], gidx_f[:, bass.ts(b, TOPK * TB)]).then_inc(gi_d, 1)

            def combine(b, nth, par):
                wait(dve, yg_ld[par], 64 * (nth + 1))
                wait(dve, f_ld[par], 32 * (nth + 1))
                for t in range(TB):
                    v.tensor_scalar(yw[:, t], yg[:, par, t], p_all[:, bass.ds(b * (TOPK * TB) + t, 1)], None,
                                    ALU.mult).then_inc(yw_d, 1)
                for t in range(TB):
                    wait(dve, yw_d, TB * b + t + 1)
                    v.scalar_tensor_tensor(yc[:, t], yg[:, par, TB + t], p_all[:, bass.ds(b * (TOPK * TB) + TB + t, 1)],
                                           yw[:, t], ALU.mult, ALU.add).then_inc(yc_d, 1)
                wait(dve, yc_d, TB * (b + 1))
                v.tensor_tensor(yb[:], yc[:], gb_f[:, par].unsqueeze(1).broadcast_to([P, TB, P]), ALU.mult).then_inc(yb_d, 1)
                wait(dve, yb_d, b + 1)
                wait(dve, out_st[par], 16 * nth)
                v.tensor_tensor(of[:, par], yb[:], x1_f[:, par], ALU.add).then_inc(of_d, 1)

            v.tensor_copy(gi[:, 0], gidx_f[:, 0:TOPK * TB]).then_inc(gi_d, 1)
            v.tensor_copy(gi[:, 1], gidx_f[:, TOPK * TB:2 * TOPK * TB]).then_inc(gi_d, 1)

            def combine_and_next(b, nth, par, more):
                combine(b, nth, par)
                if more:
                    v.tensor_copy(gi[:, par], gidx_f[:, bass.ts(b + 2, TOPK * TB)]).then_inc(gi_d, 1)

            for par in range(2):
                combine_and_next(par, 0, par, True)
            with dve.Fori(1, NB // 2 - 1) as n:
                for par in range(2):
                    combine_and_next(n * 2 + par, n, par, True)
            for par in range(2):
                combine_and_next(NB - 2 + par, NB // 2 - 1, par, False)

        @block.tensor
        def _(pe):
            t_ = nc.tensor
            pe.wait_ge(gp_const, 4)
            pe.wait_ge(s_sc, 1)
            t_.transpose(misc[:, 0:NB], sc[:], ident[0:NB, 0:NB]).then_inc(cT_ps, 1)
            pe.wait_ge(cT_done, 1)
            t_.matmul(o_ps[0:NB, :], cT[:], wm[:, 0:4 * P], start=True, stop=True)
            t_.matmul(misc[0:NB, 0:2 * P], cT[:], wm[:, 4 * P:6 * P], start=True, stop=True).then_inc(mod_ps, 1)
            pe.wait_ge(clamp, 3)
            pe.wait_ge(loads, LOADS)
            t_.transpose(misc[:, 0:E], rw[:], ident[0:E, 0:E]).then_inc(rwT_ps, 1)
            pe.wait_ge(perm, 4)
            pe.wait_ge(gp_const, 15)

            free = [(rwT_done, 1)]

            def misc_free(released_by):
                wait(pe, *free[0])
                free[0] = released_by

            def max_head(st, h):
                b, par, nth = st.at(1), st.par(1), st.nth(1)
                if h % (H // 2) == 0:
                    wait(pe, aug_ld[par][h // (H // 2)], 64 * (nth + 1))
                wait(pe, mx_d, H * b + h - 1)
                pe.nop(nofuse=True)
                for qc in range(TB):
                    last = t_.matmul(mx_ps[h % 2][:, qc], q_aug[par][0:ROWS, h, qc * P:(qc + 1) * P],
                                     k_aug[par][0:ROWS, h, :], start=True, stop=True)
                last.then_inc(mps_r, 1)

            def scores(st, u):
                b, par = st.at(0), st.par(0)
                if u == 0:
                    wait(pe, mrow_ld, 32 * (b + 1))
                wait(pe, exp_d, UNITS * b + u - 1)
                pe.nop(nofuse=True)
                for hh in range(2):
                    h = 2 * u + hh
                    for kc in range(TB):
                        last = t_.matmul(st_ps[u % 2][:, hh, kc], k_aug[par][0:ROWS + 2, h, kc * P:(kc + 1) * P],
                                         q_aug[par][0:ROWS + 2, h, :], start=True, stop=True)
                last.then_inc(st_r, 1)

            def probs_v(st, k, g):
                b, par = st.at(k), st.par(k)
                wait(pe, exp_d, UNITS * b + 2 * g + 2)
                wait(pe, oT_d, GROUPS * b + g)
                if g == 0:
                    wait(pe, v_d, b + 1)
                pe.nop(nofuse=True)
                for kc in range(TB):
                    for j in range(4):
                        h = 4 * g + j
                        last = t_.matmul(o_ps[32 * j:32 * j + VW, 0:NT], v_aug[par][:, kc, h, :],
                                         pr[(h // 2) % 4][:, h % 2, kc, :], start=(kc == 0), stop=(kc == TB - 1))
                last.then_inc(pv_d, 1)

            def step(st, do):
                h = 0
                for u in range(UNITS):
                    if u == 0 and "P" in do:
                        b = st.at(2)
                        wait(pe, h1_d, b + 1)
                        misc_free((hT_d, b + 1))
                        for t in range(TB):
                            last = t_.transpose(misc[:, t * P:(t + 1) * P], h1[:, t], ident[:])
                        last.then_inc(hT_ps, 1)
                    if "A" in do:
                        scores(st, u)
                    if u == 0 and "O" in do:
                        probs_v(st, -1, GROUPS - 1)
                    for _ in range(min(2, MAX_HEADS[u]) if "M" in do else 0):
                        max_head(st, h)
                        h += 1
                    if u == 1 and "O" in do:
                        b = st.at(-1)
                        wait(pe, oT_d, GROUPS * (b + 1))
                        for qc in range(TB):
                            misc_free((on_d, TB * b + qc + 1))
                            for g in range(GROUPS):
                                last = t_.transpose(misc[:, g * P:(g + 1) * P], oT[:, g, qc * P:(qc + 1) * P], ident[:])
                            last.then_inc(o2_ps, 1)
                    if u == 1 and "P" in do:
                        b = st.at(2)
                        for t in range(TB):
                            wait(pe, hT_d, b + 1)
                            misc_free((qkv_d, TB * b + t + 1))
                            t_.matmul(misc[:, 0:QKVG], hT[:, t * P:(t + 1) * P], wqkv[:], start=True, stop=True).then_inc(qkv_ps, 1)
                    if u in (2, 4, 6) and "A" in do:
                        probs_v(st, 0, u // 2 - 1)
                    if u == 2 and "O" in do:
                        b = st.at(-1)
                        misc_free((onT_d, b + 1))
                        for qc in range(TB):
                            last = t_.transpose(misc[:, qc * P:(qc + 1) * P], on[:, qc], ident[:])
                        last.then_inc(onT_ps, 1)
                    if u == 2 and "R" in do:
                        b = st.at(-2)
                        wait(pe, mask_d, b + 1)
                        misc_free((carry_d, b + 1))
                        m = [mask[:, t] for t in range(TB)]
                        t_.matmul(misc[:, 0:TB * E], tri[:], mask[:].rearrange("p t e -> p (t e)"), start=True, stop=False,
                                  skip_group_check=True)
                        t_.matmul(misc[:, E:2 * E], ones_b[:], m[0], start=False, stop=False, skip_group_check=True)
                        t_.matmul(misc[:, 2 * E:3 * E], ones_b[:], m[0], start=False, stop=False, skip_group_check=True)
                        t_.matmul(misc[:, 2 * E:3 * E], ones_b[:], m[1], start=False, stop=True,
                                  skip_group_check=True).then_inc(rank_ps, 1)
                    if u == 3 and "O" in do:
                        b = st.at(-1)
                        wait(pe, onT_d, b + 1)
                        misc_free((attg_d, b + 1))
                        for qc in range(TB):
                            last = t_.matmul(misc[:, qc * P:(qc + 1) * P], onT[:, qc * P:(qc + 1) * P], wo[:], start=True, stop=True)
                        last.then_inc(wo_ps, 1)
                    if u == 4 and "P" in do:
                        b = st.at(2)
                        wait(pe, qn_d, TB * (b + 1))
                        misc_free((rest_d, b + 1))
                        for k in range(2):
                            for t in range(TB):
                                last = t_.transpose(misc[:, (k * TB + t) * P:(k * TB + t + 1) * P],
                                                    qn[:, t, k * P:(k + 1) * P], ident[:])
                        last.then_inc(qkT_ps, 1)
                    if u == 6 and "M" in do:
                        b = st.at(1)
                        wait(pe, mx_d, H * (b + 1))
                        misc_free((mmid_d, b + 1))
                        for qc in range(TB):
                            last = t_.transpose(misc[0:H, qc * P:(qc + 1) * P], negmax[:, qc], ident[:])
                        last.then_inc(mT_ps, 1)
                    if u == 6 and "O" in do:
                        b, par = st.at(-1), st.par(-1)
                        wait(pe, h2_d, b + 1)
                        misc_free((h2T_d, b + 1))
                        for t in range(TB):
                            last = t_.transpose(misc[:, t * P:(t + 1) * P], h2[:, par, t], ident[:])
                        last.then_inc(h2T_ps, 1)
                    if u == 7 and "O" in do:
                        b = st.at(-1)
                        wait(pe, h2T_d, b + 1)
                        misc_free((lg_d, b + 1))
                        for t in range(TB):
                            last = t_.matmul(misc[:, t * E:(t + 1) * E], h2T[:, t * P:(t + 1) * P], rwT[:], start=True, stop=True)
                        last.then_inc(lg_ps, 1)
                    for _ in range(MAX_HEADS[u] - min(2, MAX_HEADS[u]) if "M" in do else 0):
                        max_head(st, h)
                        h += 1

            def run_pe():
                for s in range(-3, 2):
                    step(Step(s), stages(s))
                with pe.Fori(1, NB // 2 - 2) as pair:
                    free[0] = (lg_d, pair * 2 - 1)
                    for parity in range(2):
                        step(Step(pair * 2 + parity, parity, pair), {n for n, _ in STAGES})
                free[0] = (lg_d, NB - 5)
                for s in range(NB - 4, NB + 2):
                    step(Step(s), stages(s))

            run_pe()

            pe.wait_ge(tab, TABLE_STEPS)
            for k in range(4):
                last = t_.matmul(o_ps[0:1, k * P:(k + 1) * P], tcol[:, k:k + 1], ident[:], start=True, stop=True)
            last.then_inc(tab_ps, 1)
            pe.wait_ge(table_d, 2)

            pe.wait_ge(we_ld, 16)

            def expert_in(g, nth, i, first):
                pe.wait_ge(xs_ld[i], 16 * TG * (nth + 1) if isinstance(nth, int) else nth * (16 * TG) + 16 * TG)
                if not first:
                    pe.wait_ge(xsT_d, g - 1)
                pe.nop(nofuse=True)
                bank = st_ps[0][:, i].rearrange("p a b -> p (a b)")
                for k in range(TG):
                    last = t_.transpose(bank[:, k * P:(k + 1) * P], xs_sb[i][:, k, :], ident[:])
                last.then_inc(xsT_ps, 1)

            def expert_out(g, i, first):
                pe.wait_ge(xsT_d, g + 1)
                if not first:
                    pe.wait_ge(ye_d, g - 1)
                pe.nop(nofuse=True)
                bank = st_ps[1][:, i].rearrange("p a b -> p (a b)")
                for k in range(TG):
                    col = pe.value_load(table[0:1, bass.ds(g * TG + (2 * P + k), 1)], min_val=0, max_val=(E - 1) * P)
                    last = t_.matmul(bank[:, k * P:(k + 1) * P], xsT[i][:, k * P:(k + 1) * P], we[:, bass.ds(col, P)],
                                     start=True, stop=True)
                last.then_inc(ye_ps, 1)

            expert_in(0, 0, 0, True)
            expert_in(1, 0, 1, True)
            expert_out(0, 0, True)
            expert_out(1, 1, True)
            with pe.Fori(1, GROUPS_E // 2) as n:
                for i in range(2):
                    expert_in(n * 2 + i, n, i, False)
                for i in range(2):
                    expert_out(n * 2 + i, i, False)


_INS = ['L0_attn_x', 'L0_attn_Wq', 'L0_attn_bq', 'L0_attn_Wk', 'L0_attn_bk', 'L0_attn_Wv', 'L0_attn_bv', 'L0_attn_Wo',
        'L0_attn_bo', 'L0_attn_qn_w', 'L0_attn_kn_w', 'L0_ffn_router_w', 'L0_ffn_expert_weights', 'L0_c', 'L0_wmod']


def kernel(**inputs):
    import concourse.bacc as bacc
    from concourse.bass_utils import run_bass_kernel_spmd

    nc = bacc.Bacc("TRN2", target_bir_lowering=False, num_devices=1)
    arrays, args = {}, []
    for name in _INS:
        a = np.ascontiguousarray(inputs[name])
        arrays[f"in_{name}"] = a
        args.append(nc.dram_tensor(f"in_{name}", a.shape, mybir.dt.from_np(a.dtype), kind="ExternalInput").ap())
    args.append(nc.dram_tensor("out_x", (NB, NT, P), F32, kind="ExternalOutput").ap())
    build(nc, *args)
    r = run_bass_kernel_spmd(nc, [arrays], core_ids=[0])
    return r.results[0]["out_x"]
```

```python
import numpy as np

import concourse.bass as bass
import concourse.mybir as mybir

F32 = mybir.dt.float32
BF16 = mybir.dt.bfloat16
I32 = mybir.dt.int32
U32 = mybir.dt.uint32
ALU = mybir.AluOpType
ACT = mybir.ActivationFunctionType
AX = mybir.AxisListType

P = 128
NB, NT = 32, 256
TB = NT // P
H, HD = 16, 8
E, TOPK = 32, 2
TOK = NB * NT
QKVG = 3 * P + H
TERMS = (3, 2, 1)
ROWS = HD * sum(TERMS)
MROW = P - 2
GROUPS = H // 4
VW = 32
UR = 2 * P
ZR = 16
REGION = TOK + 2 * UR
DUMP = E * REGION
MAX_UNITS = (TOPK * TOK + E * (UR - 1)) // UR
UG = 2
XB = 4
GROUPS_E = -(-MAX_UNITS // (UG * XB)) * XB
UNITS = GROUPS_E * UG
TG = UG * UR // P
assert UNITS <= P and UR // ZR == ZR
LN_EPS, RMS_EPS = 1e-5, 1e-6
SCALE = float(HD) ** -0.5
TABLE_STEPS = 22
PR = 8
DEPTH = 6
LOOP_FROM = -(-(DEPTH + 1) // 2)
BANK = {"hT": 0, "qkv0": 0, "qkv1": 1, "qkT": 0, "mT": 1, "o20": 0, "o21": 1, "onT": 0, "wo": 0, "h2T": 0, "lg": 1, "rank": 1}
LAST_IN_BANK = (("h2T", 4), ("lg", 4))
SA, CA, GA, GABO, SB, CB, GB, MODS = range(8)


def build(nc, x, Wq, bq, Wk, bk, Wv, bv, Wo, bo, qn_w, kn_w, router_w, expert_w, c_in, wmod, out):
    from contextlib import ExitStack

    ctx = ExitStack()
    LOADS = 16 * (13 + 2 * HD)

    def sb(name, shape, dt=F32):
        return ctx.enter_context(nc.sbuf_tensor(name, shape, dt))

    def ps(name, shape, dt=F32):
        return ctx.enter_context(nc.psum_tensor(name, shape, dt))

    def sem(name):
        return ctx.enter_context(nc.semaphore(name))

    def dram(name, shape, dt=F32):
        return nc.dram_tensor(name, shape, dt, kind="Internal").ap()

    with ctx:
        mod_d = dram("mod_d", (NB, MODS * P))
        q_d = dram("q_d", (2, sum(TERMS), P, NT), BF16)
        k_d = dram("k_d", (2, 3, P, NT), BF16)
        x1_d = dram("x1_d", (NB, NT, P))
        xs_d = dram("xs_d", (DUMP + UR, P))
        ys_d = dram("ys_d", (UNITS * UR, P))

        ident = sb("ident", [P, P])
        ones_f = sb("ones_f", [P, P])
        tri = sb("tri", [P, P], BF16)
        ones_b = sb("ones_b", [P, P], BF16)
        iota_e = sb("iota_e", [P, E])
        iota_p = sb("iota_p", [P, 1])
        iota_n = sb("iota_n", [P, TOK // UR])
        iota_z = sb("iota_z", [P, P // ZR])
        region0 = sb("region0", [P, E])
        eps = sb("eps", [P, 2])
        zeros = sb("zeros", [P, ZR * P])
        zsel = sb("zsel", [P, P // ZR])
        zlt = sb("zlt", [P, P // ZR])
        zrow = sb("zrow", [P, 1])
        wqkv = sb("wqkv", [P, QKVG])
        bqkv = sb("bqkv", [P, QKVG])
        wo = sb("wo", [P, P])
        bo_b = sb("bo_b", [P, P])
        wraw = sb("wraw", [P, 2 * P])
        braw = sb("braw", [P, 2 * P])
        w_col = sb("w_col", [P, 2])
        rw = sb("rw", [E, P])
        rwT = sb("rwT", [P, E])
        we = sb("we", [P, E * P])
        c_sb = sb("c_sb", [NB, P])
        sc = sb("sc", [NB, P])
        cT = sb("cT", [P, NB])
        wm = sb("wm", [P, 6 * P])
        mod = sb("mod", [NB, MODS * P])
        sgn = sb("sgn", [NB, P])
        mag = sb("mag", [NB, P])

        x_p = sb("x_p", [P, 2, TB, P])
        mod_p = sb("mod_p", [P, 2, 2, P])
        st1 = sb("st1", [P, TB, 6])
        mv1 = sb("mv1", [P, TB, 2])
        lnv1 = sb("lnv1", [P, TB])
        y1 = sb("y1", [P, TB])
        n1 = sb("n1", [P, TB])
        n1b = sb("n1b", [P, TB])
        rstd1 = sb("rstd1", [P, TB])
        shift1 = sb("shift1", [P, TB])
        xh1 = sb("xh1", [P, TB, P])
        h1a = sb("h1a", [P, TB, P])
        h1 = sb("h1", [P, TB, P])
        hT = sb("hT", [P, NT])
        qkvg = sb("qkvg", [P, 2, TB, QKVG])
        sq = sb("sq", [P, TB, 2 * P])
        ss = sb("ss", [P, TB * 2 * H])
        lnm = sb("lnm", [P, TB * 2 * H])
        r0 = sb("r0", [P, TB * 2 * H])
        n2 = sb("n2", [P, TB * 2 * H])
        n2b = sb("n2b", [P, TB * 2 * H])
        rr = sb("rr", [P, TB * 2 * H])
        qn = sb("qn", [P, TB, 2 * P])
        parts = sb("parts", [P, 2, 3, NT], BF16)
        rest = sb("rest", [P, 2, NT])
        q_aug = [sb(f"q_aug{i}", [P, H, NT], BF16) for i in range(2)]
        k_aug = [sb(f"k_aug{i}", [P, H, NT], BF16) for i in range(2)]
        negmax = sb("negmax", [P, TB, H])
        mhi = sb("mhi", [H, NT], BF16)
        mmid = sb("mmid", [H, NT], BF16)
        v_aug = [sb(f"v_aug{i}", [P, TB, H, VW]) for i in range(2)]
        eg = sb("eg", [P, 2, TB, H])
        pr = sb("pr", [P, PR, TB, NT])
        oT = sb("oT", [P, GROUPS, NT])
        den = sb("den", [P, TB, H])
        fac = sb("fac", [P, TB, H])
        on = sb("on", [P, TB, P])
        onT = sb("onT", [P, NT])
        x_o = sb("x_o", [P, 2, TB, P])
        mod_o = sb("mod_o", [P, 2, 4, P])
        xga = sb("xga", [P, TB, P])
        attg = sb("attg", [P, TB, P])
        x1 = sb("x1", [P, 2, TB, P])
        st2 = sb("st2", [P, TB, 6])
        mv2 = sb("mv2", [P, TB, 2])
        lnv2 = sb("lnv2", [P, TB])
        y2 = sb("y2", [P, TB])
        n3 = sb("n3", [P, TB])
        n3b = sb("n3b", [P, TB])
        rstd2 = sb("rstd2", [P, TB])
        shift2 = sb("shift2", [P, TB])
        xh2 = sb("xh2", [P, TB, P])
        h2a = sb("h2a", [P, TB, P])
        h2 = sb("h2", [P, 2, TB, P])
        h2T = sb("h2T", [P, NT])
        lg = sb("lg", [P, TB, E])
        top = sb("top", [P, TB, 8])
        topi = sb("topi", [P, TB, 8], U32)
        dlg = sb("dlg", [P, TB, E + TOPK])
        elg = sb("elg", [P, TB, E + TOPK])
        esum = sb("esum", [P, TB])
        rsum = sb("rsum", [P, TB])
        idx = sb("idx", [P, TOPK, TB])
        oh = sb("oh", [P, TOPK, TB, E])
        mask = sb("mask", [P, TB, E], BF16)
        carry = sb("carry", [P, E])
        rk = sb("rk", [P, TB, E])
        ohr = sb("ohr", [P, TOPK, TB, E])
        slot_f = sb("slot_f", [P, TOPK * TB])
        slot = sb("slot", [P, 2, TOPK * TB], U32)
        slot_all = sb("slot_all", [P, NB * TOPK * TB])
        idx_all = sb("idx_all", [P, NB * TOPK * TB])
        p_all = sb("p_all", [P, NB * TOPK * TB])
        gtn = sb("gtn", [P, E, TOK // UR])
        cnt = sb("cnt", [P, E])
        nunit = sb("nunit", [P, E])
        uend = sb("uend", [P, E])
        ubeg = sb("ubeg", [P, E])
        ubrow = sb("ubrow", [P, E])
        cmap = sb("cmap", [P, E])
        delta = sb("delta", [P, E])
        uge = sb("uge", [P, E])
        ult = sb("ult", [P, E])
        uin = sb("uin", [P, E])
        usel = sb("usel", [P, E])
        ucol = sb("ucol", [P, 2])
        ucol2 = sb("ucol2", [P, 1])
        unum = sb("unum", [P, 1])
        table = sb("table", [P, 2 * P], I32)
        ZG = E * ZR // P
        zend = sb("zend", [P, ZG, P // ZR])
        zfirst = sb("zfirst", [P, ZG])
        zblock = sb("zblock", [P, ZG], I32)
        zidx = sb("zidx", [P, 2, ZG], U32)
        xs_sb = [sb(f"xs{i}", [P, TG, P]) for i in range(XB)]
        xsT = [sb(f"xsT{i}", [P, TG * P]) for i in range(2)]
        ys_sb = [sb(f"ys{i}", [P, TG, P]) for i in range(2)]
        NPAIR = NB * TOPK * TB
        CH = 32
        ohd = sb("ohd", [P, CH, E])
        ohd2 = sb("ohd2", [P, CH, E])
        dsl = sb("dsl", [P, NPAIR])
        gidx_f = sb("gidx_f", [P, NPAIR])
        gidx = sb("gidx", [P, NPAIR], I32)
        gi = sb("gi", [P, 2, TOPK * TB], U32)
        yg = sb("yg", [P, 2, TOPK * TB, P])
        x1_f = sb("x1_f", [P, 2, TB, P])
        gb_f = sb("gb_f", [P, 2, P])
        yw = sb("yw", [P, TB, P])
        yc = sb("yc", [P, TB, P])
        yb = sb("yb", [P, TB, P])
        of = sb("of", [P, 2, TB, P])

        st_ps = [ps(f"st_ps{i}", [P, TB, NT]) for i in range(3)]
        mx_ps = [ps(f"mx_ps{i}", [P, TB, NT]) for i in range(2)]
        o_ps = ps("o_ps", [P, 512])
        misc = [ps(f"misc{i}", [P, 512]) for i in range(2)]

        loads = sem("loads")
        we_ld = sem("we_ld")
        perm = sem("perm")
        gp_const = sem("gp_const")
        dve_const = sem("dve_const")
        s_exp = sem("s_exp")
        s_e1 = sem("s_e1")
        s_sc = sem("s_sc")
        cT_ps, cT_done, mod_ps, mod_sb, rwT_ps, rwT_done = (
            sem(n) for n in ("cT_ps", "cT_done", "mod_ps", "mod_sb", "rwT_ps", "rwT_done"))
        clamp = sem("clamp")
        mod_st = sem("mod_st")
        xp_ld = [sem(f"xp_ld{i}") for i in range(2)]
        xo_ld = [sem(f"xo_ld{i}") for i in range(2)]
        st1_d, mv1_d, lnv1_d, y1_d, n1_d, n1b_d, rstd1_d, shift1_d, xh1_d, h1a_d, h1_d = (
            sem(n) for n in ("st1_d", "mv1_d", "lnv1_d", "y1_d", "n1_d", "n1b_d", "rstd1_d", "shift1_d", "xh1_d", "h1a_d", "h1_d"))
        hT_ps, hT_d, qkv_ps, qkv_d = (sem(n) for n in ("hT_ps", "hT_d", "qkv_ps", "qkv_d"))
        sq_d, ss_d, lnm_d, r0_d, n2_d, n2b_d, rr_d, qn_d = (
            sem(n) for n in ("sq_d", "ss_d", "lnm_d", "r0_d", "n2_d", "n2b_d", "rr_d", "qn_d"))
        qkT_ps, hi_d, rest_d, mid_d, lo_d = (sem(n) for n in ("qkT_ps", "hi_d", "rest_d", "mid_d", "lo_d"))
        parts_st = sem("parts_st")
        aug_ld = [[sem(f"aug_ld{i}{j}") for j in range(2)] for i in range(2)]
        mps_r, mx_d = sem("mps_r"), sem("mx_d")
        mT_ps, mhi_d, mmid_d = sem("mT_ps"), sem("mhi_d"), sem("mmid_d")
        mrow_ld = sem("mrow_ld")
        v_d, eg_d = sem("v_d"), sem("eg_d")
        st_r, exp_d = sem("st_r"), sem("exp_d")
        pv_d, oT_d = sem("pv_d"), sem("oT_d")
        o2_ps, den_d, fac_d, on_d = sem("o2_ps"), sem("den_d"), sem("fac_d"), sem("on_d")
        onT_ps, onT_d, wo_ps, xga_d, attg_d, x1_done = (
            sem(n) for n in ("onT_ps", "onT_d", "wo_ps", "xga_d", "attg_d", "x1_done"))
        x1_st = [sem(f"x1_st{i}") for i in range(2)]
        st2_d, mv2_d, lnv2_d, y2_d, n3_d, n3b_d, rstd2_d, shift2_d, xh2_d, h2a_d, h2_d = (
            sem(n) for n in ("st2_d", "mv2_d", "lnv2_d", "y2_d", "n3_d", "n3b_d", "rstd2_d", "shift2_d", "xh2_d", "h2a_d", "h2_d"))
        h2T_ps, h2T_d, lg_ps, lg_d, top_d, topi_d, dlg_d, elg_d, esum_d, rsum_d, p_d, idx_d, idxa_d, oh_d, mask_d = (
            sem(n) for n in ("h2T_ps", "h2T_d", "lg_ps", "lg_d", "top_d", "topi_d", "dlg_d", "elg_d", "esum_d",
                             "rsum_d", "p_d", "idx_d", "idxa_d", "oh_d", "mask_d"))
        rank_ps, rk_d, carry_d, ohr_d, slotf_d, slot_d, slota_d = (
            sem(n) for n in ("rank_ps", "rk_d", "carry_d", "ohr_d", "slotf_d", "slot_d", "slota_d"))
        scat = [sem(f"scat{i}") for i in range(2)]
        tab = sem("tab")
        zc = sem("zc")
        zidx_d, tab_ps, table_d, tail_st, dump_st = (
            sem(n) for n in ("zidx_d", "tab_ps", "table_d", "tail_st", "dump_st"))
        xs_ld = [sem(f"xs_ld{i}") for i in range(XB)]
        xsT_ps, xsT_d, ye_ps, ye_d = sem("xsT_ps"), sem("xsT_d"), sem("ye_ps"), sem("ye_d")
        ys_st = [sem(f"ys_st{i}") for i in range(2)]
        look = sem("look")
        gidx_d, gi_d = sem("gidx_d"), sem("gi_d")
        yg_ld = [sem(f"yg_ld{i}") for i in range(2)]
        f_ld = [sem(f"f_ld{i}") for i in range(2)]
        yw_d, yc_d, yb_d, of_d = sem("yw_d"), sem("yc_d"), sem("yb_d"), sem("of_d")
        out_st = [sem(f"out_st{i}") for i in range(2)]

        def score_bank(b, h):
            return (h + b.par) % 3

        def score_bank_read(b, h):
            return -2 if b.par or h > 1 else -1

        def wait(eng, s, n):
            if isinstance(n, int) and n <= 0:
                return
            eng.wait_ge(s, n)

        class Batch:

            def __init__(self, n, par, nth):
                self.n, self.par, self.nth = n, par, nth

        class Step:

            def __init__(self, s, pair=None):
                self.s, self.pair = s, pair

            def batches(self):
                out = []
                for k in range(DEPTH):
                    if self.pair is None:
                        n = self.s - k
                        out.append(Batch(n, n % 2, n // 2) if 0 <= n < NB else None)
                    else:
                        par = (self.s - k) % 2
                        out.append(Batch(self.pair * 2 + (self.s - k), par, self.pair + (self.s - k - par) // 2))
                return out

        def of_batch(task):
            def call(b, *which):
                if b is not None:
                    task(b, *which)
            return call

        def run(eng, step, seed=lambda last: None):
            for s in range(2 * LOOP_FROM):
                step(*Step(s).batches())
            with eng.Fori(LOOP_FROM, NB // 2) as pair:
                seed(Step(-1, pair).batches())
                for parity in range(2):
                    step(*Step(parity, pair).batches())
            seed(Step(NB - 1).batches())
            for s in range(NB, NB + DEPTH - 1):
                step(*Step(s).batches())

        block = ctx.enter_context(nc.Block())

        @block.sync
        def _(sp):
            for dst, src in (
                (c_sb[:], c_in), (wm[:], wmod), (rw[:], router_w), (wraw[:, 0:P], Wq[:, 0:P]), (wraw[:, P:2 * P], Wk),
                (wqkv[:, 2 * P:3 * P], Wv), (wqkv[:, 3 * P:QKVG], Wq[:, P:P + H]),
                (braw[:, 0:P], bq[0:P].partition_broadcast(P)), (braw[:, P:2 * P], bk.partition_broadcast(P)),
                (bqkv[:, 2 * P:3 * P], bv.partition_broadcast(P)), (bqkv[:, 3 * P:QKVG], bq[P:P + H].partition_broadcast(P)),
                (wo[:], Wo), (bo_b[:], bo.partition_broadcast(P)),
            ):
                sp.dma_start(dst, src).then_inc(loads, 16)
            for d in range(HD):
                for k, w in enumerate((qn_w, kn_w)):
                    sp.dma_start(w_col[d * H:(d + 1) * H, k:k + 1], w[d:d + 1].partition_broadcast(H)).then_inc(loads, 16)
            sp.dma_start(we[:].rearrange("k (e n) -> k e n", e=E), expert_w.rearrange("e k n -> k e n")).then_inc(we_ld, 16)
            sp.wait_ge(mod_sb, 3)
            sp.dma_start(mod_d, mod[:]).then_inc(mod_st, 16)
            sp.wait_ge(dve_const, 1)
            sp.dma_start(xs_d[DUMP:DUMP + UR, :].rearrange("(p k) f -> p (k f)", p=P), zeros[:, 0:TB * P]).then_inc(dump_st, 16)
            sp.wait_ge(mod_st, 16)

            def load_x(dst, s, b):
                sp.dma_start(dst, x[b].rearrange("(p t) f -> p t f", t=TB) if isinstance(b, int)
                             else x[bass.ds(b, 1)].rearrange("o (p t) f -> (o p) t f", t=TB)).then_inc(s, 16)

            def mod_rows(dst, s, b, lo, n):
                row = mod_d[b, lo * P:(lo + n) * P] if isinstance(b, int) else \
                    mod_d[bass.ds(b, 1), lo * P:(lo + n) * P].rearrange("o f -> (o f)")
                sp.dma_start(dst, row.partition_broadcast(P)).then_inc(s, 16)

            @of_batch
            def load_x_norm(b):
                wait(sp, h1_d, b.n - 1)
                load_x(x_p[:, b.par], xp_ld[b.par], b.n)
                mod_rows(mod_p[:, b.par].rearrange("p a f -> p (a f)"), xp_ld[b.par], b.n, SA, 2)

            @of_batch
            def load_x_out(b):
                wait(sp, h2_d, b.n - 1)
                load_x(x_o[:, b.par], xo_ld[b.par], b.n)
                mod_rows(mod_o[:, b.par].rearrange("p a f -> p (a f)"), xo_ld[b.par], b.n, GA, 4)

            @of_batch
            def store_x1(b):
                wait(sp, x1_done, b.n + 1)
                dst = x1_d[b.n] if isinstance(b.n, int) else x1_d[bass.ds(b.n, 1)].rearrange("o t f -> (o t) f")
                sp.dma_start(dst.rearrange("(p t) f -> p t f", t=TB), x1[:, b.par]).then_inc(x1_st[b.par], 16)

            @of_batch
            def store_parts(b):
                wait(sp, lo_d, b.n + 1)
                sp.nop(nofuse=True)
                for half in range(2):
                    wait(sp, aug_ld[b.par][half], 64 * b.nth)
                sp.nop(nofuse=True)
                row = 0
                for a, n in enumerate(TERMS):
                    sp.dma_start(q_d[b.par, row:row + n].rearrange("a p t -> p a t"),
                                 parts[:, 0, a:a + 1, :].broadcast_to([P, n, NT])).then_inc(parts_st, 16)
                    row += n
                sp.dma_start(k_d[b.par].rearrange("a p t -> p a t"), parts[:, 1]).then_inc(parts_st, 16)

            @of_batch
            def load_heads(b, j):
                if isinstance(b.n, int) and b.n == 0:
                    sp.wait_ge(gp_const, 22)
                wait(sp, parts_st, 64 * (b.n + 1))
                sp.nop(nofuse=True)
                wait(sp, st_r, H * (b.n - 2) + (j + 1) * H // 2)
                hs = slice(j * H // 2, (j + 1) * H // 2)
                loaded = aug_ld[b.par][j]
                sp.dma_start(q_aug[b.par][0:ROWS, hs, :],
                             q_d[b.par].rearrange("a (d h) t -> (a d) h t", h=H)[:, hs]).then_inc(loaded, 16)
                row = 0
                for n in TERMS:
                    sp.dma_start(k_aug[b.par][row:row + n * HD, hs, :],
                                 k_d[b.par, 0:n].rearrange("a (d h) t -> (a d) h t", h=H)[:, hs]).then_inc(loaded, 16)
                    row += n * HD

            @of_batch
            def load_max_rows(b):
                wait(sp, mhi_d, b.n + 1)
                wait(sp, mmid_d, b.n + 1)
                sp.dma_start(q_aug[b.par][MROW:MROW + 1], mhi[:]).then_inc(mrow_ld, 16)
                sp.dma_start(q_aug[b.par][MROW + 1:MROW + 2], mmid[:]).then_inc(mrow_ld, 16)

            def step(b0, b1, b2, b3, b4, b5):
                load_max_rows(b4)
                load_heads(b3, 1)
                load_x_out(b4)
                load_x_norm(b0)
                store_parts(b2)
                store_x1(b5)
                load_heads(b2, 0)

            run(sp, step)

            for i in range(2):
                sp.wait_ge(scat[i], 16 * TOPK * TB * NB // 2)
            sp.wait_ge(dump_st, 16)
            sp.wait_ge(tail_st, 16 * 2 * ZG)
            sp.wait_ge(table_d, 1)

            def rows_in(g, i, first):
                if not first:
                    sp.wait_ge(xsT_ps, g - (XB - 1))
                for k in range(UG):
                    row = sp.value_load(table[0:1, bass.ds(g * UG + k, 1)], min_val=0, max_val=DUMP)
                    sp.dma_start(xs_sb[i][:, k * TB:(k + 1) * TB, :],
                                 xs_d[bass.ds(row, UR), :].rearrange("(p k) f -> p k f", k=TB)).then_inc(xs_ld[i], 16)

            for i in range(XB):
                rows_in(i, i, True)
            with sp.Fori(1, GROUPS_E // XB) as n:
                for i in range(XB):
                    rows_in(n * XB + i, i, False)

            for i in range(2):
                sp.wait_ge(x1_st[i], 16 * NB // 2)

            def final_loads(b, nth, par):
                wait(sp, of_d, b - 1)
                src = x1_d[b] if isinstance(b, int) else x1_d[bass.ds(b, 1)].rearrange("o t f -> (o t) f")
                sp.dma_start(x1_f[:, par], src.rearrange("(p t) f -> p t f", t=TB)).then_inc(f_ld[par], 16)
                mod_rows(gb_f[:, par], f_ld[par], b, GB, 1)

            def final_store(b, par):
                wait(sp, of_d, b + 1)
                dst = out[b] if isinstance(b, int) else out[bass.ds(b, 1)].rearrange("o t f -> (o t) f")
                sp.dma_start(dst.rearrange("(p t) f -> p t f", t=TB), of[:, par]).then_inc(out_st[par], 16)

            final_loads(0, 0, 0)
            final_loads(1, 0, 1)
            with sp.Fori(1, NB // 2) as n:
                for par in range(2):
                    final_store(n * 2 + (par - 2), par)
                    final_loads(n * 2 + par, n, par)
            final_store(NB - 2, 0)
            final_store(NB - 1, 1)
            for i in range(2):
                sp.wait_ge(out_st[i], 16 * NB // 2)

        @block.gpsimd
        def _(gp):
            nc.gpsimd.memset(ones_f[:], 1.0).then_inc(gp_const, 1)
            nc.gpsimd.memset(ones_b[:], 1.0).then_inc(gp_const, 1)
            gp.wait_ge(gp_const, 2)
            nc.gpsimd.affine_select(out=ident[:], in_=ones_f[:], pattern=[[1, P]], compare_op=ALU.is_equal,
                                    fill=0.0, base=0, channel_multiplier=-1).then_inc(gp_const, 1)
            nc.gpsimd.affine_select(out=tri[:], in_=ones_b[:], pattern=[[1, P]], compare_op=ALU.is_gt,
                                    fill=0.0, base=0, channel_multiplier=-1).then_inc(gp_const, 1)
            for dst, pattern, mult in (
                (iota_e, [[1, E]], 0), (iota_p, [[1, 1]], 1), (iota_n, [[UR, TOK // UR]], 0), (region0, [[REGION, E]], 0),
                (iota_z, [[-ZR, P // ZR]], 1),
                (carry, [[REGION, E]], 0),
            ):
                nc.gpsimd.iota(dst[:], pattern=pattern, base=0, channel_multiplier=mult,
                               allow_small_or_imprecise_dtypes=True).then_inc(gp_const, 1)
            for i in range(2):
                nc.gpsimd.memset(v_aug[i][:], 0.0).then_inc(gp_const, 1)
                nc.gpsimd.memset(q_aug[i][:], 0.0).then_inc(gp_const, 1)
                nc.gpsimd.memset(k_aug[i][:], 1.0).then_inc(gp_const, 1)
            gp.wait_ge(gp_const, 16)
            for i in range(2):
                nc.gpsimd.memset(v_aug[i][:, :, :, HD:HD + 1], 1.0).then_inc(gp_const, 1)
            gp.wait_ge(gp_const, 18)
            for i in range(2):
                nc.gpsimd.memset(k_aug[i][0:96], 0.0).then_inc(gp_const, 1)
                nc.gpsimd.memset(k_aug[i][96:MROW], 0.0).then_inc(gp_const, 1)
            gp.wait_ge(gp_const, 22)

            @of_batch
            def copy_v(b):
                wait(gp, qkv_d, TB * (b.n + 1))
                wait(gp, pv_d, GROUPS * (b.n - 1))
                gp.nop(nofuse=True)
                nc.gpsimd.tensor_copy(v_aug[b.par][:, :, :, 0:HD],
                                      qkvg[:, b.par, :, 2 * P:3 * P].rearrange("p t (h d) -> p t h d", d=HD)).then_inc(v_d, 1)

            @of_batch
            def scale_ln1(b):
                wait(gp, xp_ld[b.par], 32 * (b.nth + 1))
                wait(gp, xh1_d, b.n + 1)
                wait(gp, h1_d, b.n)
                gp.nop(nofuse=True)
                nc.gpsimd.tensor_tensor(h1a[:], xh1[:], mod_p[:, b.par, 1:2, :].broadcast_to([P, TB, P]),
                                        ALU.mult).then_inc(h1a_d, 1)

            @of_batch
            def shift_ln1(b):
                wait(gp, h1a_d, b.n + 1)
                wait(gp, hT_ps, b.n)
                nc.gpsimd.tensor_tensor(h1[:], h1a[:], mod_p[:, b.par, 0:1, :].broadcast_to([P, TB, P]),
                                        ALU.add).then_inc(h1_d, 1)

            @of_batch
            def norm_qk(b, t):
                wait(gp, rr_d, b.n + 1)
                wait(gp, qkT_ps, b.n)
                gp.nop(nofuse=True)
                nc.gpsimd.tensor_tensor(
                    qn[:, t].rearrange("p (k d h) -> p k d h", k=2, h=H),
                    qkvg[:, b.par, t, 0:2 * P].rearrange("p (k d h) -> p k d h", k=2, h=H),
                    rr[:, t * 2 * H:(t + 1) * 2 * H].rearrange("p (k h) -> p k h", h=H).unsqueeze(2).broadcast_to(
                        [P, 2, HD, H]), ALU.mult).then_inc(qn_d, 1)

            @of_batch
            def low_part(b):
                wait(gp, mid_d, b.n + 1)
                wait(gp, parts_st, 64 * b.n)
                gp.nop(nofuse=True)
                nc.gpsimd.tensor_tensor(parts[:, :, 2], rest[:], parts[:, :, 1], ALU.subtract).then_inc(lo_d, 1)

            @of_batch
            def x_plus_bias(b):
                wait(gp, xo_ld[b.par], 32 * (b.nth + 1))
                wait(gp, x1_done, b.n)
                gp.nop(nofuse=True)
                nc.gpsimd.tensor_tensor(xga[:], x_o[:, b.par], mod_o[:, b.par, 1:2, :].broadcast_to([P, TB, P]),
                                        ALU.add).then_inc(xga_d, 1)

            @of_batch
            def residual(b):
                wait(gp, attg_d, b.n + 1)
                wait(gp, xga_d, b.n + 1)
                wait(gp, xh2_d, b.n - 1)
                wait(gp, x1_st[b.par], 16 * b.nth)
                gp.nop(nofuse=True)
                nc.gpsimd.tensor_tensor(x1[:, b.par], attg[:], xga[:], ALU.add).then_inc(x1_done, 1)

            @of_batch
            def scale_ln2(b):
                wait(gp, xh2_d, b.n + 1)
                wait(gp, h2_d, b.n)
                gp.nop(nofuse=True)
                nc.gpsimd.tensor_tensor(h2a[:], xh2[:], mod_o[:, b.par, 3:4, :].broadcast_to([P, TB, P]),
                                        ALU.mult).then_inc(h2a_d, 1)

            @of_batch
            def shift_ln2(b):
                wait(gp, h2a_d, b.n + 1)
                wait(gp, scat[b.par], 64 * b.nth)
                gp.nop(nofuse=True)
                nc.gpsimd.tensor_tensor(h2[:, b.par], h2a[:], mod_o[:, b.par, 2:3, :].broadcast_to([P, TB, P]),
                                        ALU.add).then_inc(h2_d, 1)

            @of_batch
            def keep_index(b):
                wait(gp, idx_d, b.n + 1)
                gp.nop(nofuse=True)
                nc.gpsimd.tensor_copy(idx_all[:, bass.ts(b.n, TOPK * TB)], idx[:].rearrange("p j t -> p (j t)")).then_inc(idxa_d, 1)

            @of_batch
            def keep_weights(b):
                wait(gp, rsum_d, b.n + 1)
                gp.nop(nofuse=True)
                nc.gpsimd.tensor_tensor(p_all[:, bass.ts(b.n, TOPK * TB)].rearrange("p (j t) -> p j t", t=TB),
                                        elg[:, :, E:E + TOPK].rearrange("p t j -> p j t"),
                                        rsum[:].unsqueeze(1).broadcast_to([P, TOPK, TB]), ALU.mult).then_inc(p_d, 1)

            @of_batch
            def keep_slot(b):
                wait(gp, slotf_d, b.n + 1)
                gp.nop(nofuse=True)
                nc.gpsimd.tensor_copy(slot_all[:, bass.ts(b.n, TOPK * TB)], slot_f[:]).then_inc(slota_d, 1)

            @of_batch
            def scatter(b, k):
                wait(gp, slot_d, b.n + 1)
                gp.nop(nofuse=True)
                nc.gpsimd.indirect_dma_start(xs_d, bass.IndirectOffsetOnAxis(ap=slot[:, b.par, k:k + 1], axis=0),
                                             h2[:, b.par, k % TB, :], None).then_inc(scat[b.par], 16)

            def step(b0, b1, b2, b3, b4, b5):
                low_part(b1)
                shift_ln2(b4)
                scale_ln1(b0)
                keep_slot(b5)
                keep_weights(b5)
                scatter(b5, 0)
                shift_ln1(b0)
                scatter(b5, 1)
                scatter(b5, 2)
                x_plus_bias(b3)
                scatter(b5, 3)
                residual(b3)
                copy_v(b1)
                norm_qk(b0, 0)
                norm_qk(b0, 1)
                keep_index(b4)
                scale_ln2(b3)

            run(gp, step)

            for i in range(2):
                gp.wait_ge(scat[i], 16 * TOPK * TB * NB // 2)
            gp.wait_ge(zidx_d, 2)
            gp.nop(nofuse=True)
            for g in range(ZG):
                nc.gpsimd.indirect_dma_start(xs_d, bass.IndirectOffsetOnAxis(ap=zidx[:, 0, g:g + 1], axis=0),
                                             zeros[:, 0:P], None).then_inc(tail_st, 16)
            gp.wait_ge(tail_st, 16 * ZG)
            gp.nop(nofuse=True)
            for g in range(ZG):
                nc.gpsimd.indirect_dma_start(xs_d.rearrange("(b r) f -> b (r f)", r=ZR),
                                             bass.IndirectOffsetOnAxis(ap=zidx[:, 1, g:g + 1], axis=0),
                                             zeros[:], None).then_inc(tail_st, 16)

            for i in range(2):
                gp.wait_ge(ys_st[i], 16 * GROUPS_E // 2)

            def gathers(b, par):
                wait(gp, gi_d, b + 1)
                wait(gp, yc_d, TB * (b - 1))
                gp.nop(nofuse=True)
                for k in range(TOPK * TB):
                    nc.gpsimd.indirect_dma_start(
                        yg[:, par, k, :], None, ys_d,
                        bass.IndirectOffsetOnAxis(ap=gi[:, par, k:k + 1], axis=0)).then_inc(yg_ld[par], 16)

            gathers(0, 0)
            gathers(1, 1)
            with gp.Fori(1, NB // 2) as n:
                for par in range(2):
                    gathers(n * 2 + par, par)

        @block.scalar
        def _(act):
            act.preload_act_table_set("natural_log_exp_and_others")
            act.wait_ge(loads, LOADS)
            nc.scalar.activation(sc[:], c_sb[:], ACT.Exp, scale=-1.0).then_inc(s_exp, 1)
            act.wait_ge(cT_ps, 1)
            nc.scalar.activation(cT[:], misc[0][:, 0:NB], ACT.Copy).then_inc(cT_done, 1)
            act.wait_ge(rwT_ps, 1)
            nc.scalar.activation(rwT[:], misc[0][:, 0:E], ACT.Copy).then_inc(rwT_done, 1)
            act.wait_ge(dve_const, 3)

            def log_var(n, src, scale, eps_col, ready, tmp, tmp_d):
                wait(act, ready, n + 1)
                nc.scalar.activation(tmp, src, ACT.Ln, bias=eps[:, eps_col:eps_col + 1], scale=scale).then_inc(tmp_d, 1)

            def rsqrt_seed(n, tmp, tmp_d, dst, dst_d):
                wait(act, tmp_d, n + 1)
                nc.scalar.activation(dst, tmp, ACT.Exp, scale=-0.5).then_inc(dst_d, 1)

            def normalise(src, rstd, shift, dst, dst_d):
                for t in range(TB):
                    ins = nc.scalar.activation(dst[:, t], src[:, t], ACT.Identity, scale=rstd[:, t:t + 1], bias=shift[:, t:t + 1])
                ins.then_inc(dst_d, 1)

            @of_batch
            def ln1_log(b):
                log_var(b.n, mv1[:, :, 1], 1.0, 0, mv1_d, lnv1[:], lnv1_d)

            @of_batch
            def ln1_seed(b):
                rsqrt_seed(b.n, lnv1[:], lnv1_d, y1[:], y1_d)

            @of_batch
            def ln1_normalise(b):
                wait(act, shift1_d, b.n + 1)
                wait(act, h1a_d, b.n)
                normalise(x_p[:, b.par], rstd1, shift1, xh1, xh1_d)

            @of_batch
            def h1_transposed(b):
                wait(act, hT_ps, b.n + 1)
                wait(act, qkv_ps, TB * b.n)
                nc.scalar.activation(hT[:], misc[BANK["hT"]][:, 0:NT], ACT.Copy).then_inc(hT_d, 1)

            @of_batch
            def squares(b):
                wait(act, qkv_d, TB * (b.n + 1))
                wait(act, ss_d, b.n)
                nc.scalar.activation(sq[:], qkvg[:, b.par, :, 0:2 * P], ACT.Square).then_inc(sq_d, 1)

            @of_batch
            def rms_log(b):
                log_var(b.n, ss[:], 1.0 / HD, 1, ss_d, lnm[:], lnm_d)

            @of_batch
            def rms_seed(b):
                wait(act, rr_d, b.n)
                rsqrt_seed(b.n, lnm[:], lnm_d, r0[:], r0_d)

            @of_batch
            def gate_exp(b):
                wait(act, qkv_d, TB * (b.n + 1))
                wait(act, den_d, TB * (b.n - 1))
                nc.scalar.activation(eg[:, b.par], qkvg[:, b.par, :, 3 * P:QKVG], ACT.Exp, scale=-1.0).then_inc(eg_d, 1)

            @of_batch
            def high_part(b):
                wait(act, qkT_ps, b.n + 1)
                wait(act, parts_st, 64 * b.n)
                for k in range(2):
                    nc.scalar.activation(parts[:, k, 0], misc[BANK["qkT"]][:, k * NT:(k + 1) * NT], ACT.Copy,
                                         scale=w_col[:, k:k + 1]).then_inc(hi_d, 1)

            @of_batch
            def middle_part(b):
                wait(act, rest_d, b.n + 1)
                wait(act, parts_st, 64 * b.n)
                nc.scalar.activation(parts[:, :, 1], rest[:], ACT.Copy).then_inc(mid_d, 1)

            @of_batch
            def max_high(b):
                wait(act, mT_ps, b.n + 1)
                wait(act, mrow_ld, 32 * b.n)
                nc.scalar.activation(mhi[:], misc[BANK["mT"]][0:H, 0:NT], ACT.Copy).then_inc(mhi_d, 1)

            @of_batch
            def exp_head(b, h):
                wait(act, st_r, H * b.n + h + 1)
                wait(act, pv_d, GROUPS * b.n + h // 4 - 1)
                nc.scalar.activation(pr[:, h % PR], st_ps[score_bank(b, h)][:], ACT.Exp, scale=SCALE).then_inc(exp_d, 1)

            @of_batch
            def out_transposed(b, g):
                wait(act, pv_d, GROUPS * b.n + g + 1)
                wait(act, o2_ps, TB * b.n)
                nc.scalar.activation(oT[:, g, :], o_ps[:, 0:NT], ACT.Copy).then_inc(oT_d, 1)

            @of_batch
            def on_transposed(b):
                wait(act, onT_ps, b.n + 1)
                wait(act, wo_ps, b.n)
                nc.scalar.activation(onT[:], misc[BANK["onT"]][:, 0:NT], ACT.Copy).then_inc(onT_d, 1)

            @of_batch
            def ln2_log(b):
                log_var(b.n, mv2[:, :, 1], 1.0, 0, mv2_d, lnv2[:], lnv2_d)

            @of_batch
            def ln2_seed(b):
                rsqrt_seed(b.n, lnv2[:], lnv2_d, y2[:], y2_d)

            @of_batch
            def ln2_normalise(b):
                wait(act, shift2_d, b.n + 1)
                wait(act, h2a_d, b.n)
                normalise(x1[:, b.par], rstd2, shift2, xh2, xh2_d)

            @of_batch
            def h2_transposed(b):
                wait(act, h2T_ps, b.n + 1)
                wait(act, lg_ps, b.n)
                nc.scalar.activation(h2T[:], misc[BANK["h2T"]][:, 0:NT], ACT.Copy).then_inc(h2T_d, 1)

            @of_batch
            def router_exp(b):
                wait(act, dlg_d, 2 * (b.n + 1))
                wait(act, esum_d, b.n)
                wait(act, p_d, b.n)
                nc.scalar.activation(elg[:], dlg[:], ACT.Exp).then_inc(elg_d, 1)

            def step(b0, b1, b2, b3, b4, b5):
                out_transposed(b4, 1)
                exp_head(b4, 13)
                exp_head(b4, 14)
                h2_transposed(b5)
                exp_head(b4, 15)
                out_transposed(b4, 2)
                out_transposed(b4, 3)
                h1_transposed(b1)
                max_high(b3)
                gate_exp(b2)
                on_transposed(b4)
                ln1_log(b0)
                squares(b1)
                exp_head(b3, 0)
                exp_head(b3, 1)
                rms_log(b1)
                exp_head(b3, 2)
                rms_seed(b1)
                exp_head(b3, 3)
                exp_head(b3, 4)
                router_exp(b5)
                exp_head(b3, 5)
                ln1_seed(b0)
                ln2_log(b4)
                exp_head(b3, 6)
                ln2_seed(b4)
                out_transposed(b3, 0)
                exp_head(b3, 7)
                exp_head(b3, 8)
                high_part(b1)
                exp_head(b3, 9)
                ln2_normalise(b4)
                middle_part(b1)
                exp_head(b3, 10)
                exp_head(b3, 11)
                exp_head(b3, 12)
                ln1_normalise(b0)

            run(act, step)

            def results(g, nth, i, first):
                act.wait_ge(ye_ps, g + 1)
                if not first:
                    act.wait_ge(ys_st[i], 16 * nth)
                nc.scalar.activation(ys_sb[i][:].rearrange("p k f -> p (k f)"), mx_ps[i][:].rearrange("p a b -> p (a b)"),
                                     ACT.Copy).then_inc(ye_d, 1)
                act.wait_ge(ye_d, g + 1)
                dst = ys_d[g * UG * UR:(g + 1) * UG * UR, :] if isinstance(g, int) else ys_d[bass.ds(g * (UG * UR), UG * UR), :]
                act.dma_start(dst.rearrange("(u p k) f -> p u k f", u=UG, k=TB),
                              ys_sb[i][:].rearrange("p (u k) f -> p u k f", u=UG)).then_inc(ys_st[i], 16)

            results(0, 0, 0, True)
            results(1, 0, 1, True)
            with act.Fori(1, GROUPS_E // 2) as n:
                for i in range(2):
                    results(n * 2 + i, n, i, False)

        @block.vector
        def _(dve):
            v = nc.vector
            v.memset(zeros[:], 0.0).then_inc(dve_const, 1)
            v.memset(eps[:, 0:1], LN_EPS).then_inc(dve_const, 1)
            v.memset(eps[:, 1:2], RMS_EPS).then_inc(dve_const, 1)
            dve.wait_ge(gp_const, 10)
            v.tensor_scalar(zsel[:], iota_z[:], 0.0, None, ALU.is_ge).then_inc(zc, 1)
            v.tensor_scalar(zlt[:], iota_z[:], float(ZR), None, ALU.is_lt).then_inc(zc, 1)
            dve.wait_ge(zc, 2)
            v.tensor_tensor(zsel[:], zsel[:], zlt[:], ALU.mult).then_inc(zc, 1)
            dve.wait_ge(zc, 3)
            v.tensor_tensor(zlt[:], zsel[:], iota_z[:], ALU.mult).then_inc(zc, 1)
            dve.wait_ge(zc, 4)
            v.tensor_reduce(zrow[:], zlt[:], AX.X, ALU.add).then_inc(zc, 1)
            dve.wait_ge(zc, 5)
            dve.wait_ge(s_exp, 1)
            v.tensor_scalar(sgn[:], sc[:], 1.0, None, ALU.add).then_inc(s_e1, 1)
            dve.wait_ge(s_e1, 1)
            v.reciprocal(mag[:], sgn[:]).then_inc(s_e1, 1)
            dve.wait_ge(s_e1, 2)
            v.tensor_tensor(sc[:], c_sb[:], mag[:], ALU.mult).then_inc(s_sc, 1)
            dve.wait_ge(mod_ps, 1)
            v.tensor_copy(mod[:, SA * P:GABO * P], o_ps[0:NB, 0:3 * P]).then_inc(clamp, 1)
            v.tensor_copy(mod[:, SB * P:CB * P], o_ps[0:NB, 3 * P:4 * P]).then_inc(clamp, 1)
            v.tensor_copy(mod[:, CB * P:MODS * P], misc[0][0:NB, 0:2 * P]).then_inc(clamp, 1)
            dve.wait_ge(clamp, 3)
            k = 3
            for col in (CA, CB):
                m = mod[:, col * P:(col + 1) * P]
                v.tensor_scalar(m, m, 1.0, None, ALU.add).then_inc(mod_sb, 1)
            for col in (GA, GB):
                m = mod[:, col * P:(col + 1) * P]
                for ins in (
                    lambda: v.tensor_scalar(sgn[:], m, 0.0, 2.0, ALU.is_ge, ALU.mult),
                    lambda: v.scalar_tensor_tensor(mag[:], m, -1.0, m, ALU.mult, ALU.max),
                    lambda: v.tensor_scalar(mag[:], mag[:], 0.25, None, ALU.max),
                    lambda: v.scalar_tensor_tensor(m, sgn[:], -1.0, mag[:], ALU.add, ALU.mult),
                ):
                    ins().then_inc(clamp, 1)
                    k += 1
                    dve.wait_ge(clamp, k)
            v.tensor_tensor(mod[:, GABO * P:SB * P], mod[:, GA * P:GABO * P], bo_b[0:NB, :], ALU.mult).then_inc(mod_sb, 1)
            for raw, dst in ((wraw, wqkv), (braw, bqkv)):
                for k in range(2):
                    v.tensor_copy(dst[:, k * P:(k + 1) * P].rearrange("p (d h) -> p d h", h=H),
                                  raw[:, k * P:(k + 1) * P].rearrange("p (h d) -> p d h", d=HD)).then_inc(perm, 1)
            dve.wait_ge(perm, 4)

            def stats(src, st_t, st_d):
                for t in range(TB):
                    v.bn_stats(st_t[:, t], src[:, t]).then_inc(st_d, 1)

            def aggregate(n, st_t, st_d, mv, mv_d):
                wait(dve, st_d, TB * (n + 1))
                dve.nop(nofuse=True)
                for t in range(TB):
                    ins = v.bn_aggr(mv[:, t], st_t[:, t])
                ins.then_inc(mv_d, 1)

            def newton_a(n, y, half, y_d, t1, t1_d):
                wait(dve, y_d, n + 1)
                v.scalar_tensor_tensor(t1, y, half, y, ALU.mult, ALU.mult).then_inc(t1_d, 1)

            def newton_b(n, var, eps_v, t1, t1_d, t2, t2_d):
                wait(dve, t1_d, n + 1)
                v.scalar_tensor_tensor(t2, var, eps_v, t1, ALU.add, ALU.mult).then_inc(t2_d, 1)

            def newton_c(n, y, t2, t2_d, dst, dst_d):
                wait(dve, t2_d, n + 1)
                v.scalar_tensor_tensor(dst, t2, 1.5, y, ALU.add, ALU.mult).then_inc(dst_d, 1)

            def mean_shift(n, mv, rstd, rstd_d, shift, shift_d):
                wait(dve, rstd_d, n + 1)
                v.scalar_tensor_tensor(shift[:], mv[:, :, 0], -1.0, rstd[:], ALU.mult, ALU.mult).then_inc(shift_d, 1)

            @of_batch
            def ln1_stats(b):
                wait(dve, xp_ld[b.par], 32 * (b.nth + 1))
                stats(x_p[:, b.par], st1, st1_d)

            @of_batch
            def ln1_aggregate(b):
                aggregate(b.n, st1, st1_d, mv1, mv1_d)

            @of_batch
            def ln1_newton_a(b):
                newton_a(b.n, y1[:], -0.5, y1_d, n1[:], n1_d)

            @of_batch
            def ln1_newton_b(b):
                newton_b(b.n, mv1[:, :, 1], LN_EPS, n1[:], n1_d, n1b[:], n1b_d)

            @of_batch
            def ln1_newton_c(b):
                wait(dve, xh1_d, b.n)
                newton_c(b.n, y1[:], n1b[:], n1b_d, rstd1[:], rstd1_d)

            @of_batch
            def ln1_shift(b):
                mean_shift(b.n, mv1, rstd1, rstd1_d, shift1, shift1_d)

            @of_batch
            def qkv_out(b, t):
                wait(dve, v_d, b.n - 1)
                wait(dve, eg_d, b.n - 1)
                wait(dve, qn_d, TB * (b.n - 1))
                wait(dve, qkv_ps, TB * b.n + t + 1)
                v.tensor_tensor(qkvg[:, b.par, t], misc[BANK[f"qkv{t}"]][:, 0:QKVG], bqkv[:], ALU.add).then_inc(qkv_d, 1)

            @of_batch
            def square_sums(b):
                wait(dve, sq_d, b.n + 1)
                v.tensor_reduce(ss[:].rearrange("p (k h) -> p k h", h=H),
                                sq[:].rearrange("p t (k d h) -> p (t k) h d", k=2, h=H), AX.X, ALU.add).then_inc(ss_d, 1)

            @of_batch
            def rms_newton_a(b):
                newton_a(b.n, r0[:], -0.5 / HD, r0_d, n2[:], n2_d)

            @of_batch
            def rms_newton_b(b):
                newton_b(b.n, ss[:], RMS_EPS * HD, n2[:], n2_d, n2b[:], n2b_d)

            @of_batch
            def rms_newton_c(b):
                wait(dve, qn_d, TB * b.n)
                newton_c(b.n, r0[:], n2b[:], n2b_d, rr[:], rr_d)

            @of_batch
            def rest_part(b):
                wait(dve, hi_d, 2 * (b.n + 1))
                wait(dve, lo_d, b.n)
                for k in range(2):
                    ins = v.scalar_tensor_tensor(rest[:, k], misc[BANK["qkT"]][:, k * NT:(k + 1) * NT], w_col[:, k:k + 1],
                                                 parts[:, k, 0], ALU.mult, ALU.subtract)
                ins.then_inc(rest_d, 1)

            @of_batch
            def max_head(b, h):
                wait(dve, mps_r, H * b.n + h + 1)
                if h == 0:
                    wait(dve, mT_ps, b.n)
                v.tensor_reduce(negmax[:, :, h], mx_ps[h % 2][:], AX.X, ALU.max, negate=True).then_inc(mx_d, 1)

            @of_batch
            def max_rest(b):
                wait(dve, mhi_d, b.n + 1)
                wait(dve, mrow_ld, 32 * b.n)
                v.tensor_tensor(mmid[:], misc[BANK["mT"]][0:H, 0:NT], mhi[:], ALU.subtract).then_inc(mmid_d, 1)

            def heads_out(qc):
                return misc[BANK[f"o2{qc}"]][:].rearrange("p (h w) -> p h w", w=VW)

            @of_batch
            def denominator(b, qc):
                wait(dve, eg_d, b.n + 1)
                wait(dve, o2_ps, TB * b.n + qc + 1)
                v.scalar_tensor_tensor(den[:, qc], eg[:, b.par, qc], 1.0, heads_out(qc)[:, :, HD], ALU.add,
                                       ALU.mult).then_inc(den_d, 1)

            @of_batch
            def factor(b, qc):
                wait(dve, den_d, TB * b.n + qc + 1)
                v.reciprocal(fac[:, qc], den[:, qc]).then_inc(fac_d, 1)

            @of_batch
            def gated_out(b, qc):
                wait(dve, fac_d, TB * b.n + qc + 1)
                wait(dve, onT_ps, b.n)
                v.tensor_tensor(on[:, qc].rearrange("p (h d) -> p h d", d=HD), heads_out(qc)[:, :, 0:HD],
                                fac[:, qc].unsqueeze(2).broadcast_to([P, H, HD]), ALU.mult).then_inc(on_d, 1)

            @of_batch
            def attention_ga(b):
                wait(dve, wo_ps, b.n + 1)
                wait(dve, xo_ld[b.par], 32 * (b.nth + 1))
                wait(dve, x1_done, b.n)
                v.tensor_tensor(attg[:], misc[BANK["wo"]][:, 0:NT].rearrange("p (t f) -> p t f", f=P),
                                mod_o[:, b.par, 0:1, :].broadcast_to([P, TB, P]), ALU.mult).then_inc(attg_d, 1)

            @of_batch
            def ln2_stats(b):
                wait(dve, x1_done, b.n + 1)
                stats(x1[:, b.par], st2, st2_d)

            @of_batch
            def ln2_aggregate(b):
                aggregate(b.n, st2, st2_d, mv2, mv2_d)

            @of_batch
            def ln2_newton_a(b):
                newton_a(b.n, y2[:], -0.5, y2_d, n3[:], n3_d)

            @of_batch
            def ln2_newton_b(b):
                newton_b(b.n, mv2[:, :, 1], LN_EPS, n3[:], n3_d, n3b[:], n3b_d)

            @of_batch
            def ln2_newton_c(b):
                wait(dve, xh2_d, b.n)
                newton_c(b.n, y2[:], n3b[:], n3b_d, rstd2[:], rstd2_d)

            @of_batch
            def ln2_shift(b):
                mean_shift(b.n, mv2, rstd2, rstd2_d, shift2, shift2_d)

            @of_batch
            def logits_out(b):
                wait(dve, lg_ps, b.n + 1)
                v.tensor_copy(lg[:].rearrange("p t e -> p (t e)"), misc[BANK["lg"]][:, 0:TB * E]).then_inc(lg_d, 1)

            @of_batch
            def top_logits(b):
                wait(dve, lg_d, b.n + 1)
                dve.nop(nofuse=True)
                for t in range(TB):
                    ins = v.max(top[:, t], lg[:, t])
                ins.then_inc(top_d, 1)

            @of_batch
            def less_largest(b):
                wait(dve, top_d, b.n + 1)
                wait(dve, elg_d, b.n)
                v.tensor_tensor(dlg[:, :, 0:E], lg[:], top[:, :, 0:1].broadcast_to([P, TB, E]), ALU.subtract).then_inc(dlg_d, 1)
                v.tensor_tensor(dlg[:, :, E:E + TOPK], top[:, :, 0:TOPK], top[:, :, 0:1].broadcast_to([P, TB, TOPK]),
                                ALU.subtract).then_inc(dlg_d, 1)

            @of_batch
            def top_experts(b):
                wait(dve, top_d, b.n + 1)
                dve.nop(nofuse=True)
                for t in range(TB):
                    ins = v.max_index(topi[:, t], top[:, t], lg[:, t])
                ins.then_inc(topi_d, 1)

            @of_batch
            def expert_index(b):
                wait(dve, topi_d, b.n + 1)
                wait(dve, idxa_d, b.n)
                v.tensor_copy(idx[:], topi[:, :, 0:TOPK].rearrange("p t j -> p j t")).then_inc(idx_d, 1)

            @of_batch
            def one_hot(b):
                wait(dve, idx_d, b.n + 1)
                v.tensor_tensor(oh[:].rearrange("p j t e -> p (j t) e"),
                                iota_e[:].unsqueeze(1).broadcast_to([P, TOPK * TB, E]),
                                idx[:].rearrange("p j t -> p (j t)").unsqueeze(2).broadcast_to([P, TOPK * TB, E]),
                                ALU.is_equal).then_inc(oh_d, 1)

            @of_batch
            def router_sum(b):
                wait(dve, elg_d, b.n + 1)
                v.tensor_reduce(esum[:], elg[:, :, 0:E], AX.X, ALU.add).then_inc(esum_d, 1)

            @of_batch
            def router_inverse(b):
                wait(dve, esum_d, b.n + 1)
                wait(dve, p_d, b.n)
                v.reciprocal(rsum[:], esum[:]).then_inc(rsum_d, 1)

            @of_batch
            def chosen(b):
                wait(dve, oh_d, b.n + 1)
                wait(dve, rank_ps, b.n)
                v.tensor_tensor(mask[:], oh[:, 0], oh[:, 1], ALU.add).then_inc(mask_d, 1)

            @of_batch
            def ranks(b):
                wait(dve, rank_ps, b.n + 1)
                wait(dve, carry_d, b.n)
                v.tensor_tensor(rk[:], misc[BANK["rank"]][:, 0:TB * E].rearrange("p (t e) -> p t e", e=E),
                                carry[:].unsqueeze(1).broadcast_to([P, TB, E]), ALU.add).then_inc(rk_d, 1)

            @of_batch
            def add_counts(b):
                wait(dve, rk_d, b.n + 1)
                v.tensor_tensor(carry[:], misc[BANK["rank"]][:, TB * E:(TB + 1) * E], carry[:], ALU.add).then_inc(carry_d, 1)

            @of_batch
            def chosen_ranks(b):
                wait(dve, rk_d, b.n + 1)
                v.tensor_tensor(ohr[:].rearrange("p j t e -> p j (t e)"), oh[:].rearrange("p j t e -> p j (t e)"),
                                rk[:].rearrange("p t e -> p (t e)").unsqueeze(1).broadcast_to([P, TOPK, TB * E]),
                                ALU.mult).then_inc(ohr_d, 1)

            @of_batch
            def slot_value(b):
                wait(dve, ohr_d, b.n + 1)
                wait(dve, slota_d, b.n)
                v.tensor_reduce(slot_f[:].rearrange("p (j t) -> p j t", t=TB), ohr[:], AX.X, ALU.add).then_inc(slotf_d, 1)

            @of_batch
            def slot_number(b):
                wait(dve, slotf_d, b.n + 1)
                wait(dve, scat[b.par], 64 * b.nth)
                v.tensor_copy(slot[:, b.par], slot_f[:]).then_inc(slot_d, 1)

            def step(b0, b1, b2, b3, b4, b5):
                ln1_stats(b0)
                top_logits(b5)
                top_experts(b5)
                max_rest(b3)
                denominator(b4, 0)
                factor(b4, 0)
                ln1_aggregate(b0)
                gated_out(b4, 0)
                denominator(b4, 1)
                factor(b4, 1)
                gated_out(b4, 1)
                expert_index(b5)
                one_hot(b5)
                qkv_out(b1, 0)
                qkv_out(b1, 1)
                max_head(b2, 0)
                max_head(b2, 1)
                square_sums(b1)
                attention_ga(b4)
                chosen(b5)
                max_head(b2, 2)
                rms_newton_a(b1)
                less_largest(b5)
                rms_newton_b(b1)
                ln2_stats(b4)
                rms_newton_c(b1)
                ln2_aggregate(b4)
                max_head(b2, 3)
                max_head(b2, 4)
                ln1_newton_a(b0)
                ranks(b5)
                ln1_newton_b(b0)
                ln2_newton_a(b4)
                max_head(b2, 5)
                ln2_newton_b(b4)
                ln1_newton_c(b0)
                max_head(b2, 6)
                ln2_newton_c(b4)
                ln1_shift(b0)
                router_sum(b5)
                ln2_shift(b4)
                rest_part(b1)
                max_head(b2, 7)
                max_head(b2, 8)
                max_head(b2, 9)
                max_head(b2, 10)
                add_counts(b5)
                max_head(b2, 11)
                chosen_ranks(b5)
                slot_value(b5)
                router_inverse(b5)
                max_head(b2, 12)
                slot_number(b5)
                max_head(b2, 13)
                max_head(b2, 14)
                max_head(b2, 15)
                logits_out(b4)

            run(dve, step)

            steps = [0]

            def chained(ins, s=tab, n=steps):
                ins.then_inc(s, 1)
                n[0] += 1
                dve.wait_ge(s, n[0])

            dve.wait_ge(carry_d, NB)
            groups = [P, ZG, P // ZR]
            chained(v.tensor_tensor(zend[:], carry[:].rearrange("p (g e) -> p g e", g=ZG),
                                    zsel[:].unsqueeze(1).broadcast_to(groups), ALU.mult))
            chained(v.tensor_reduce(zfirst[:], zend[:], AX.X, ALU.add))
            v.tensor_scalar(zidx[:, 0], zfirst[:], zrow[:, 0:1], None, ALU.add).then_inc(zidx_d, 1)
            chained(v.tensor_scalar(zblock[:], zfirst[:], 1.0 / ZR, 0.5 - 0.5 / ZR, ALU.mult, ALU.add))
            v.tensor_scalar(zidx[:, 1], zblock[:], zrow[:, 0:1], None, ALU.add).then_inc(zidx_d, 1)
            chained(v.tensor_tensor(cnt[:], carry[:], region0[:], ALU.subtract))
            chained(v.tensor_tensor(gtn[:], cnt[:].unsqueeze(2).broadcast_to([P, E, TOK // UR]),
                                    iota_n[:].unsqueeze(1).broadcast_to([P, E, TOK // UR]), ALU.is_gt))
            chained(v.tensor_reduce(nunit[:], gtn[:], AX.X, ALU.add))
            chained(v.tensor_tensor_scan(uend[:], ones_f[:, 0:E], nunit[:], 0.0, ALU.mult, ALU.add))
            chained(v.tensor_tensor(ubeg[:], uend[:], nunit[:], ALU.subtract))
            chained(v.tensor_scalar(ubrow[:], ubeg[:], float(UR), None, ALU.mult))
            chained(v.tensor_tensor(delta[:], ubrow[:], region0[:], ALU.subtract))
            chained(v.tensor_scalar(cmap[:], delta[:], -1.0, -float(DUMP), ALU.mult, ALU.add))
            chained(v.tensor_scalar(uge[:], ubeg[:], iota_p[:, 0:1], None, ALU.is_le))
            chained(v.tensor_scalar(ult[:], uend[:], iota_p[:, 0:1], None, ALU.is_gt))
            chained(v.tensor_tensor(uin[:], uge[:], ult[:], ALU.mult))
            chained(v.tensor_scalar(unum[:], iota_p[:], float(UR), None, ALU.mult))
            chained(v.tensor_scalar(usel[:], cmap[:], unum[:, 0:1], None, ALU.add))
            chained(v.tensor_tensor(cmap[:], usel[:], uin[:], ALU.mult))
            chained(v.tensor_reduce(ucol2[:], cmap[:], AX.X, ALU.add))
            chained(v.tensor_scalar(ucol[:, 0:1], ucol2[:], float(DUMP), None, ALU.add))
            chained(v.tensor_tensor(usel[:], iota_e[:], uin[:], ALU.mult))
            chained(v.tensor_reduce(ucol2[:], usel[:], AX.X, ALU.add))
            chained(v.tensor_scalar(ucol[:, 1:2], ucol2[:], float(P), None, ALU.mult))
            assert steps[0] == TABLE_STEPS
            dve.wait_ge(tab_ps, 1)
            v.tensor_copy(table[0:1, :], o_ps[0:1, 0:2 * P]).then_inc(table_d, 1)

            nlook = [0]

            def rows_out(g, i):
                wait(dve, xsT_ps, g + 1)
                wait(dve, ye_ps, g - 1)
                v.tensor_copy(xsT[i][:], st_ps[i][:].rearrange("p a b -> p (a b)")).then_inc(xsT_d, 1)

            rows_out(0, 0)
            rows_out(1, 1)
            dve.wait_ge(slota_d, NB)
            dve.wait_ge(idxa_d, NB)
            dve.wait_ge(p_d, NB)
            for c in range(NPAIR // CH):
                pairs = slice(c * CH, (c + 1) * CH)
                chained(v.tensor_tensor(ohd[:], iota_e[:].unsqueeze(1).broadcast_to([P, CH, E]),
                                        idx_all[:, pairs].unsqueeze(2).broadcast_to([P, CH, E]), ALU.is_equal), look, nlook)
                chained(v.tensor_tensor(ohd2[:], ohd[:], delta[:].unsqueeze(1).broadcast_to([P, CH, E]), ALU.mult), look, nlook)
                chained(v.tensor_reduce(dsl[:, pairs], ohd2[:], AX.X, ALU.add), look, nlook)
            chained(v.tensor_tensor(gidx_f[:], slot_all[:], dsl[:], ALU.add), look, nlook)
            with dve.Fori(1, GROUPS_E // 2) as n:
                for i in range(2):
                    rows_out(n * 2 + i, i)

            def gather_rows(b, par, first):
                if not first:
                    dve.wait_ge(yg_ld[par], 64 * (b // 2) if isinstance(b, int) else b)
                v.tensor_copy(gi[:, par], gidx_f[:, bass.ts(b, TOPK * TB)]).then_inc(gi_d, 1)

            def combine(b, nth, par):
                wait(dve, yg_ld[par], 64 * (nth + 1))
                wait(dve, f_ld[par], 32 * (nth + 1))
                for t in range(TB):
                    v.tensor_scalar(yw[:, t], yg[:, par, t], p_all[:, bass.ds(b * (TOPK * TB) + t, 1)], None,
                                    ALU.mult).then_inc(yw_d, 1)
                for t in range(TB):
                    wait(dve, yw_d, TB * b + t + 1)
                    v.scalar_tensor_tensor(yc[:, t], yg[:, par, TB + t], p_all[:, bass.ds(b * (TOPK * TB) + TB + t, 1)],
                                           yw[:, t], ALU.mult, ALU.add).then_inc(yc_d, 1)
                wait(dve, yc_d, TB * (b + 1))
                v.tensor_tensor(yb[:], yc[:], gb_f[:, par].unsqueeze(1).broadcast_to([P, TB, P]), ALU.mult).then_inc(yb_d, 1)
                wait(dve, yb_d, b + 1)
                wait(dve, out_st[par], 16 * nth)
                v.tensor_tensor(of[:, par], yb[:], x1_f[:, par], ALU.add).then_inc(of_d, 1)

            v.tensor_copy(gi[:, 0], gidx_f[:, 0:TOPK * TB]).then_inc(gi_d, 1)
            v.tensor_copy(gi[:, 1], gidx_f[:, TOPK * TB:2 * TOPK * TB]).then_inc(gi_d, 1)

            def combine_and_next(b, nth, par, more):
                combine(b, nth, par)
                if more:
                    v.tensor_copy(gi[:, par], gidx_f[:, bass.ts(b + 2, TOPK * TB)]).then_inc(gi_d, 1)

            for par in range(2):
                combine_and_next(par, 0, par, True)
            with dve.Fori(1, NB // 2 - 1) as n:
                for par in range(2):
                    combine_and_next(n * 2 + par, n, par, True)
            for par in range(2):
                combine_and_next(NB - 2 + par, NB // 2 - 1, par, False)

        @block.tensor
        def _(pe):
            t_ = nc.tensor
            pe.wait_ge(gp_const, 4)
            pe.wait_ge(s_sc, 1)
            t_.transpose(misc[0][:, 0:NB], sc[:], ident[0:NB, 0:NB]).then_inc(cT_ps, 1)
            pe.wait_ge(cT_done, 1)
            t_.matmul(o_ps[0:NB, :], cT[:], wm[:, 0:4 * P], start=True, stop=True)
            t_.matmul(misc[0][0:NB, 0:2 * P], cT[:], wm[:, 4 * P:6 * P], start=True, stop=True).then_inc(mod_ps, 1)
            pe.wait_ge(clamp, 3)
            pe.wait_ge(loads, LOADS)
            t_.transpose(misc[0][:, 0:E], rw[:], ident[0:E, 0:E]).then_inc(rwT_ps, 1)
            pe.wait_ge(perm, 4)

            free = [(rwT_done, 1), None]

            def emptied(item, b):
                return {
                    "hT": (hT_d, b.n + 1), "qkv0": (qkv_d, TB * b.n + 1), "qkv1": (qkv_d, TB * b.n + 2),
                    "qkT": (rest_d, b.n + 1), "mT": (mmid_d, b.n + 1), "o20": (on_d, TB * b.n + 1), "o21": (on_d, TB * b.n + 2),
                    "onT": (onT_d, b.n + 1), "wo": (attg_d, b.n + 1), "h2T": (h2T_d, b.n + 1), "lg": (lg_d, b.n + 1),
                    "rank": (carry_d, b.n + 1),
                }[item]

            def take(item, b):
                bank = BANK[item]
                if free[bank] is not None:
                    wait(pe, *free[bank])
                free[bank] = emptied(item, b)
                return misc[bank]

            @of_batch
            def transpose_h1(b):
                wait(pe, h1_d, b.n + 1)
                bank = take("hT", b)
                for t in range(TB):
                    last = t_.transpose(bank[:, t * P:(t + 1) * P], h1[:, t], ident[:])
                last.then_inc(hT_ps, 1)

            @of_batch
            def project(b, t):
                wait(pe, hT_d, b.n + 1)
                bank = take(f"qkv{t}", b)
                t_.matmul(bank[:, 0:QKVG], hT[:, t * P:(t + 1) * P], wqkv[:], start=True, stop=True).then_inc(qkv_ps, 1)

            @of_batch
            def transpose_qk(b):
                wait(pe, qn_d, TB * (b.n + 1))
                bank = take("qkT", b)
                for k in range(2):
                    for t in range(TB):
                        last = t_.transpose(bank[:, (k * TB + t) * P:(k * TB + t + 1) * P], qn[:, t, k * P:(k + 1) * P], ident[:])
                last.then_inc(qkT_ps, 1)

            @of_batch
            def scores_q(b, h):
                if h % (H // 2) == 0:
                    wait(pe, aug_ld[b.par][h // (H // 2)], 64 * (b.nth + 1))
                wait(pe, mx_d, H * b.n + h - 1)
                pe.nop(nofuse=True)
                for qc in range(TB):
                    last = t_.matmul(mx_ps[h % 2][:, qc], q_aug[b.par][0:MROW, h, qc * P:(qc + 1) * P],
                                     k_aug[b.par][0:MROW, h, :], start=True, stop=True)
                last.then_inc(mps_r, 1)

            @of_batch
            def transpose_max(b):
                wait(pe, mx_d, H * (b.n + 1))
                bank = take("mT", b)
                for qc in range(TB):
                    last = t_.transpose(bank[0:H, qc * P:(qc + 1) * P], negmax[:, qc], ident[:])
                last.then_inc(mT_ps, 1)

            @of_batch
            def scores_k(b, h):
                if h == 0:
                    wait(pe, mrow_ld, 32 * (b.n + 1))
                wait(pe, exp_d, H * b.n + h + score_bank_read(b, h))
                pe.nop(nofuse=True)
                for kc in range(TB):
                    last = t_.matmul(st_ps[score_bank(b, h)][:, kc], k_aug[b.par][:, h, kc * P:(kc + 1) * P],
                                     q_aug[b.par][:, h, :], start=True, stop=True)
                last.then_inc(st_r, 1)

            @of_batch
            def probs_v(b, g):
                wait(pe, exp_d, H * b.n + 4 * g + 4)
                wait(pe, oT_d, GROUPS * b.n + g)
                if g == 0:
                    wait(pe, v_d, b.n + 1)
                pe.nop(nofuse=True)
                for kc in range(TB):
                    for j in range(4):
                        h = 4 * g + j
                        last = t_.matmul(o_ps[32 * j:32 * j + VW, 0:NT], v_aug[b.par][:, kc, h, :],
                                         pr[:, h % PR, kc, :], start=(kc == 0), stop=(kc == TB - 1))
                last.then_inc(pv_d, 1)

            @of_batch
            def transpose_out(b, qc):
                wait(pe, oT_d, GROUPS * (b.n + 1))
                bank = take(f"o2{qc}", b)
                for g in range(GROUPS):
                    last = t_.transpose(bank[:, g * P:(g + 1) * P], oT[:, g, qc * P:(qc + 1) * P], ident[:])
                last.then_inc(o2_ps, 1)

            @of_batch
            def transpose_on(b):
                wait(pe, on_d, TB * (b.n + 1))
                bank = take("onT", b)
                for qc in range(TB):
                    last = t_.transpose(bank[:, qc * P:(qc + 1) * P], on[:, qc], ident[:])
                last.then_inc(onT_ps, 1)

            @of_batch
            def project_out(b):
                wait(pe, onT_d, b.n + 1)
                bank = take("wo", b)
                for qc in range(TB):
                    last = t_.matmul(bank[:, qc * P:(qc + 1) * P], onT[:, qc * P:(qc + 1) * P], wo[:], start=True, stop=True)
                last.then_inc(wo_ps, 1)

            @of_batch
            def transpose_h2(b):
                wait(pe, h2_d, b.n + 1)
                bank = take("h2T", b)
                for t in range(TB):
                    last = t_.transpose(bank[:, t * P:(t + 1) * P], h2[:, b.par, t], ident[:])
                last.then_inc(h2T_ps, 1)

            @of_batch
            def logits(b):
                wait(pe, h2T_d, b.n + 1)
                bank = take("lg", b)
                for t in range(TB):
                    last = t_.matmul(bank[:, t * E:(t + 1) * E], h2T[:, t * P:(t + 1) * P], rwT[:], start=True, stop=True)
                last.then_inc(lg_ps, 1)

            @of_batch
            def count_before(b):
                wait(pe, mask_d, b.n + 1)
                bank = take("rank", b)
                m = [mask[:, t] for t in range(TB)]
                t_.matmul(bank[:, 0:TB * E], tri[:], mask[:].rearrange("p t e -> p (t e)"), start=True, stop=False,
                          skip_group_check=True)
                t_.matmul(bank[:, E:2 * E], ones_b[:], m[0], start=False, stop=False, skip_group_check=True)
                t_.matmul(bank[:, 2 * E:3 * E], ones_b[:], m[0], start=False, stop=False, skip_group_check=True)
                t_.matmul(bank[:, 2 * E:3 * E], ones_b[:], m[1], start=False, stop=True,
                          skip_group_check=True).then_inc(rank_ps, 1)

            def step(b0, b1, b2, b3, b4, b5):
                scores_q(b3, 15)
                probs_v(b4, 3)
                transpose_h1(b1)
                transpose_max(b3)
                transpose_out(b4, 0)
                transpose_out(b4, 1)
                project(b1, 0)
                project(b1, 1)
                scores_q(b2, 0)
                transpose_on(b4)
                scores_q(b2, 1)
                scores_k(b3, 0)
                scores_k(b3, 1)
                project_out(b4)
                scores_k(b3, 2)
                scores_q(b2, 2)
                scores_k(b3, 3)
                scores_k(b3, 4)
                count_before(b5)
                scores_q(b2, 3)
                scores_k(b3, 5)
                scores_q(b2, 4)
                scores_k(b3, 6)
                probs_v(b3, 0)
                scores_k(b3, 7)
                scores_q(b2, 5)
                scores_k(b3, 8)
                scores_q(b2, 6)
                transpose_qk(b1)
                scores_k(b3, 9)
                scores_k(b3, 10)
                scores_q(b2, 7)
                probs_v(b3, 1)
                scores_q(b2, 8)
                scores_k(b3, 11)
                scores_q(b2, 9)
                scores_k(b3, 12)
                scores_q(b2, 10)
                scores_k(b3, 13)
                scores_q(b2, 11)
                scores_k(b3, 14)
                scores_k(b3, 15)
                scores_q(b2, 12)
                transpose_h2(b4)
                scores_q(b2, 13)
                probs_v(b3, 2)
                scores_q(b2, 14)
                logits(b4)

            def seed(last):
                for item, k in LAST_IN_BANK:
                    free[BANK[item]] = emptied(item, last[k])

            run(pe, step, seed)

            pe.wait_ge(tab, TABLE_STEPS)
            for k in range(2):
                last = t_.matmul(o_ps[0:1, k * P:(k + 1) * P], ucol[:, k:k + 1], ident[:], start=True, stop=True)
            last.then_inc(tab_ps, 1)
            pe.wait_ge(table_d, 1)

            pe.wait_ge(we_ld, 16)

            def expert_in(g, nth, i, first):
                pe.wait_ge(xs_ld[i], 16 * UG * (nth + 1) if isinstance(nth, int) else nth * (16 * UG) + 16 * UG)
                if not first:
                    pe.wait_ge(xsT_d, g - 1)
                pe.nop(nofuse=True)
                bank = st_ps[i % 2][:].rearrange("p a b -> p (a b)")
                for k in range(TG):
                    last = t_.transpose(bank[:, k * P:(k + 1) * P], xs_sb[i][:, k, :], ident[:])
                last.then_inc(xsT_ps, 1)

            def expert_out(g, i, first):
                cols = [pe.value_load(table[0:1, bass.ds(g * UG + (P + k), 1)], min_val=0, max_val=(E - 1) * P)
                        for k in range(UG)]
                pe.wait_ge(xsT_d, g + 1)
                if not first:
                    pe.wait_ge(ye_d, g - 1)
                pe.nop(nofuse=True)
                bank = mx_ps[i % 2][:].rearrange("p a b -> p (a b)")
                for k in range(TG):
                    last = t_.matmul(bank[:, k * P:(k + 1) * P], xsT[i % 2][:, k * P:(k + 1) * P],
                                     we[:, bass.ds(cols[k // TB], P)], start=True, stop=True)
                last.then_inc(ye_ps, 1)

            for pair in range(XB // 2):
                for i in (2 * pair, 2 * pair + 1):
                    expert_in(i, 0, i, i < 2)
                for i in (2 * pair, 2 * pair + 1):
                    expert_out(i, i, i < 2)
            with pe.Fori(1, GROUPS_E // XB) as n:
                for pair in range(XB // 2):
                    for i in (2 * pair, 2 * pair + 1):
                        expert_in(n * XB + i, n, i, False)
                    for i in (2 * pair, 2 * pair + 1):
                        expert_out(n * XB + i, i, False)


_INS = ['L0_attn_x', 'L0_attn_Wq', 'L0_attn_bq', 'L0_attn_Wk', 'L0_attn_bk', 'L0_attn_Wv', 'L0_attn_bv', 'L0_attn_Wo',
        'L0_attn_bo', 'L0_attn_qn_w', 'L0_attn_kn_w', 'L0_ffn_router_w', 'L0_ffn_expert_weights', 'L0_c', 'L0_wmod']


def kernel(**inputs):
    import concourse.bacc as bacc
    from concourse.bass_utils import run_bass_kernel_spmd

    nc = bacc.Bacc("TRN2", target_bir_lowering=False, num_devices=1)
    arrays, args = {}, []
    for name in _INS:
        a = np.ascontiguousarray(inputs[name])
        arrays[f"in_{name}"] = a
        args.append(nc.dram_tensor(f"in_{name}", a.shape, mybir.dt.from_np(a.dtype), kind="ExternalInput").ap())
    args.append(nc.dram_tensor("out_x", (NB, NT, P), F32, kind="ExternalOutput").ap())
    build(nc, *args)
    r = run_bass_kernel_spmd(nc, [arrays], core_ids=[0])
    return r.results[0]["out_x"]
```

```python
import numpy as np

import concourse.bass as bass
import concourse.mybir as mybir

F32 = mybir.dt.float32
BF16 = mybir.dt.bfloat16
I32 = mybir.dt.int32
U32 = mybir.dt.uint32
ALU = mybir.AluOpType
ACT = mybir.ActivationFunctionType
AX = mybir.AxisListType

P = 128
NB, NT = 32, 256
TB = NT // P
H, HD = 16, 8
E, TOPK = 32, 2
TOK = NB * NT
QKVG = 3 * P + H
TERMS = (3, 2, 1)
ROWS = HD * sum(TERMS)
MROW = P - 2
GROUPS = H // 4
VW = 32
UR = 2 * P
ZR = 16
REGION = TOK + 2 * UR
DUMP = E * REGION
MAX_UNITS = (TOPK * TOK + E * (UR - 1)) // UR
UG = 2
XB = 4
GROUPS_E = -(-MAX_UNITS // (UG * XB)) * XB
UNITS = GROUPS_E * UG
TG = UG * UR // P
assert UNITS <= P and UR // ZR == ZR
LN_EPS, RMS_EPS = 1e-5, 1e-6
SCALE = float(HD) ** -0.5
TABLE_STEPS = 22
PR = 8
DEPTH = 9
LOOP_FROM = -(-(DEPTH + 1) // 2)
BANK = {"hT": 0, "qkv0": 1, "qkv1": 0, "qkT": 0, "mT": 1, "o20": 1, "o21": 0, "onT": 0, "wo": 0, "h2T": 1, "lg": 0, "rank": 1}
LAST_IN_BANK = (("lg", 5), ("o20", 3))
SA, CA, GA, GABO, SB, CB, GB, MODS = range(8)


def build(nc, x, Wq, bq, Wk, bk, Wv, bv, Wo, bo, qn_w, kn_w, router_w, expert_w, c_in, wmod, out):
    from contextlib import ExitStack

    ctx = ExitStack()
    LOADS = 16 * (11 + 2)

    def sb(name, shape, dt=F32):
        return ctx.enter_context(nc.sbuf_tensor(name, shape, dt))

    def ps(name, shape, dt=F32):
        return ctx.enter_context(nc.psum_tensor(name, shape, dt))

    def sem(name):
        return ctx.enter_context(nc.semaphore(name))

    def dram(name, shape, dt=F32):
        return nc.dram_tensor(name, shape, dt, kind="Internal").ap()

    with ctx:
        mod_d = dram("mod_d", (NB, MODS * P))
        q_d = dram("q_d", (2, sum(TERMS), P, NT), BF16)
        k_d = dram("k_d", (2, 3, P, NT), BF16)
        x1_d = dram("x1_d", (NB, NT, P))
        xs_d = dram("xs_d", (DUMP + UR, P))
        ys_d = dram("ys_d", (UNITS * UR, P))

        ident = sb("ident", [P, P])
        ones_f = sb("ones_f", [P, P])
        tri = sb("tri", [P, P], BF16)
        ones_b = sb("ones_b", [P, P], BF16)
        iota_e = sb("iota_e", [P, E])
        iota_p = sb("iota_p", [P, 1])
        iota_n = sb("iota_n", [P, TOK // UR])
        iota_z = sb("iota_z", [P, P // ZR])
        region0 = sb("region0", [P, E])
        eps = sb("eps", [P, 2])
        zeros = sb("zeros", [P, ZR * P])
        zsel = sb("zsel", [P, P // ZR])
        zlt = sb("zlt", [P, P // ZR])
        zrow = sb("zrow", [P, 1])
        wqkv = sb("wqkv", [P, QKVG])
        bqkv = sb("bqkv", [P, QKVG])
        wo = sb("wo", [P, P])
        bo_b = sb("bo_b", [P, P])
        wraw = sb("wraw", [P, 2 * P])
        braw = sb("braw", [P, 2 * P])
        w_col = sb("w_col", [P, 2])
        rw = sb("rw", [E, P])
        rwT = sb("rwT", [P, E])
        we = sb("we", [P, E * P])
        c_sb = sb("c_sb", [NB, P])
        sc = sb("sc", [NB, P])
        cT = sb("cT", [P, NB])
        wm = sb("wm", [P, 6 * P])
        mod = sb("mod", [NB, MODS * P])
        sgn = sb("sgn", [NB, P])
        mag = sb("mag", [NB, P])

        x_p = sb("x_p", [P, 2, TB, P])
        mod_p = sb("mod_p", [P, 2, 2, P])
        st1 = sb("st1", [P, TB, 6])
        mv1 = sb("mv1", [P, TB, 2])
        lnv1 = sb("lnv1", [P, TB])
        y1 = sb("y1", [P, TB])
        n1 = sb("n1", [P, TB])
        n1b = sb("n1b", [P, TB])
        rstd1 = sb("rstd1", [P, TB])
        shift1 = sb("shift1", [P, TB])
        xh1 = sb("xh1", [P, TB, P])
        h1a = sb("h1a", [P, TB, P])
        h1 = sb("h1", [P, TB, P])
        hT = sb("hT", [P, NT])
        qkvg = sb("qkvg", [P, 2, TB, QKVG])
        sq = sb("sq", [P, TB, 2 * P])
        ss = sb("ss", [P, TB * 2 * H])
        lnm = sb("lnm", [P, TB * 2 * H])
        r0 = sb("r0", [P, TB * 2 * H])
        n2 = sb("n2", [P, TB * 2 * H])
        n2b = sb("n2b", [P, TB * 2 * H])
        rr = sb("rr", [P, TB * 2 * H])
        qn = sb("qn", [P, TB, 2 * P])
        parts = sb("parts", [P, 2, 3, NT], BF16)
        rest = sb("rest", [P, 2, NT])
        q_aug = [sb(f"q_aug{i}", [P, H, NT], BF16) for i in range(2)]
        k_aug = [sb(f"k_aug{i}", [P, H, NT], BF16) for i in range(2)]
        negmax = sb("negmax", [P, TB, H])
        msplit = sb("msplit", [P, TB, 2, H])
        mlead = sb("mlead", [P, TB, H], BF16)
        mrows = sb("mrows", [2 * H, NT], BF16)
        v_aug = [sb(f"v_aug{i}", [P, TB, H, VW]) for i in range(2)]
        eg = sb("eg", [P, 2, TB, H])
        pr = sb("pr", [P, PR, TB, NT])
        oT = sb("oT", [P, GROUPS, NT])
        den = sb("den", [P, TB, H])
        fac = sb("fac", [P, TB, H])
        on = sb("on", [P, TB, P])
        onT = sb("onT", [P, NT])
        x_o = sb("x_o", [P, 2, TB, P])
        mod_o = sb("mod_o", [P, 2, 4, P])
        xga = sb("xga", [P, TB, P])
        attg = sb("attg", [P, TB, P])
        x1 = sb("x1", [P, 2, TB, P])
        st2 = sb("st2", [P, TB, 6])
        mv2 = sb("mv2", [P, TB, 2])
        lnv2 = sb("lnv2", [P, TB])
        y2 = sb("y2", [P, TB])
        n3 = sb("n3", [P, TB])
        n3b = sb("n3b", [P, TB])
        rstd2 = sb("rstd2", [P, TB])
        shift2 = sb("shift2", [P, TB])
        xh2 = sb("xh2", [P, TB, P])
        h2a = sb("h2a", [P, TB, P])
        h2 = sb("h2", [P, 2, TB, P])
        h2T = sb("h2T", [P, NT])
        lg = sb("lg", [P, TB, E])
        top = sb("top", [P, TB, 8])
        topi = sb("topi", [P, TB, 8], U32)
        dlg = sb("dlg", [P, TB, E + TOPK])
        elg = sb("elg", [P, TB, E + TOPK])
        esum = sb("esum", [P, TB])
        rsum = sb("rsum", [P, TB])
        idx = sb("idx", [P, TOPK, TB])
        oh = sb("oh", [P, TOPK, TB, E])
        mask = sb("mask", [P, TB, E], BF16)
        carry = sb("carry", [P, E])
        rk = sb("rk", [P, TB, E])
        ohr = sb("ohr", [P, TOPK, TB, E])
        slot_f = sb("slot_f", [P, TOPK * TB])
        slot = sb("slot", [P, 2, TOPK * TB], U32)
        slot_all = sb("slot_all", [P, NB * TOPK * TB])
        idx_all = sb("idx_all", [P, NB * TOPK * TB])
        p_all = sb("p_all", [P, NB * TOPK * TB])
        gtn = sb("gtn", [P, E, TOK // UR])
        cnt = sb("cnt", [P, E])
        nunit = sb("nunit", [P, E])
        uend = sb("uend", [P, E])
        ubeg = sb("ubeg", [P, E])
        ubrow = sb("ubrow", [P, E])
        cmap = sb("cmap", [P, E])
        delta = sb("delta", [P, E])
        uge = sb("uge", [P, E])
        ult = sb("ult", [P, E])
        uin = sb("uin", [P, E])
        usel = sb("usel", [P, E])
        ucol = sb("ucol", [P, 2])
        ucol2 = sb("ucol2", [P, 1])
        unum = sb("unum", [P, 1])
        table = sb("table", [P, 2 * P], I32)
        ZG = E * ZR // P
        zend = sb("zend", [P, ZG, P // ZR])
        zfirst = sb("zfirst", [P, ZG])
        zblock = sb("zblock", [P, ZG], I32)
        zidx = sb("zidx", [P, 2, ZG], U32)
        xs_sb = [sb(f"xs{i}", [P, TG, P]) for i in range(XB)]
        xsT = [sb(f"xsT{i}", [P, TG * P]) for i in range(XB)]
        ys_sb = [sb(f"ys{i}", [P, TG, P]) for i in range(2)]
        NPAIR = NB * TOPK * TB
        CH = 32
        ohd = sb("ohd", [P, CH, E])
        ohd2 = sb("ohd2", [P, CH, E])
        dsl = sb("dsl", [P, NPAIR])
        gidx_f = sb("gidx_f", [P, NPAIR])
        gi = sb("gi", [P, 2, TOPK * TB], U32)
        yg = sb("yg", [P, 2, TOPK * TB, P])
        x1_f = sb("x1_f", [P, 2, TB, P])
        gb_f = sb("gb_f", [P, 2, P])
        yw = sb("yw", [P, TB, P])
        yc = sb("yc", [P, TB, P])
        yb = sb("yb", [P, TB, P])
        of = sb("of", [P, 2, TB, P])

        st_ps = [ps(f"st_ps{i}", [P, TB, NT]) for i in range(3)]
        mx_ps = [ps(f"mx_ps{i}", [P, TB, NT]) for i in range(2)]
        o_ps = ps("o_ps", [P, 512])
        misc = [ps(f"misc{i}", [P, 512]) for i in range(2)]

        in_bank = [t[:].rearrange("p a b -> p (a b)") for t in st_ps] + [o_ps[:]]
        out_bank = [t[:].rearrange("p a b -> p (a b)") for t in mx_ps] + [t[:] for t in misc]

        loads = sem("loads")
        c_ld = sem("c_ld")
        aug_z, ones_ld = sem("aug_z"), sem("ones_ld")
        we_ld = sem("we_ld")
        perm = sem("perm")
        gp_const = sem("gp_const")
        dve_const = sem("dve_const")
        s_exp = sem("s_exp")
        s_e1 = sem("s_e1")
        s_sc = sem("s_sc")
        cT_ps, cT_done, mod_ps, mod_sb, rwT_ps, rwT_done = (
            sem(n) for n in ("cT_ps", "cT_done", "mod_ps", "mod_sb", "rwT_ps", "rwT_done"))
        clamp = sem("clamp")
        mod_st = sem("mod_st")
        xp_ld = [sem(f"xp_ld{i}") for i in range(2)]
        xo_ld = [sem(f"xo_ld{i}") for i in range(2)]
        st1_d, mv1_d, lnv1_d, y1_d, n1_d, n1b_d, rstd1_d, shift1_d, xh1_d, h1a_d, h1_d = (
            sem(n) for n in ("st1_d", "mv1_d", "lnv1_d", "y1_d", "n1_d", "n1b_d", "rstd1_d", "shift1_d", "xh1_d", "h1a_d", "h1_d"))
        hT_ps, hT_d, qkv_ps, qkv_d = (sem(n) for n in ("hT_ps", "hT_d", "qkv_ps", "qkv_d"))
        sq_d, ss_d, lnm_d, r0_d, n2_d, n2b_d, rr_d, qn_d = (
            sem(n) for n in ("sq_d", "ss_d", "lnm_d", "r0_d", "n2_d", "n2b_d", "rr_d", "qn_d"))
        qkT_ps, hi_d, rest_d, mid_d, lo_d = (sem(n) for n in ("qkT_ps", "hi_d", "rest_d", "mid_d", "lo_d"))
        parts_st = sem("parts_st")
        aug_ld = [[sem(f"aug_ld{i}{j}") for j in range(2)] for i in range(2)]
        mps_r, mx_d = sem("mps_r"), sem("mx_d")
        mlead_d, mwide_d, msplit_d, mT_ps, mrows_d = (sem(n) for n in ("mlead_d", "mwide_d", "msplit_d", "mT_ps", "mrows_d"))
        mrow_ld = sem("mrow_ld")
        v_d, eg_d = sem("v_d"), sem("eg_d")
        st_r, exp_d = sem("st_r"), sem("exp_d")
        pv_d, oT_d = sem("pv_d"), sem("oT_d")
        o2_ps, den_d, fac_d, on_d = sem("o2_ps"), sem("den_d"), sem("fac_d"), sem("on_d")
        onT_ps, onT_d, wo_ps, xga_d, attg_d, x1_done = (
            sem(n) for n in ("onT_ps", "onT_d", "wo_ps", "xga_d", "attg_d", "x1_done"))
        x1_st = [sem(f"x1_st{i}") for i in range(2)]
        st2_d, mv2_d, lnv2_d, y2_d, n3_d, n3b_d, rstd2_d, shift2_d, xh2_d, h2a_d, h2_d = (
            sem(n) for n in ("st2_d", "mv2_d", "lnv2_d", "y2_d", "n3_d", "n3b_d", "rstd2_d", "shift2_d", "xh2_d", "h2a_d", "h2_d"))
        h2T_ps, h2T_d, lg_ps, lg_d, top_d, topi_d, dlg_d, elg_d, esum_d, rsum_d, p_d, idx_d, idxa_d, oh_d, mask_d = (
            sem(n) for n in ("h2T_ps", "h2T_d", "lg_ps", "lg_d", "top_d", "topi_d", "dlg_d", "elg_d", "esum_d",
                             "rsum_d", "p_d", "idx_d", "idxa_d", "oh_d", "mask_d"))
        rank_ps, rk_d, carry_d, ohr_d, slotf_d, slot_d, slota_d = (
            sem(n) for n in ("rank_ps", "rk_d", "carry_d", "ohr_d", "slotf_d", "slot_d", "slota_d"))
        scat = [sem(f"scat{i}") for i in range(2)]
        tab = sem("tab")
        zc = sem("zc")
        zidx_d, tab_ps, table_d, tail_st, dump_st = (
            sem(n) for n in ("zidx_d", "tab_ps", "table_d", "tail_st", "dump_st"))
        xs_ld = [sem(f"xs_ld{i}") for i in range(XB)]
        xsT_ps, xsT_d, ye_ps, ye_d = sem("xsT_ps"), sem("xsT_d"), sem("ye_ps"), sem("ye_d")
        ys_st = [sem(f"ys_st{i}") for i in range(2)]
        look = sem("look")
        gidx_d, gi_d = sem("gidx_d"), sem("gi_d")
        yg_ld = [sem(f"yg_ld{i}") for i in range(2)]
        f_ld = [sem(f"f_ld{i}") for i in range(2)]
        yw_d, yc_d, yb_d, of_d = sem("yw_d"), sem("yc_d"), sem("yb_d"), sem("of_d")
        out_st = [sem(f"out_st{i}") for i in range(2)]

        def score_bank(b, h):
            return (h + b.par) % 3

        def score_bank_read(b, h):
            return -2 if b.par or h > 1 else -1

        def wait(eng, s, n):
            if isinstance(n, int) and n <= 0:
                return
            eng.wait_ge(s, n)

        class Batch:

            def __init__(self, n, par, nth):
                self.n, self.par, self.nth = n, par, nth

        class Step:

            def __init__(self, s, pair=None):
                self.s, self.pair = s, pair

            def batches(self):
                out = []
                for k in range(DEPTH):
                    if self.pair is None:
                        n = self.s - k
                        out.append(Batch(n, n % 2, n // 2) if 0 <= n < NB else None)
                    else:
                        par = (self.s - k) % 2
                        out.append(Batch(self.pair * 2 + (self.s - k), par, self.pair + (self.s - k - par) // 2))
                return out

        def of_batch(task):
            def call(b, *which):
                if b is not None:
                    task(b, *which)
            return call

        def run(eng, step, seed=lambda last: None):
            for s in range(2 * LOOP_FROM):
                step(*Step(s).batches())
            with eng.Fori(LOOP_FROM, NB // 2) as pair:
                seed(Step(-1, pair).batches())
                for parity in range(2):
                    step(*Step(parity, pair).batches())
            seed(Step(NB - 1).batches())
            for s in range(NB, NB + DEPTH - 1):
                step(*Step(s).batches())

        def load_unit(eng, g, k, i):
            row = eng.value_load(table[0:1, bass.ds(g * UG + k, 1)], min_val=0, max_val=DUMP)
            eng.dma_start(xs_sb[i][:, k * TB:(k + 1) * TB, :],
                          xs_d[bass.ds(row, UR), :].rearrange("(p k) f -> p k f", k=TB)).then_inc(xs_ld[i], 16)

        def rows_complete(eng):
            for i in range(2):
                eng.wait_ge(scat[i], 16 * TOPK * TB * NB // 2)
            eng.wait_ge(dump_st, 16)
            eng.wait_ge(tail_st, 16 * 2 * ZG)
            eng.wait_ge(table_d, 1)

        block = ctx.enter_context(nc.Block())

        @block.sync
        def _(sp):
            for dst, src in ((c_sb[:], c_in), (wm[:], wmod)):
                sp.dma_start(dst, src).then_inc(c_ld, 16)
            for dst, src in (
                (rw[:], router_w), (wraw[:, 0:P], Wq[:, 0:P]), (wraw[:, P:2 * P], Wk),
                (wqkv[:, 2 * P:3 * P], Wv), (wqkv[:, 3 * P:QKVG], Wq[:, P:P + H]),
                (braw[:, 0:P], bq[0:P].partition_broadcast(P)), (braw[:, P:2 * P], bk.partition_broadcast(P)),
                (bqkv[:, 2 * P:3 * P], bv.partition_broadcast(P)), (bqkv[:, 3 * P:QKVG], bq[P:P + H].partition_broadcast(P)),
                (wo[:], Wo), (bo_b[:], bo.partition_broadcast(P)),
            ):
                sp.dma_start(dst, src).then_inc(loads, 16)
            for k, w in enumerate((qn_w, kn_w)):
                sp.dma_start(w_col[:, k:k + 1], w.unsqueeze(1).unsqueeze(2).broadcast_to([HD, H, 1])).then_inc(loads, 16)
            sp.wait_ge(dve_const, 1)
            sp.dma_start(xs_d[DUMP:DUMP + UR, :].rearrange("(p k) f -> p (k f)", p=P), zeros[:, 0:TB * P]).then_inc(dump_st, 16)

            def load_x(dst, s, b):
                sp.dma_start(dst, x[b].rearrange("(p t) f -> p t f", t=TB) if isinstance(b, int)
                             else x[bass.ds(b, 1)].rearrange("o (p t) f -> (o p) t f", t=TB)).then_inc(s, 16)

            def mod_rows(dst, s, b, lo, n):
                row = mod_d[b, lo * P:(lo + n) * P] if isinstance(b, int) else \
                    mod_d[bass.ds(b, 1), lo * P:(lo + n) * P].rearrange("o f -> (o f)")
                sp.dma_start(dst, row.partition_broadcast(P)).then_inc(s, 16)

            @of_batch
            def load_x_norm(b):
                wait(sp, h1_d, b.n - 1)
                load_x(x_p[:, b.par], xp_ld[b.par], b.n)
                if isinstance(b.n, int) and b.n == 0:
                    sp.wait_ge(mod_st, 16)
                mod_rows(mod_p[:, b.par].rearrange("p a f -> p (a f)"), xp_ld[b.par], b.n, SA, 2)

            @of_batch
            def load_x_out(b):
                wait(sp, h2_d, b.n - 1)
                load_x(x_o[:, b.par], xo_ld[b.par], b.n)
                mod_rows(mod_o[:, b.par].rearrange("p a f -> p (a f)"), xo_ld[b.par], b.n, GA, 4)

            @of_batch
            def store_x1(b):
                wait(sp, x1_done, b.n + 1)
                dst = x1_d[b.n] if isinstance(b.n, int) else x1_d[bass.ds(b.n, 1)].rearrange("o t f -> (o t) f")
                sp.dma_start(dst.rearrange("(p t) f -> p t f", t=TB), x1[:, b.par]).then_inc(x1_st[b.par], 16)

            @of_batch
            def store_parts(b):
                wait(sp, lo_d, b.n + 1)
                sp.nop(nofuse=True)
                for half in range(2):
                    wait(sp, aug_ld[b.par][half], 64 * b.nth)
                sp.nop(nofuse=True)
                row = 0
                for a, n in enumerate(TERMS):
                    sp.dma_start(q_d[b.par, row:row + n].rearrange("a p t -> p a t"),
                                 parts[:, 0, a:a + 1, :].broadcast_to([P, n, NT])).then_inc(parts_st, 16)
                    row += n
                sp.dma_start(k_d[b.par].rearrange("a p t -> p a t"), parts[:, 1]).then_inc(parts_st, 16)

            @of_batch
            def load_heads(b, j):
                if isinstance(b.n, int) and b.n == 0:
                    sp.wait_ge(aug_z, 2)
                    sp.wait_ge(gp_const, 16)
                    if j == 0:
                        for i in range(2):
                            sp.dma_start(k_aug[i][MROW:P], ones_b[0:2 * H * NT // P, :]).then_inc(ones_ld, 16)
                if isinstance(b.n, int) and b.n == 2 and j == 0:
                    sp.dma_start(we[:].rearrange("k (e n) -> k e n", e=E), expert_w.rearrange("e k n -> k e n")).then_inc(we_ld, 16)
                wait(sp, parts_st, 64 * (b.n + 1))
                sp.nop(nofuse=True)
                wait(sp, st_r, H * (b.n - 2) + (j + 1) * H // 2)
                hs = slice(j * H // 2, (j + 1) * H // 2)
                loaded = aug_ld[b.par][j]
                sp.dma_start(q_aug[b.par][0:ROWS, hs, :],
                             q_d[b.par].rearrange("a (d h) t -> (a d) h t", h=H)[:, hs]).then_inc(loaded, 16)
                row = 0
                for n in TERMS:
                    sp.dma_start(k_aug[b.par][row:row + n * HD, hs, :],
                                 k_d[b.par, 0:n].rearrange("a (d h) t -> (a d) h t", h=H)[:, hs]).then_inc(loaded, 16)
                    row += n * HD

            @of_batch
            def load_max_rows(b):
                wait(sp, mrows_d, b.n + 1)
                sp.dma_start(q_aug[b.par][MROW:MROW + 2], mrows[:]).then_inc(mrow_ld, 16)

            def step(b0, b1, b2, b3, b4, b5, b6, b7, b8):
                load_x_norm(b0)
                load_heads(b2, 1)
                load_x_out(b4)
                store_parts(b1)
                load_heads(b1, 0)
                load_max_rows(b2)
                store_x1(b4)

            run(sp, step)

            rows_complete(sp)
            for i in range(XB):
                load_unit(sp, i, 0, i)
            with sp.Fori(1, GROUPS_E // XB) as n:
                for i in range(XB):
                    sp.wait_ge(xsT_ps, n * XB + (i - XB + 1))
                    load_unit(sp, n * XB + i, 0, i)

            for i in range(2):
                sp.wait_ge(x1_st[i], 16 * NB // 2)

            def final_loads(b, nth, par):
                wait(sp, of_d, b - 1)
                src = x1_d[b] if isinstance(b, int) else x1_d[bass.ds(b, 1)].rearrange("o t f -> (o t) f")
                sp.dma_start(x1_f[:, par], src.rearrange("(p t) f -> p t f", t=TB)).then_inc(f_ld[par], 16)
                mod_rows(gb_f[:, par], f_ld[par], b, GB, 1)

            def final_store(b, par):
                wait(sp, of_d, b + 1)
                dst = out[b] if isinstance(b, int) else out[bass.ds(b, 1)].rearrange("o t f -> (o t) f")
                sp.dma_start(dst.rearrange("(p t) f -> p t f", t=TB), of[:, par]).then_inc(out_st[par], 16)

            final_loads(0, 0, 0)
            final_loads(1, 0, 1)
            with sp.Fori(1, NB // 2) as n:
                for par in range(2):
                    final_store(n * 2 + (par - 2), par)
                    final_loads(n * 2 + par, n, par)
            final_store(NB - 2, 0)
            final_store(NB - 1, 1)
            for i in range(2):
                sp.wait_ge(out_st[i], 16 * NB // 2)

        @block.gpsimd
        def _(gp):
            nc.gpsimd.memset(ones_f[:], 1.0).then_inc(gp_const, 1)
            nc.gpsimd.memset(ones_b[:], 1.0).then_inc(gp_const, 1)
            gp.wait_ge(gp_const, 2)
            nc.gpsimd.affine_select(out=ident[:], in_=ones_f[:], pattern=[[1, P]], compare_op=ALU.is_equal,
                                    fill=0.0, base=0, channel_multiplier=-1).then_inc(gp_const, 1)
            nc.gpsimd.affine_select(out=tri[:], in_=ones_b[:], pattern=[[1, P]], compare_op=ALU.is_gt,
                                    fill=0.0, base=0, channel_multiplier=-1).then_inc(gp_const, 1)
            for dst, pattern, mult in (
                (iota_e, [[1, E]], 0), (iota_p, [[1, 1]], 1), (iota_n, [[UR, TOK // UR]], 0), (region0, [[REGION, E]], 0),
                (iota_z, [[-ZR, P // ZR]], 1),
                (carry, [[REGION, E]], 0),
            ):
                nc.gpsimd.iota(dst[:], pattern=pattern, base=0, channel_multiplier=mult,
                               allow_small_or_imprecise_dtypes=True).then_inc(gp_const, 1)
            for i in range(2):
                nc.gpsimd.memset(v_aug[i][:], 0.0).then_inc(gp_const, 1)
            gp.wait_ge(gp_const, 12)
            for i in range(2):
                nc.gpsimd.memset(v_aug[i][:, :, :, HD:HD + 1], 1.0).then_inc(gp_const, 1)
            for i in range(2):
                nc.gpsimd.memset(k_aug[i][:], 0.0).then_inc(gp_const, 1)
            gp.wait_ge(gp_const, 16)

            @of_batch
            def copy_v(b):
                wait(gp, qkv_d, TB * (b.n + 1))
                wait(gp, pv_d, GROUPS * (b.n - 1))
                gp.nop(nofuse=True)
                nc.gpsimd.tensor_copy(v_aug[b.par][:, :, :, 0:HD],
                                      qkvg[:, b.par, :, 2 * P:3 * P].rearrange("p t (h d) -> p t h d", d=HD)).then_inc(v_d, 1)

            @of_batch
            def scale_ln1(b):
                wait(gp, xp_ld[b.par], 32 * (b.nth + 1))
                wait(gp, xh1_d, b.n + 1)
                wait(gp, h1_d, b.n)
                gp.nop(nofuse=True)
                nc.gpsimd.tensor_tensor(h1a[:], xh1[:], mod_p[:, b.par, 1:2, :].broadcast_to([P, TB, P]),
                                        ALU.mult).then_inc(h1a_d, 1)

            @of_batch
            def shift_ln1(b):
                wait(gp, h1a_d, b.n + 1)
                wait(gp, hT_ps, b.n)
                nc.gpsimd.tensor_tensor(h1[:], h1a[:], mod_p[:, b.par, 0:1, :].broadcast_to([P, TB, P]),
                                        ALU.add).then_inc(h1_d, 1)

            @of_batch
            def norm_qk(b, t):
                wait(gp, rr_d, b.n + 1)
                wait(gp, qkT_ps, b.n)
                gp.nop(nofuse=True)
                nc.gpsimd.tensor_tensor(
                    qn[:, t].rearrange("p (k d h) -> p k d h", k=2, h=H),
                    qkvg[:, b.par, t, 0:2 * P].rearrange("p (k d h) -> p k d h", k=2, h=H),
                    rr[:, t * 2 * H:(t + 1) * 2 * H].rearrange("p (k h) -> p k h", h=H).unsqueeze(2).broadcast_to(
                        [P, 2, HD, H]), ALU.mult).then_inc(qn_d, 1)

            @of_batch
            def low_part(b):
                wait(gp, mid_d, b.n + 1)
                wait(gp, parts_st, 64 * b.n)
                gp.nop(nofuse=True)
                nc.gpsimd.tensor_tensor(parts[:, :, 2], rest[:], parts[:, :, 1], ALU.subtract).then_inc(lo_d, 1)

            @of_batch
            def max_lead(b):
                wait(gp, mx_d, H * (b.n + 1))
                gp.nop(nofuse=True)
                nc.gpsimd.tensor_copy(mlead[:], negmax[:]).then_inc(mlead_d, 1)

            @of_batch
            def max_lead_wide(b):
                wait(gp, mlead_d, b.n + 1)
                wait(gp, mT_ps, b.n)
                gp.nop(nofuse=True)
                nc.gpsimd.tensor_copy(msplit[:, :, 0], mlead[:]).then_inc(mwide_d, 1)

            @of_batch
            def max_rest(b):
                wait(gp, mwide_d, b.n + 1)
                gp.nop(nofuse=True)
                nc.gpsimd.tensor_tensor(msplit[:, :, 1], negmax[:], mlead[:], ALU.subtract).then_inc(msplit_d, 1)

            @of_batch
            def x_plus_bias(b):
                wait(gp, xo_ld[b.par], 32 * (b.nth + 1))
                wait(gp, x1_done, b.n)
                gp.nop(nofuse=True)
                nc.gpsimd.tensor_tensor(xga[:], x_o[:, b.par], mod_o[:, b.par, 1:2, :].broadcast_to([P, TB, P]),
                                        ALU.add).then_inc(xga_d, 1)

            @of_batch
            def residual(b):
                wait(gp, attg_d, b.n + 1)
                wait(gp, xga_d, b.n + 1)
                wait(gp, xh2_d, b.n - 1)
                wait(gp, x1_st[b.par], 16 * b.nth)
                gp.nop(nofuse=True)
                nc.gpsimd.tensor_tensor(x1[:, b.par], attg[:], xga[:], ALU.add).then_inc(x1_done, 1)

            @of_batch
            def scale_ln2(b):
                wait(gp, xh2_d, b.n + 1)
                wait(gp, h2_d, b.n)
                gp.nop(nofuse=True)
                nc.gpsimd.tensor_tensor(h2a[:], xh2[:], mod_o[:, b.par, 3:4, :].broadcast_to([P, TB, P]),
                                        ALU.mult).then_inc(h2a_d, 1)

            @of_batch
            def shift_ln2(b):
                wait(gp, h2a_d, b.n + 1)
                wait(gp, scat[b.par], 64 * b.nth)
                gp.nop(nofuse=True)
                nc.gpsimd.tensor_tensor(h2[:, b.par], h2a[:], mod_o[:, b.par, 2:3, :].broadcast_to([P, TB, P]),
                                        ALU.add).then_inc(h2_d, 1)

            @of_batch
            def less_largest(b):
                wait(gp, top_d, b.n + 1)
                wait(gp, elg_d, b.n)
                gp.nop(nofuse=True)
                nc.gpsimd.tensor_tensor(dlg[:, :, 0:E], lg[:], top[:, :, 0:1].broadcast_to([P, TB, E]), ALU.subtract).then_inc(dlg_d, 1)
                nc.gpsimd.tensor_tensor(dlg[:, :, E:E + TOPK], top[:, :, 0:TOPK], top[:, :, 0:1].broadcast_to([P, TB, TOPK]),
                                ALU.subtract).then_inc(dlg_d, 1)

            @of_batch
            def chosen(b):
                wait(gp, oh_d, b.n + 1)
                wait(gp, rank_ps, b.n)
                gp.nop(nofuse=True)
                nc.gpsimd.tensor_tensor(mask[:], oh[:, 0], oh[:, 1], ALU.add).then_inc(mask_d, 1)

            @of_batch
            def chosen_ranks(b):
                wait(gp, rk_d, b.n + 1)
                wait(gp, oh_d, b.n + 1)
                wait(gp, slotf_d, b.n)
                gp.nop(nofuse=True)
                nc.gpsimd.tensor_tensor(ohr[:].rearrange("p j t e -> p j (t e)"), oh[:].rearrange("p j t e -> p j (t e)"),
                                rk[:].rearrange("p t e -> p (t e)").unsqueeze(1).broadcast_to([P, TOPK, TB * E]),
                                ALU.mult).then_inc(ohr_d, 1)

            @of_batch
            def keep_index(b):
                wait(gp, idx_d, b.n + 1)
                gp.nop(nofuse=True)
                nc.gpsimd.tensor_copy(idx_all[:, bass.ts(b.n, TOPK * TB)], idx[:].rearrange("p j t -> p (j t)")).then_inc(idxa_d, 1)

            @of_batch
            def keep_weights(b):
                wait(gp, rsum_d, b.n + 1)
                gp.nop(nofuse=True)
                nc.gpsimd.tensor_tensor(p_all[:, bass.ts(b.n, TOPK * TB)].rearrange("p (j t) -> p j t", t=TB),
                                        elg[:, :, E:E + TOPK].rearrange("p t j -> p j t"),
                                        rsum[:].unsqueeze(1).broadcast_to([P, TOPK, TB]), ALU.mult).then_inc(p_d, 1)

            @of_batch
            def keep_slot(b):
                wait(gp, slotf_d, b.n + 1)
                gp.nop(nofuse=True)
                nc.gpsimd.tensor_copy(slot_all[:, bass.ts(b.n, TOPK * TB)], slot_f[:]).then_inc(slota_d, 1)

            @of_batch
            def scatter(b, k):
                wait(gp, slot_d, b.n + 1)
                gp.nop(nofuse=True)
                nc.gpsimd.indirect_dma_start(xs_d, bass.IndirectOffsetOnAxis(ap=slot[:, b.par, k:k + 1], axis=0),
                                             h2[:, b.par, k % TB, :], None).then_inc(scat[b.par], 16)

            def step(b0, b1, b2, b3, b4, b5, b6, b7, b8):
                scatter(b7, 3)
                copy_v(b2)
                x_plus_bias(b4)
                low_part(b1)
                keep_slot(b7)
                scale_ln1(b0)
                chosen(b6)
                shift_ln1(b0)
                scale_ln2(b5)
                keep_index(b6)
                chosen_ranks(b6)
                shift_ln2(b5)
                max_lead(b2)
                max_lead_wide(b2)
                max_rest(b2)
                residual(b4)
                scatter(b6, 0)
                scatter(b6, 1)
                keep_weights(b8)
                scatter(b6, 2)
                less_largest(b6)
                norm_qk(b0, 0)
                norm_qk(b0, 1)

            run(gp, step)

            for i in range(2):
                gp.wait_ge(scat[i], 16 * TOPK * TB * NB // 2)
            gp.wait_ge(zidx_d, 2)
            gp.nop(nofuse=True)
            for g in range(ZG):
                nc.gpsimd.indirect_dma_start(xs_d, bass.IndirectOffsetOnAxis(ap=zidx[:, 0, g:g + 1], axis=0),
                                             zeros[:, 0:P], None).then_inc(tail_st, 16)
            gp.wait_ge(tail_st, 16 * ZG)
            gp.nop(nofuse=True)
            for g in range(ZG):
                nc.gpsimd.indirect_dma_start(xs_d.rearrange("(b r) f -> b (r f)", r=ZR),
                                             bass.IndirectOffsetOnAxis(ap=zidx[:, 1, g:g + 1], axis=0),
                                             zeros[:], None).then_inc(tail_st, 16)

            def store_results(g, i):
                wait(gp, ye_d, g + 1)
                gp.nop(nofuse=True)
                dst = ys_d[g * UG * UR:(g + 1) * UG * UR, :] if isinstance(g, int) else ys_d[bass.ds(g * (UG * UR), UG * UR), :]
                gp.dma_start(dst.rearrange("(u p k) f -> p u k f", u=UG, k=TB),
                             ys_sb[i][:].rearrange("p (u k) f -> p u k f", u=UG)).then_inc(ys_st[i], 16)

            store_results(0, 0)
            store_results(1, 1)
            with gp.Fori(1, GROUPS_E // 2) as n:
                for i in range(2):
                    store_results(n * 2 + i, i)

            for i in range(2):
                gp.wait_ge(ys_st[i], 16 * GROUPS_E // 2)

            def gathers(b, par):
                wait(gp, gi_d, b + 1)
                wait(gp, yc_d, TB * (b - 1))
                gp.nop(nofuse=True)
                for k in range(TOPK * TB):
                    nc.gpsimd.indirect_dma_start(
                        yg[:, par, k, :], None, ys_d,
                        bass.IndirectOffsetOnAxis(ap=gi[:, par, k:k + 1], axis=0)).then_inc(yg_ld[par], 16)

            gathers(0, 0)
            gathers(1, 1)
            with gp.Fori(1, NB // 2) as n:
                for par in range(2):
                    gathers(n * 2 + par, par)

        @block.scalar
        def _(act):
            act.preload_act_table_set("natural_log_exp_and_others")
            act.wait_ge(c_ld, 32)
            nc.scalar.activation(sc[:], c_sb[:], ACT.Exp, scale=-1.0).then_inc(s_exp, 1)
            act.wait_ge(cT_ps, 1)
            nc.scalar.activation(cT[:], misc[0][:, 0:NB], ACT.Copy).then_inc(cT_done, 1)
            act.wait_ge(rwT_ps, 1)
            nc.scalar.activation(rwT[:], misc[0][:, 0:E], ACT.Copy).then_inc(rwT_done, 1)
            act.wait_ge(mod_sb, 3)
            act.dma_start(mod_d, mod[:]).then_inc(mod_st, 16)
            act.wait_ge(dve_const, 3)

            def log_var(n, src, scale, eps_col, ready, tmp, tmp_d):
                wait(act, ready, n + 1)
                nc.scalar.activation(tmp, src, ACT.Ln, bias=eps[:, eps_col:eps_col + 1], scale=scale).then_inc(tmp_d, 1)

            def rsqrt_seed(n, tmp, tmp_d, dst, dst_d):
                wait(act, tmp_d, n + 1)
                nc.scalar.activation(dst, tmp, ACT.Exp, scale=-0.5).then_inc(dst_d, 1)

            def normalise(src, rstd, shift, dst, dst_d):
                for t in range(TB):
                    ins = nc.scalar.activation(dst[:, t], src[:, t], ACT.Identity, scale=rstd[:, t:t + 1], bias=shift[:, t:t + 1])
                ins.then_inc(dst_d, 1)

            @of_batch
            def ln1_log(b):
                log_var(b.n, mv1[:, :, 1], 1.0, 0, mv1_d, lnv1[:], lnv1_d)

            @of_batch
            def ln1_seed(b):
                rsqrt_seed(b.n, lnv1[:], lnv1_d, y1[:], y1_d)

            @of_batch
            def ln1_normalise(b):
                wait(act, shift1_d, b.n + 1)
                wait(act, h1a_d, b.n)
                normalise(x_p[:, b.par], rstd1, shift1, xh1, xh1_d)

            @of_batch
            def h1_transposed(b):
                wait(act, hT_ps, b.n + 1)
                wait(act, qkv_ps, TB * b.n)
                nc.scalar.activation(hT[:], misc[BANK["hT"]][:, 0:NT], ACT.Copy).then_inc(hT_d, 1)

            @of_batch
            def squares(b):
                wait(act, qkv_d, TB * (b.n + 1))
                wait(act, ss_d, b.n)
                nc.scalar.activation(sq[:], qkvg[:, b.par, :, 0:2 * P], ACT.Square).then_inc(sq_d, 1)

            @of_batch
            def rms_log(b):
                log_var(b.n, ss[:], 1.0 / HD, 1, ss_d, lnm[:], lnm_d)

            @of_batch
            def rms_seed(b):
                wait(act, rr_d, b.n)
                rsqrt_seed(b.n, lnm[:], lnm_d, r0[:], r0_d)

            @of_batch
            def gate_exp(b):
                wait(act, qkv_d, TB * (b.n + 1))
                wait(act, den_d, TB * (b.n - 1))
                nc.scalar.activation(eg[:, b.par], qkvg[:, b.par, :, 3 * P:QKVG], ACT.Exp, scale=-1.0).then_inc(eg_d, 1)

            @of_batch
            def high_part(b):
                wait(act, qkT_ps, b.n + 1)
                wait(act, parts_st, 64 * b.n)
                for k in range(2):
                    nc.scalar.activation(parts[:, k, 0], misc[BANK["qkT"]][:, k * NT:(k + 1) * NT], ACT.Copy,
                                         scale=w_col[:, k:k + 1]).then_inc(hi_d, 1)

            @of_batch
            def middle_part(b):
                wait(act, rest_d, b.n + 1)
                wait(act, parts_st, 64 * b.n)
                nc.scalar.activation(parts[:, :, 1], rest[:], ACT.Copy).then_inc(mid_d, 1)

            @of_batch
            def max_rows(b):
                wait(act, mT_ps, b.n + 1)
                wait(act, mrow_ld, 16 * b.n)
                nc.scalar.activation(mrows[:], misc[BANK["mT"]][0:2 * H, 0:NT], ACT.Copy).then_inc(mrows_d, 1)

            @of_batch
            def exp_head(b, h):
                wait(act, st_r, H * b.n + h + 1)
                wait(act, pv_d, GROUPS * b.n + h // 4 - 1)
                nc.scalar.activation(pr[:, h % PR], st_ps[score_bank(b, h)][:], ACT.Exp, scale=SCALE).then_inc(exp_d, 1)

            @of_batch
            def out_transposed(b, g):
                wait(act, pv_d, GROUPS * b.n + g + 1)
                wait(act, o2_ps, TB * b.n)
                nc.scalar.activation(oT[:, g, :], o_ps[:, 0:NT], ACT.Copy).then_inc(oT_d, 1)

            @of_batch
            def on_transposed(b):
                wait(act, onT_ps, b.n + 1)
                wait(act, wo_ps, b.n)
                nc.scalar.activation(onT[:], misc[BANK["onT"]][:, 0:NT], ACT.Copy).then_inc(onT_d, 1)

            @of_batch
            def ln2_log(b):
                log_var(b.n, mv2[:, :, 1], 1.0, 0, mv2_d, lnv2[:], lnv2_d)

            @of_batch
            def ln2_seed(b):
                rsqrt_seed(b.n, lnv2[:], lnv2_d, y2[:], y2_d)

            @of_batch
            def ln2_normalise(b):
                wait(act, shift2_d, b.n + 1)
                wait(act, h2a_d, b.n)
                normalise(x1[:, b.par], rstd2, shift2, xh2, xh2_d)

            @of_batch
            def h2_transposed(b):
                wait(act, h2T_ps, b.n + 1)
                wait(act, lg_ps, b.n)
                nc.scalar.activation(h2T[:], misc[BANK["h2T"]][:, 0:NT], ACT.Copy).then_inc(h2T_d, 1)

            @of_batch
            def router_exp(b):
                wait(act, dlg_d, 2 * (b.n + 1))
                wait(act, esum_d, b.n)
                wait(act, p_d, b.n)
                nc.scalar.activation(elg[:], dlg[:], ACT.Exp).then_inc(elg_d, 1)

            def step(b0, b1, b2, b3, b4, b5, b6, b7, b8):
                exp_head(b3, 2)
                exp_head(b3, 3)
                ln1_log(b0)
                high_part(b1)
                exp_head(b3, 4)
                ln1_seed(b0)
                exp_head(b3, 5)
                middle_part(b1)
                exp_head(b3, 6)
                exp_head(b3, 7)
                out_transposed(b3, 0)
                ln1_normalise(b0)
                ln2_normalise(b5)
                exp_head(b3, 8)
                gate_exp(b2)
                exp_head(b3, 9)
                on_transposed(b4)
                exp_head(b3, 10)
                h1_transposed(b0)
                out_transposed(b3, 1)
                exp_head(b3, 11)
                exp_head(b3, 12)
                exp_head(b3, 13)
                exp_head(b3, 14)
                max_rows(b2)
                squares(b0)
                exp_head(b3, 15)
                out_transposed(b3, 2)
                rms_log(b0)
                ln2_log(b4)
                h2_transposed(b5)
                rms_seed(b0)
                ln2_seed(b4)
                router_exp(b7)
                out_transposed(b3, 3)
                exp_head(b2, 0)
                exp_head(b2, 1)

            run(act, step)

            rows_complete(act)
            for i in range(XB):
                load_unit(act, i, 1, i)

            def results(g, nth, i):
                act.wait_ge(ye_ps, g + 1)
                wait(act, ys_st[i % 2], 16 * nth)
                nc.scalar.activation(ys_sb[i % 2][:].rearrange("p k f -> p (k f)"), out_bank[i], ACT.Copy).then_inc(ye_d, 1)

            def next_unit(g, i):
                act.wait_ge(xsT_ps, g + 1)
                load_unit(act, g + XB, 1, i)

            for i in range(XB):
                results(i, i // 2, i)
                next_unit(i, i)
            with act.Fori(1, GROUPS_E // XB - 1) as n:
                for i in range(XB):
                    results(n * XB + i, n * 2 + i // 2, i)
                    next_unit(n * XB + i, i)
            for i in range(XB):
                results(GROUPS_E - XB + i, (GROUPS_E - XB + i) // 2, i)

        @block.vector
        def _(dve):
            v = nc.vector
            v.memset(zeros[:], 0.0).then_inc(dve_const, 1)
            v.memset(eps[:, 0:1], LN_EPS).then_inc(dve_const, 1)
            v.memset(eps[:, 1:2], RMS_EPS).then_inc(dve_const, 1)
            dve.wait_ge(s_exp, 1)
            v.tensor_scalar(sgn[:], sc[:], 1.0, None, ALU.add).then_inc(s_e1, 1)
            dve.wait_ge(s_e1, 1)
            v.reciprocal(mag[:], sgn[:]).then_inc(s_e1, 1)
            dve.wait_ge(s_e1, 2)
            v.tensor_tensor(sc[:], c_sb[:], mag[:], ALU.mult).then_inc(s_sc, 1)
            dve.wait_ge(mod_ps, 1)
            v.tensor_copy(mod[:, SA * P:GABO * P], o_ps[0:NB, 0:3 * P]).then_inc(clamp, 1)
            v.tensor_copy(mod[:, SB * P:CB * P], o_ps[0:NB, 3 * P:4 * P]).then_inc(clamp, 1)
            v.tensor_copy(mod[:, CB * P:MODS * P], misc[0][0:NB, 0:2 * P]).then_inc(clamp, 1)
            dve.wait_ge(clamp, 3)
            k = 3
            for col in (CA, CB):
                m = mod[:, col * P:(col + 1) * P]
                v.tensor_scalar(m, m, 1.0, None, ALU.add).then_inc(mod_sb, 1)
            for col in (GA, GB):
                m = mod[:, col * P:(col + 1) * P]
                for ins in (
                    lambda: v.tensor_scalar(sgn[:], m, 0.0, 2.0, ALU.is_ge, ALU.mult),
                    lambda: v.scalar_tensor_tensor(mag[:], m, -1.0, m, ALU.mult, ALU.max),
                    lambda: v.tensor_scalar(mag[:], mag[:], 0.25, None, ALU.max),
                    lambda: v.scalar_tensor_tensor(m, sgn[:], -1.0, mag[:], ALU.add, ALU.mult),
                ):
                    ins().then_inc(clamp, 1)
                    k += 1
                    dve.wait_ge(clamp, k)
            dve.wait_ge(loads, LOADS)
            v.tensor_tensor(mod[:, GABO * P:SB * P], mod[:, GA * P:GABO * P], bo_b[0:NB, :], ALU.mult).then_inc(mod_sb, 1)
            for i in range(2):
                v.memset(q_aug[i][:], 0.0).then_inc(aug_z, 1)
            dve.wait_ge(loads, LOADS)
            for raw, dst in ((wraw, wqkv), (braw, bqkv)):
                for k in range(2):
                    v.tensor_copy(dst[:, k * P:(k + 1) * P].rearrange("p (d h) -> p d h", h=H),
                                  raw[:, k * P:(k + 1) * P].rearrange("p (h d) -> p d h", d=HD)).then_inc(perm, 1)
            dve.wait_ge(perm, 4)

            def stats(src, st_t, st_d):
                for t in range(TB):
                    v.bn_stats(st_t[:, t], src[:, t]).then_inc(st_d, 1)

            def aggregate(n, st_t, st_d, mv, mv_d):
                wait(dve, st_d, TB * (n + 1))
                dve.nop(nofuse=True)
                for t in range(TB):
                    ins = v.bn_aggr(mv[:, t], st_t[:, t])
                ins.then_inc(mv_d, 1)

            def newton_a(n, y, half, y_d, t1, t1_d):
                wait(dve, y_d, n + 1)
                v.scalar_tensor_tensor(t1, y, half, y, ALU.mult, ALU.mult).then_inc(t1_d, 1)

            def newton_b(n, var, eps_v, t1, t1_d, t2, t2_d):
                wait(dve, t1_d, n + 1)
                v.scalar_tensor_tensor(t2, var, eps_v, t1, ALU.add, ALU.mult).then_inc(t2_d, 1)

            def newton_c(n, y, t2, t2_d, dst, dst_d):
                wait(dve, t2_d, n + 1)
                v.scalar_tensor_tensor(dst, t2, 1.5, y, ALU.add, ALU.mult).then_inc(dst_d, 1)

            def mean_shift(n, mv, rstd, rstd_d, shift, shift_d):
                wait(dve, rstd_d, n + 1)
                v.scalar_tensor_tensor(shift[:], mv[:, :, 0], -1.0, rstd[:], ALU.mult, ALU.mult).then_inc(shift_d, 1)

            @of_batch
            def ln1_stats(b):
                wait(dve, xp_ld[b.par], 32 * (b.nth + 1))
                stats(x_p[:, b.par], st1, st1_d)

            @of_batch
            def ln1_aggregate(b):
                aggregate(b.n, st1, st1_d, mv1, mv1_d)

            @of_batch
            def ln1_newton_a(b):
                newton_a(b.n, y1[:], -0.5, y1_d, n1[:], n1_d)

            @of_batch
            def ln1_newton_b(b):
                newton_b(b.n, mv1[:, :, 1], LN_EPS, n1[:], n1_d, n1b[:], n1b_d)

            @of_batch
            def ln1_newton_c(b):
                wait(dve, xh1_d, b.n)
                newton_c(b.n, y1[:], n1b[:], n1b_d, rstd1[:], rstd1_d)

            @of_batch
            def ln1_shift(b):
                mean_shift(b.n, mv1, rstd1, rstd1_d, shift1, shift1_d)

            @of_batch
            def qkv_out(b, t):
                wait(dve, v_d, b.n - 1)
                wait(dve, eg_d, b.n - 1)
                wait(dve, qn_d, TB * (b.n - 1))
                wait(dve, qkv_ps, TB * b.n + t + 1)
                v.tensor_tensor(qkvg[:, b.par, t], misc[BANK[f"qkv{t}"]][:, 0:QKVG], bqkv[:], ALU.add).then_inc(qkv_d, 1)

            @of_batch
            def square_sums(b):
                wait(dve, sq_d, b.n + 1)
                v.tensor_reduce(ss[:].rearrange("p (k h) -> p k h", h=H),
                                sq[:].rearrange("p t (k d h) -> p (t k) h d", k=2, h=H), AX.X, ALU.add).then_inc(ss_d, 1)

            @of_batch
            def rms_newton_a(b):
                newton_a(b.n, r0[:], -0.5 / HD, r0_d, n2[:], n2_d)

            @of_batch
            def rms_newton_b(b):
                newton_b(b.n, ss[:], RMS_EPS * HD, n2[:], n2_d, n2b[:], n2b_d)

            @of_batch
            def rms_newton_c(b):
                wait(dve, qn_d, TB * b.n)
                newton_c(b.n, r0[:], n2b[:], n2b_d, rr[:], rr_d)

            @of_batch
            def rest_part(b):
                wait(dve, hi_d, 2 * (b.n + 1))
                wait(dve, lo_d, b.n)
                for k in range(2):
                    ins = v.scalar_tensor_tensor(rest[:, k], misc[BANK["qkT"]][:, k * NT:(k + 1) * NT], w_col[:, k:k + 1],
                                                 parts[:, k, 0], ALU.mult, ALU.subtract)
                ins.then_inc(rest_d, 1)

            @of_batch
            def max_head(b, h):
                wait(dve, mps_r, H * b.n + h + 1)
                if h == 0:
                    wait(dve, msplit_d, b.n)
                v.tensor_reduce(negmax[:, :, h], mx_ps[h % 2][:], AX.X, ALU.max, negate=True).then_inc(mx_d, 1)

            def heads_out(qc):
                return misc[BANK[f"o2{qc}"]][:].rearrange("p (h w) -> p h w", w=VW)

            @of_batch
            def denominator(b, qc):
                wait(dve, eg_d, b.n + 1)
                wait(dve, o2_ps, TB * b.n + qc + 1)
                v.scalar_tensor_tensor(den[:, qc], eg[:, b.par, qc], 1.0, heads_out(qc)[:, :, HD], ALU.add,
                                       ALU.mult).then_inc(den_d, 1)

            @of_batch
            def factor(b, qc):
                wait(dve, den_d, TB * b.n + qc + 1)
                v.reciprocal(fac[:, qc], den[:, qc]).then_inc(fac_d, 1)

            @of_batch
            def gated_out(b, qc):
                wait(dve, fac_d, TB * b.n + qc + 1)
                wait(dve, onT_ps, b.n)
                v.tensor_tensor(on[:, qc].rearrange("p (h d) -> p h d", d=HD), heads_out(qc)[:, :, 0:HD],
                                fac[:, qc].unsqueeze(2).broadcast_to([P, H, HD]), ALU.mult).then_inc(on_d, 1)

            @of_batch
            def attention_ga(b):
                wait(dve, wo_ps, b.n + 1)
                wait(dve, xo_ld[b.par], 32 * (b.nth + 1))
                wait(dve, x1_done, b.n)
                v.tensor_tensor(attg[:], misc[BANK["wo"]][:, 0:NT].rearrange("p (t f) -> p t f", f=P),
                                mod_o[:, b.par, 0:1, :].broadcast_to([P, TB, P]), ALU.mult).then_inc(attg_d, 1)

            @of_batch
            def ln2_stats(b):
                wait(dve, x1_done, b.n + 1)
                stats(x1[:, b.par], st2, st2_d)

            @of_batch
            def ln2_aggregate(b):
                aggregate(b.n, st2, st2_d, mv2, mv2_d)

            @of_batch
            def ln2_newton_a(b):
                newton_a(b.n, y2[:], -0.5, y2_d, n3[:], n3_d)

            @of_batch
            def ln2_newton_b(b):
                newton_b(b.n, mv2[:, :, 1], LN_EPS, n3[:], n3_d, n3b[:], n3b_d)

            @of_batch
            def ln2_newton_c(b):
                wait(dve, xh2_d, b.n)
                newton_c(b.n, y2[:], n3b[:], n3b_d, rstd2[:], rstd2_d)

            @of_batch
            def ln2_shift(b):
                mean_shift(b.n, mv2, rstd2, rstd2_d, shift2, shift2_d)

            @of_batch
            def logits_out(b):
                wait(dve, lg_ps, b.n + 1)
                wait(dve, dlg_d, 2 * b.n)
                v.tensor_copy(lg[:].rearrange("p t e -> p (t e)"), misc[BANK["lg"]][:, 0:TB * E]).then_inc(lg_d, 1)

            @of_batch
            def top_logits(b):
                wait(dve, lg_d, b.n + 1)
                dve.nop(nofuse=True)
                for t in range(TB):
                    ins = v.max(top[:, t], lg[:, t])
                ins.then_inc(top_d, 1)

            @of_batch
            def top_experts(b):
                wait(dve, top_d, b.n + 1)
                dve.nop(nofuse=True)
                for t in range(TB):
                    ins = v.max_index(topi[:, t], top[:, t], lg[:, t])
                ins.then_inc(topi_d, 1)

            @of_batch
            def expert_index(b):
                wait(dve, topi_d, b.n + 1)
                wait(dve, idxa_d, b.n)
                v.tensor_copy(idx[:], topi[:, :, 0:TOPK].rearrange("p t j -> p j t")).then_inc(idx_d, 1)

            @of_batch
            def one_hot(b):
                wait(dve, idx_d, b.n + 1)
                wait(dve, mask_d, b.n)
                wait(dve, ohr_d, b.n)
                v.tensor_tensor(oh[:].rearrange("p j t e -> p (j t) e"),
                                iota_e[:].unsqueeze(1).broadcast_to([P, TOPK * TB, E]),
                                idx[:].rearrange("p j t -> p (j t)").unsqueeze(2).broadcast_to([P, TOPK * TB, E]),
                                ALU.is_equal).then_inc(oh_d, 1)

            @of_batch
            def router_sum(b):
                wait(dve, elg_d, b.n + 1)
                v.tensor_reduce(esum[:], elg[:, :, 0:E], AX.X, ALU.add).then_inc(esum_d, 1)

            @of_batch
            def router_inverse(b):
                wait(dve, esum_d, b.n + 1)
                wait(dve, p_d, b.n)
                v.reciprocal(rsum[:], esum[:]).then_inc(rsum_d, 1)

            @of_batch
            def ranks(b):
                wait(dve, rank_ps, b.n + 1)
                wait(dve, ohr_d, b.n)
                wait(dve, carry_d, b.n)
                v.tensor_tensor(rk[:], misc[BANK["rank"]][:, 0:TB * E].rearrange("p (t e) -> p t e", e=E),
                                carry[:].unsqueeze(1).broadcast_to([P, TB, E]), ALU.add).then_inc(rk_d, 1)

            @of_batch
            def add_counts(b):
                wait(dve, rk_d, b.n + 1)
                v.tensor_tensor(carry[:], misc[BANK["rank"]][:, TB * E:(TB + 1) * E], carry[:], ALU.add).then_inc(carry_d, 1)

            @of_batch
            def slot_value(b):
                wait(dve, ohr_d, b.n + 1)
                wait(dve, slota_d, b.n)
                v.tensor_reduce(slot_f[:].rearrange("p (j t) -> p j t", t=TB), ohr[:], AX.X, ALU.add).then_inc(slotf_d, 1)

            @of_batch
            def slot_number(b):
                wait(dve, slotf_d, b.n + 1)
                wait(dve, scat[b.par], 64 * b.nth)
                v.tensor_copy(slot[:, b.par], slot_f[:]).then_inc(slot_d, 1)

            def step(b0, b1, b2, b3, b4, b5, b6, b7, b8):
                ln1_stats(b0)
                max_head(b2, 4)
                ln1_aggregate(b0)
                top_logits(b6)
                max_head(b2, 5)
                max_head(b2, 6)
                rest_part(b1)
                max_head(b2, 7)
                ln1_newton_a(b0)
                denominator(b4, 0)
                ln2_shift(b5)
                ln1_newton_b(b0)
                max_head(b2, 8)
                ln1_newton_c(b0)
                top_experts(b6)
                denominator(b4, 1)
                factor(b4, 0)
                ln1_shift(b0)
                max_head(b2, 9)
                max_head(b2, 10)
                factor(b4, 1)
                gated_out(b4, 0)
                expert_index(b6)
                gated_out(b4, 1)
                one_hot(b6)
                max_head(b2, 11)
                max_head(b2, 12)
                max_head(b2, 13)
                ranks(b6)
                max_head(b2, 14)
                add_counts(b6)
                max_head(b2, 15)
                attention_ga(b4)
                router_sum(b8)
                slot_value(b6)
                qkv_out(b0, 0)
                router_inverse(b8)
                slot_number(b6)
                qkv_out(b0, 1)
                ln2_stats(b4)
                ln2_aggregate(b4)
                square_sums(b0)
                max_head(b1, 0)
                max_head(b1, 1)
                rms_newton_a(b0)
                ln2_newton_a(b4)
                rms_newton_b(b0)
                ln2_newton_b(b4)
                rms_newton_c(b0)
                max_head(b1, 2)
                ln2_newton_c(b4)
                max_head(b1, 3)
                logits_out(b5)

            run(dve, step)

            steps = [0]

            def chained(ins, s=tab, n=steps):
                ins.then_inc(s, 1)
                n[0] += 1
                dve.wait_ge(s, n[0])

            dve.wait_ge(gp_const, 10)
            v.tensor_scalar(zsel[:], iota_z[:], 0.0, None, ALU.is_ge).then_inc(zc, 1)
            v.tensor_scalar(zlt[:], iota_z[:], float(ZR), None, ALU.is_lt).then_inc(zc, 1)
            dve.wait_ge(zc, 2)
            v.tensor_tensor(zsel[:], zsel[:], zlt[:], ALU.mult).then_inc(zc, 1)
            dve.wait_ge(zc, 3)
            v.tensor_tensor(zlt[:], zsel[:], iota_z[:], ALU.mult).then_inc(zc, 1)
            dve.wait_ge(zc, 4)
            v.tensor_reduce(zrow[:], zlt[:], AX.X, ALU.add).then_inc(zc, 1)
            dve.wait_ge(zc, 5)
            dve.wait_ge(carry_d, NB)
            groups = [P, ZG, P // ZR]
            chained(v.tensor_tensor(zend[:], carry[:].rearrange("p (g e) -> p g e", g=ZG),
                                    zsel[:].unsqueeze(1).broadcast_to(groups), ALU.mult))
            chained(v.tensor_reduce(zfirst[:], zend[:], AX.X, ALU.add))
            v.tensor_scalar(zidx[:, 0], zfirst[:], zrow[:, 0:1], None, ALU.add).then_inc(zidx_d, 1)
            chained(v.tensor_scalar(zblock[:], zfirst[:], 1.0 / ZR, 0.5 - 0.5 / ZR, ALU.mult, ALU.add))
            v.tensor_scalar(zidx[:, 1], zblock[:], zrow[:, 0:1], None, ALU.add).then_inc(zidx_d, 1)
            chained(v.tensor_tensor(cnt[:], carry[:], region0[:], ALU.subtract))
            chained(v.tensor_tensor(gtn[:], cnt[:].unsqueeze(2).broadcast_to([P, E, TOK // UR]),
                                    iota_n[:].unsqueeze(1).broadcast_to([P, E, TOK // UR]), ALU.is_gt))
            chained(v.tensor_reduce(nunit[:], gtn[:], AX.X, ALU.add))
            chained(v.tensor_tensor_scan(uend[:], ones_f[:, 0:E], nunit[:], 0.0, ALU.mult, ALU.add))
            chained(v.tensor_tensor(ubeg[:], uend[:], nunit[:], ALU.subtract))
            chained(v.tensor_scalar(ubrow[:], ubeg[:], float(UR), None, ALU.mult))
            chained(v.tensor_tensor(delta[:], ubrow[:], region0[:], ALU.subtract))
            chained(v.tensor_scalar(cmap[:], delta[:], -1.0, -float(DUMP), ALU.mult, ALU.add))
            chained(v.tensor_scalar(uge[:], ubeg[:], iota_p[:, 0:1], None, ALU.is_le))
            chained(v.tensor_scalar(ult[:], uend[:], iota_p[:, 0:1], None, ALU.is_gt))
            chained(v.tensor_tensor(uin[:], uge[:], ult[:], ALU.mult))
            chained(v.tensor_scalar(unum[:], iota_p[:], float(UR), None, ALU.mult))
            chained(v.tensor_scalar(usel[:], cmap[:], unum[:, 0:1], None, ALU.add))
            chained(v.tensor_tensor(cmap[:], usel[:], uin[:], ALU.mult))
            chained(v.tensor_reduce(ucol2[:], cmap[:], AX.X, ALU.add))
            chained(v.tensor_scalar(ucol[:, 0:1], ucol2[:], float(DUMP), None, ALU.add))
            chained(v.tensor_tensor(usel[:], iota_e[:], uin[:], ALU.mult))
            chained(v.tensor_reduce(ucol2[:], usel[:], AX.X, ALU.add))
            chained(v.tensor_scalar(ucol[:, 1:2], ucol2[:], float(P), None, ALU.mult))
            assert steps[0] == TABLE_STEPS
            dve.wait_ge(tab_ps, 1)
            v.tensor_copy(table[0:1, :], o_ps[0:1, 0:2 * P]).then_inc(table_d, 1)

            nlook = [0]

            def rows_out(g, i):
                wait(dve, xsT_ps, g + 1)
                wait(dve, ye_ps, g - (XB - 1))
                v.tensor_copy(xsT[i][:], in_bank[i]).then_inc(xsT_d, 1)

            dve.wait_ge(slota_d, NB)
            dve.wait_ge(idxa_d, NB)
            dve.wait_ge(p_d, NB)
            for c in range(NPAIR // CH):
                pairs = slice(c * CH, (c + 1) * CH)
                chained(v.tensor_tensor(ohd[:], iota_e[:].unsqueeze(1).broadcast_to([P, CH, E]),
                                        idx_all[:, pairs].unsqueeze(2).broadcast_to([P, CH, E]), ALU.is_equal), look, nlook)
                chained(v.tensor_tensor(ohd2[:], ohd[:], delta[:].unsqueeze(1).broadcast_to([P, CH, E]), ALU.mult), look, nlook)
                chained(v.tensor_reduce(dsl[:, pairs], ohd2[:], AX.X, ALU.add), look, nlook)
            chained(v.tensor_tensor(gidx_f[:], slot_all[:], dsl[:], ALU.add), look, nlook)
            for i in range(XB):
                rows_out(i, i)
            with dve.Fori(1, GROUPS_E // XB) as n:
                for i in range(XB):
                    rows_out(n * XB + i, i)

            def gather_rows(b, par, first):
                if not first:
                    dve.wait_ge(yg_ld[par], 64 * (b // 2) if isinstance(b, int) else b)
                v.tensor_copy(gi[:, par], gidx_f[:, bass.ts(b, TOPK * TB)]).then_inc(gi_d, 1)

            def combine(b, nth, par):
                wait(dve, yg_ld[par], 64 * (nth + 1))
                wait(dve, f_ld[par], 32 * (nth + 1))
                for t in range(TB):
                    v.tensor_scalar(yw[:, t], yg[:, par, t], p_all[:, bass.ds(b * (TOPK * TB) + t, 1)], None,
                                    ALU.mult).then_inc(yw_d, 1)
                for t in range(TB):
                    wait(dve, yw_d, TB * b + t + 1)
                    v.scalar_tensor_tensor(yc[:, t], yg[:, par, TB + t], p_all[:, bass.ds(b * (TOPK * TB) + TB + t, 1)],
                                           yw[:, t], ALU.mult, ALU.add).then_inc(yc_d, 1)
                wait(dve, yc_d, TB * (b + 1))
                v.tensor_tensor(yb[:], yc[:], gb_f[:, par].unsqueeze(1).broadcast_to([P, TB, P]), ALU.mult).then_inc(yb_d, 1)
                wait(dve, yb_d, b + 1)
                wait(dve, out_st[par], 16 * nth)
                v.tensor_tensor(of[:, par], yb[:], x1_f[:, par], ALU.add).then_inc(of_d, 1)

            v.tensor_copy(gi[:, 0], gidx_f[:, 0:TOPK * TB]).then_inc(gi_d, 1)
            v.tensor_copy(gi[:, 1], gidx_f[:, TOPK * TB:2 * TOPK * TB]).then_inc(gi_d, 1)

            def combine_and_next(b, nth, par, more):
                combine(b, nth, par)
                if more:
                    v.tensor_copy(gi[:, par], gidx_f[:, bass.ts(b + 2, TOPK * TB)]).then_inc(gi_d, 1)

            for par in range(2):
                combine_and_next(par, 0, par, True)
            with dve.Fori(1, NB // 2 - 1) as n:
                for par in range(2):
                    combine_and_next(n * 2 + par, n, par, True)
            for par in range(2):
                combine_and_next(NB - 2 + par, NB // 2 - 1, par, False)

        @block.tensor
        def _(pe):
            t_ = nc.tensor
            pe.wait_ge(gp_const, 4)
            pe.wait_ge(s_sc, 1)
            t_.transpose(misc[0][:, 0:NB], sc[:], ident[0:NB, 0:NB]).then_inc(cT_ps, 1)
            pe.wait_ge(cT_done, 1)
            t_.matmul(o_ps[0:NB, :], cT[:], wm[:, 0:4 * P], start=True, stop=True)
            t_.matmul(misc[0][0:NB, 0:2 * P], cT[:], wm[:, 4 * P:6 * P], start=True, stop=True).then_inc(mod_ps, 1)
            pe.wait_ge(clamp, 3)
            pe.wait_ge(loads, LOADS)
            t_.transpose(misc[0][:, 0:E], rw[:], ident[0:E, 0:E]).then_inc(rwT_ps, 1)
            pe.wait_ge(perm, 4)

            free = [(rwT_done, 1), None]

            def emptied(item, b):
                return {
                    "hT": (hT_d, b.n + 1), "qkv0": (qkv_d, TB * b.n + 1), "qkv1": (qkv_d, TB * b.n + 2),
                    "qkT": (rest_d, b.n + 1), "mT": (mrows_d, b.n + 1), "o20": (on_d, TB * b.n + 1), "o21": (on_d, TB * b.n + 2),
                    "onT": (onT_d, b.n + 1), "wo": (attg_d, b.n + 1), "h2T": (h2T_d, b.n + 1), "lg": (lg_d, b.n + 1),
                    "rank": (carry_d, b.n + 1),
                }[item]

            def take(item, b):
                bank = BANK[item]
                if free[bank] is not None:
                    wait(pe, *free[bank])
                free[bank] = emptied(item, b)
                return misc[bank]

            @of_batch
            def transpose_h1(b):
                wait(pe, h1_d, b.n + 1)
                bank = take("hT", b)
                for t in range(TB):
                    last = t_.transpose(bank[:, t * P:(t + 1) * P], h1[:, t], ident[:])
                last.then_inc(hT_ps, 1)

            @of_batch
            def project(b, t):
                wait(pe, hT_d, b.n + 1)
                bank = take(f"qkv{t}", b)
                t_.matmul(bank[:, 0:QKVG], hT[:, t * P:(t + 1) * P], wqkv[:], start=True, stop=True).then_inc(qkv_ps, 1)

            @of_batch
            def transpose_qk(b):
                wait(pe, qn_d, TB * (b.n + 1))
                bank = take("qkT", b)
                for k in range(2):
                    for t in range(TB):
                        last = t_.transpose(bank[:, (k * TB + t) * P:(k * TB + t + 1) * P], qn[:, t, k * P:(k + 1) * P], ident[:])
                last.then_inc(qkT_ps, 1)

            @of_batch
            def scores_q(b, h):
                if h % (H // 2) == 0:
                    wait(pe, aug_ld[b.par][h // (H // 2)], 64 * (b.nth + 1))
                wait(pe, mx_d, H * b.n + h - 1)
                pe.nop(nofuse=True)
                for qc in range(TB):
                    last = t_.matmul(mx_ps[h % 2][:, qc], q_aug[b.par][0:MROW, h, qc * P:(qc + 1) * P],
                                     k_aug[b.par][0:MROW, h, :], start=True, stop=True)
                last.then_inc(mps_r, 1)

            @of_batch
            def transpose_max(b):
                wait(pe, msplit_d, b.n + 1)
                bank = take("mT", b)
                for qc in range(TB):
                    last = t_.transpose(bank[0:2 * H, qc * P:(qc + 1) * P], msplit[:, qc].rearrange("p a h -> p (a h)"), ident[:])
                last.then_inc(mT_ps, 1)

            @of_batch
            def scores_k(b, h):
                if isinstance(b.n, int) and b.n == 0 and h == 0:
                    pe.wait_ge(ones_ld, 32)
                if h == 0:
                    wait(pe, mrow_ld, 16 * (b.n + 1))
                wait(pe, exp_d, H * b.n + h + score_bank_read(b, h))
                pe.nop(nofuse=True)
                for kc in range(TB):
                    last = t_.matmul(st_ps[score_bank(b, h)][:, kc], k_aug[b.par][:, h, kc * P:(kc + 1) * P],
                                     q_aug[b.par][:, h, :], start=True, stop=True)
                last.then_inc(st_r, 1)

            @of_batch
            def probs_v(b, g):
                wait(pe, exp_d, H * b.n + 4 * g + 4)
                wait(pe, oT_d, GROUPS * b.n + g)
                if g == 0:
                    wait(pe, v_d, b.n + 1)
                pe.nop(nofuse=True)
                for kc in range(TB):
                    for j in range(4):
                        h = 4 * g + j
                        last = t_.matmul(o_ps[32 * j:32 * j + VW, 0:NT], v_aug[b.par][:, kc, h, :],
                                         pr[:, h % PR, kc, :], start=(kc == 0), stop=(kc == TB - 1))
                last.then_inc(pv_d, 1)

            @of_batch
            def transpose_out(b, qc):
                wait(pe, oT_d, GROUPS * (b.n + 1))
                bank = take(f"o2{qc}", b)
                for g in range(GROUPS):
                    last = t_.transpose(bank[:, g * P:(g + 1) * P], oT[:, g, qc * P:(qc + 1) * P], ident[:])
                last.then_inc(o2_ps, 1)

            @of_batch
            def transpose_on(b):
                wait(pe, on_d, TB * (b.n + 1))
                bank = take("onT", b)
                for qc in range(TB):
                    last = t_.transpose(bank[:, qc * P:(qc + 1) * P], on[:, qc], ident[:])
                last.then_inc(onT_ps, 1)

            @of_batch
            def project_out(b):
                wait(pe, onT_d, b.n + 1)
                bank = take("wo", b)
                for qc in range(TB):
                    last = t_.matmul(bank[:, qc * P:(qc + 1) * P], onT[:, qc * P:(qc + 1) * P], wo[:], start=True, stop=True)
                last.then_inc(wo_ps, 1)

            @of_batch
            def transpose_h2(b):
                wait(pe, h2_d, b.n + 1)
                bank = take("h2T", b)
                for t in range(TB):
                    last = t_.transpose(bank[:, t * P:(t + 1) * P], h2[:, b.par, t], ident[:])
                last.then_inc(h2T_ps, 1)

            @of_batch
            def logits(b):
                wait(pe, h2T_d, b.n + 1)
                bank = take("lg", b)
                for t in range(TB):
                    last = t_.matmul(bank[:, t * E:(t + 1) * E], h2T[:, t * P:(t + 1) * P], rwT[:], start=True, stop=True)
                last.then_inc(lg_ps, 1)

            @of_batch
            def count_before(b):
                wait(pe, mask_d, b.n + 1)
                bank = take("rank", b)
                m = [mask[:, t] for t in range(TB)]
                t_.matmul(bank[:, 0:TB * E], tri[:], mask[:].rearrange("p t e -> p (t e)"), start=True, stop=False,
                          skip_group_check=True)
                t_.matmul(bank[:, E:2 * E], ones_b[:], m[0], start=False, stop=False, skip_group_check=True)
                t_.matmul(bank[:, 2 * E:3 * E], ones_b[:], m[0], start=False, stop=False, skip_group_check=True)
                t_.matmul(bank[:, 2 * E:3 * E], ones_b[:], m[1], start=False, stop=True,
                          skip_group_check=True).then_inc(rank_ps, 1)

            def step(b0, b1, b2, b3, b4, b5, b6, b7, b8):
                scores_k(b3, 3)
                scores_q(b2, 5)
                transpose_qk(b1)
                scores_q(b2, 6)
                scores_k(b3, 4)
                scores_k(b3, 5)
                scores_k(b3, 6)
                scores_q(b2, 7)
                probs_v(b3, 0)
                scores_q(b2, 8)
                scores_k(b3, 7)
                transpose_out(b4, 1)
                scores_q(b2, 9)
                scores_q(b2, 10)
                scores_k(b3, 8)
                scores_k(b3, 9)
                scores_k(b3, 10)
                scores_q(b2, 11)
                probs_v(b3, 1)
                scores_q(b2, 12)
                transpose_on(b4)
                count_before(b6)
                scores_q(b2, 13)
                scores_k(b3, 11)
                transpose_h1(b0)
                scores_q(b2, 14)
                scores_k(b3, 12)
                scores_q(b2, 15)
                project_out(b4)
                scores_k(b3, 13)
                project(b0, 0)
                scores_k(b3, 14)
                project(b0, 1)
                transpose_max(b2)
                scores_k(b3, 15)
                probs_v(b3, 2)
                scores_q(b1, 0)
                transpose_h2(b5)
                scores_q(b1, 1)
                probs_v(b3, 3)
                scores_q(b1, 2)
                scores_q(b1, 3)
                scores_k(b2, 0)
                logits(b5)
                scores_k(b2, 1)
                scores_k(b2, 2)
                scores_q(b1, 4)
                transpose_out(b3, 0)

            def seed(last):
                for item, k in LAST_IN_BANK:
                    free[BANK[item]] = emptied(item, last[k])

            run(pe, step, seed)

            pe.wait_ge(tab, TABLE_STEPS)
            for k in range(2):
                last = t_.matmul(o_ps[0:1, k * P:(k + 1) * P], ucol[:, k:k + 1], ident[:], start=True, stop=True)
            last.then_inc(tab_ps, 1)
            pe.wait_ge(table_d, 1)

            pe.wait_ge(we_ld, 16)

            def expert_in(g, nth, i):
                pe.wait_ge(xs_ld[i], nth * (16 * UG) + 16 * UG)
                wait(pe, xsT_d, g - (XB - 1))
                pe.nop(nofuse=True)
                for k in range(TG):
                    last = t_.transpose(in_bank[i][:, k * P:(k + 1) * P], xs_sb[i][:, k, :], ident[:])
                last.then_inc(xsT_ps, 1)

            def expert_out(g, i):
                cols = [pe.value_load(table[0:1, bass.ds(g * UG + (P + k), 1)], min_val=0, max_val=(E - 1) * P)
                        for k in range(UG)]
                pe.wait_ge(xsT_d, g + 1)
                wait(pe, ye_d, g - (XB - 1))
                pe.nop(nofuse=True)
                for k in range(TG):
                    last = t_.matmul(out_bank[i][:, k * P:(k + 1) * P], xsT[i][:, k * P:(k + 1) * P],
                                     we[:, bass.ds(cols[k // TB], P)], start=True, stop=True)
                last.then_inc(ye_ps, 1)

            expert_in(0, 0, 0)
            for i in range(XB):
                expert_in(i + 1, (i + 1) // XB, (i + 1) % XB)
                expert_out(i, i)
            with pe.Fori(1, GROUPS_E // XB - 1) as n:
                for i in range(XB):
                    expert_in(n * XB + i + 1, n + (i + 1) // XB, (i + 1) % XB)
                    expert_out(n * XB + i, i)
            for i in range(XB):
                g = GROUPS_E - XB + i
                if g + 1 < GROUPS_E:
                    expert_in(g + 1, (g + 1) // XB, (g + 1) % XB)
                expert_out(g, i)


_INS = ['L0_attn_x', 'L0_attn_Wq', 'L0_attn_bq', 'L0_attn_Wk', 'L0_attn_bk', 'L0_attn_Wv', 'L0_attn_bv', 'L0_attn_Wo',
        'L0_attn_bo', 'L0_attn_qn_w', 'L0_attn_kn_w', 'L0_ffn_router_w', 'L0_ffn_expert_weights', 'L0_c', 'L0_wmod']


def kernel(**inputs):
    import concourse.bacc as bacc
    from concourse.bass_utils import run_bass_kernel_spmd

    nc = bacc.Bacc("TRN2", target_bir_lowering=False, num_devices=1)
    arrays, args = {}, []
    for name in _INS:
        a = np.ascontiguousarray(inputs[name])
        arrays[f"in_{name}"] = a
        args.append(nc.dram_tensor(f"in_{name}", a.shape, mybir.dt.from_np(a.dtype), kind="ExternalInput").ap())
    args.append(nc.dram_tensor("out_x", (NB, NT, P), F32, kind="ExternalOutput").ap())
    build(nc, *args)
    r = run_bass_kernel_spmd(nc, [arrays], core_ids=[0])
    return r.results[0]["out_x"]
```
